# Optimizing a Trainium2 kernel written in Bass

```python
import numpy as np
import jax
import jax.numpy as jnp

def _softmax(x, axis=-1):
    return jax.nn.softmax(x, axis=axis)

def _gelu(x):
    return jax.nn.gelu(x, approximate=True)

def _silu(x):
    return jax.nn.silu(x)

def _sigmoid(x):
    return jax.nn.sigmoid(x)

def _layernorm(x, axis=-1, eps=1e-05):
    m = jnp.mean(x, axis=axis, keepdims=True)
    v = jnp.var(x, axis=axis, keepdims=True)
    return (x - m) / jnp.sqrt(v + eps)

def _scatter_add(tgt, idx, src, axis=0):
    return tgt.at[idx].add(src)

def _segment_sum(src, seg, n):
    return jax.ops.segment_sum(src, seg, n)
kernel_name = 'mk_adaln_attn_ffn_d2_seqx_r4_6bc801'

def setup_inputs(seed: int=0):
    np.random.seed(seed)
    _w = jnp.asarray

    def _rec_inputs():
        import jax
        import jax.numpy as jnp
        _rk = jax.random.key(seed)
        x = 7.971e-05 + 1 * jax.random.normal(jax.random.fold_in(_rk, 1), (2, 1024, 256), jnp.float32)
        _lenS = 1024 - jax.random.randint(jax.random.fold_in(_rk, 7), (2,), 0, max(1, 1024 // 4) + 1, jnp.int32)
        _lenS2 = 1024 - jax.random.randint(jax.random.fold_in(_rk, 8), (2,), 0, max(1, 1024 // 4) + 1, jnp.int32)
        itok_B_0_6 = jax.random.randint(jax.random.fold_in(_rk, 11), (2,), 0, 7, jnp.int32)
        itok_B_0_7 = jax.random.randint(jax.random.fold_in(_rk, 12), (2,), 0, 8, jnp.int32)
        itok_Sx32_0_1023 = jax.random.randint(jax.random.fold_in(_rk, 14), (1024, 32), 0, 256, jnp.int32)
        condB_uprev = -0.456674 + 0.753242 * jax.random.normal(jax.random.fold_in(_rk, 16), (2,), jnp.float32)
        itok_B_0_8 = jax.random.randint(jax.random.fold_in(_rk, 17), (2,), 0, 9, jnp.int32)
        _validS = jnp.arange(1024)[None, :] < _lenS[:, None]
        _validS2 = jnp.arange(1024)[None, :] < _lenS2[:, None]
        _causal = jnp.tril(jnp.ones((1024, 1024), dtype=bool))
        mask_SxS_bk0 = jnp.logical_not(jnp.broadcast_to(_validS[0:1, :], (1024, 1024)))
        mask_Sx32_bk1 = jnp.ones((1024, 32), dtype=bool)
        return (x, itok_B_0_6, itok_B_0_7, itok_Sx32_0_1023, condB_uprev, itok_B_0_8, mask_SxS_bk0, mask_Sx32_bk1)
    x, itok_B_0_6, itok_B_0_7, itok_Sx32_0_1023, condB_uprev, itok_B_0_8, mask_SxS_bk0, mask_Sx32_bk1 = _rec_inputs()

    def _L0_cond_setup():
        import jax, jax.numpy as jnp
        import numpy as np
        N_PROFILES = 8
        HIDDEN = 256
        BOTTLENECK = 128
        EPS = 1e-05
        key = jax.random.key(seed)
        ks = jax.random.split(key, 8)
        B, S, H, K, P = (16, 512, HIDDEN, BOTTLENECK, N_PROFILES)
        down_w = jax.random.normal(ks[0], (P, H, K), dtype=jnp.float32) * (1.0 / np.sqrt(H))
        down_b = jax.random.normal(ks[1], (P, K), dtype=jnp.float32) * 0.01
        up_w = jax.random.normal(ks[2], (P, K, H), dtype=jnp.float32) * (1.0 / np.sqrt(K))
        up_b = jax.random.normal(ks[3], (P, H), dtype=jnp.float32) * 0.01
        ln_g = jnp.ones((P, H), dtype=jnp.float32)
        ln_b = jnp.zeros((P, H), dtype=jnp.float32)
        hidden = jax.random.normal(ks[4], (B, S, H), dtype=jnp.float32)
        profile_ids = jax.random.randint(ks[5], (B,), 0, P)
        return {'hidden': hidden, 'profile_ids': profile_ids, 'down_w': down_w, 'down_b': down_b, 'up_w': up_w, 'up_b': up_b, 'ln_g': ln_g, 'ln_b': ln_b}
    _L0_cond_all = _L0_cond_setup()
    _L0_cond_in = {k: v for k, v in _L0_cond_all.items() if k in ('down_w', 'down_b', 'up_w', 'up_b', 'ln_g', 'ln_b')}
    del _L0_cond_all

    def _L0_attn_setup():
        import jax, jax.numpy as jnp
        import numpy as np
        B, T, C = (4, 256, 256)
        HEAD = 64
        H = C // HEAD
        LORA_MIX = 32
        LORA_DECAY = 64
        LN_EPS = 0.00064

        def _wkv6(r, k, v, w, u):
            rT = jnp.moveaxis(r, 1, 0)
            kT = jnp.moveaxis(k, 1, 0)
            vT = jnp.moveaxis(v, 1, 0)
            wT = jnp.moveaxis(w, 1, 0)

            def step(S, inputs):
                rt, kt, vt, wt = inputs
                kv = kt[..., :, None] * vt[..., None, :]
                y = jnp.einsum('bhi,bhij->bhj', rt, S + u[None, :, :, None] * kv)
                S = wt[..., :, None] * S + kv
                return (S, y)
            S0 = jnp.zeros((r.shape[0], H, HEAD, HEAD), r.dtype)
            _, yT = jax.lax.scan(step, S0, (rT, kT, vT, wT))
            return jnp.moveaxis(yT, 0, 1)

        def _tmix_forward(x, time_maa_x, time_maa_w, time_maa_k, time_maa_v, time_maa_r, time_maa_w1, time_maa_w2, time_decay, time_decay_w1, time_decay_w2, time_faaaa, W_r, W_k, W_v, W_o, ln_w, ln_b):
            b, t, c = x.shape
            xshift = jnp.pad(x, ((0, 0), (1, 0), (0, 0)))[:, :t]
            xx = xshift - x
            xxx = x + xx * time_maa_x
            m = jnp.tanh(xxx @ time_maa_w1).reshape(b, t, 4, LORA_MIX)
            m = jnp.einsum('btfl,flc->fbtc', m, time_maa_w2)
            mw, mk, mv, mr = (m[0], m[1], m[2], m[3])
            xw = x + xx * (time_maa_w + mw)
            xk = x + xx * (time_maa_k + mk)
            xv = x + xx * (time_maa_v + mv)
            xr = x + xx * (time_maa_r + mr)
            r = (xr @ W_r).reshape(b, t, H, HEAD)
            k = (xk @ W_k).reshape(b, t, H, HEAD)
            v = (xv @ W_v).reshape(b, t, H, HEAD)
            ww = time_decay + jnp.tanh(xw @ time_decay_w1) @ time_decay_w2
            w = jnp.exp(-jnp.exp(ww)).reshape(b, t, H, HEAD)
            y = _wkv6(r, k, v, w, time_faaaa)
            mean = y.mean(-1, keepdims=True)
            var = y.var(-1, keepdims=True)
            yn = ((y - mean) * jax.lax.rsqrt(var + LN_EPS)).reshape(b, t, c)
            yn = yn * ln_w + ln_b
            return yn @ W_o
        key0 = jax.random.key(seed)
        ks = jax.random.split(key0, 24)
        rn = lambda k, shape, s: jax.random.normal(k, shape, jnp.float32) * s
        inp = {'query': jax.random.normal(ks[0], (B, T, C), jnp.float32), 'key': jax.random.normal(ks[1], (B, T, C), jnp.float32), 'value': jax.random.normal(ks[2], (B, T, C), jnp.float32), 'time_maa_x': rn(ks[3], (C,), 0.1) + 0.5, 'time_maa_w': rn(ks[4], (C,), 0.1) + 0.5, 'time_maa_k': rn(ks[5], (C,), 0.1) + 0.5, 'time_maa_v': rn(ks[6], (C,), 0.1) + 0.5, 'time_maa_r': rn(ks[7], (C,), 0.1) + 0.5, 'time_maa_w1': rn(ks[8], (C, 4 * LORA_MIX), 0.02), 'time_maa_w2': rn(ks[9], (4, LORA_MIX, C), 0.02), 'time_decay': rn(ks[10], (C,), 0.5) - 5.0, 'time_decay_w1': rn(ks[11], (C, LORA_DECAY), 0.02), 'time_decay_w2': rn(ks[12], (LORA_DECAY, C), 0.02), 'time_faaaa': rn(ks[13], (H, HEAD), 0.5), 'W_r': rn(ks[14], (C, C), 0.02), 'W_k': rn(ks[15], (C, C), 0.02), 'W_v': rn(ks[16], (C, C), 0.02), 'W_o': rn(ks[17], (C, C), 0.02), 'ln_w': jnp.ones((C,), jnp.float32), 'ln_b': jnp.zeros((C,), jnp.float32)}
        return inp
    _L0_attn_all = _L0_attn_setup()
    _L0_attn_in = {k: v for k, v in _L0_attn_all.items() if k in ('key', 'value', 'time_maa_x', 'time_maa_w', 'time_maa_k', 'time_maa_v', 'time_maa_r', 'time_maa_w1', 'time_maa_w2', 'time_decay', 'time_decay_w1', 'time_decay_w2', 'time_faaaa', 'W_r', 'W_k', 'W_v', 'W_o', 'ln_w', 'ln_b')}
    del _L0_attn_all

    def _L0_cond2_setup():
        import jax, jax.numpy as jnp
        import numpy as np
        IN, HID, OUT, PART, E = (256, 1024, 256, 64, 8)
        B, N = (16, 512)
        key = jax.random.key(seed)
        ks = jax.random.split(key, 8)
        s1 = 1.0 / np.sqrt(IN)
        s2 = 1.0 / np.sqrt(HID)
        return {'x': jax.random.normal(ks[0], (B, N, IN), dtype=jnp.float32), 'indices': jax.random.randint(ks[1], (B,), 0, E, dtype=jnp.int64), 'W1': jax.random.uniform(ks[2], (IN, HID), jnp.float32, -s1, s1), 'b1': jax.random.uniform(ks[3], (HID,), jnp.float32, -s1, s1), 'W2': jax.random.uniform(ks[4], (HID, OUT - PART), jnp.float32, -s2, s2), 'b2': jax.random.uniform(ks[5], (OUT - PART,), jnp.float32, -s2, s2), 'We': jax.random.uniform(ks[6], (E, HID, PART), jnp.float32, -s2, s2), 'be': jax.random.uniform(ks[7], (E, PART), jnp.float32, -s2, s2)}
    _L0_cond2_all = _L0_cond2_setup()
    _L0_cond2_in = {k: v for k, v in _L0_cond2_all.items() if k in ('W1', 'b1', 'W2', 'b2', 'We', 'be')}
    del _L0_cond2_all

    def _L0_ffn_setup():
        import jax, jax.numpy as jnp
        import numpy as np
        E = 8
        TOP_K = 2
        B, S, D = (2, 1024, 256)
        H = 1024
        CAPACITY = 512

        def _moe(x, Wg, W1, b1, W2, b2):
            b, s, d = x.shape
            xf = x.reshape(b * s, d)
            logits = xf.astype(jnp.float32) @ Wg.astype(jnp.float32)
            probs = jax.nn.softmax(logits, axis=-1)
            vals, idx = jax.lax.top_k(probs, TOP_K)
            w = vals / (jnp.sum(vals, axis=-1, keepdims=True) + 1e-09)
            counts = jnp.zeros((E,), dtype=jnp.int32)
            combine = jnp.zeros((b * s, E), dtype=jnp.float32)
            for k in range(TOP_K):
                oh = jax.nn.one_hot(idx[:, k], E, dtype=jnp.int32)
                pos = jnp.cumsum(oh, axis=0) - 1 + counts[None, :]
                keep = (oh == 1) & (pos < CAPACITY)
                counts = counts + jnp.sum(keep.astype(jnp.int32), axis=0)
                combine = combine + w[:, k][:, None] * keep.astype(jnp.float32)
            out = jnp.zeros_like(xf)
            for e in range(E):
                h = jax.nn.gelu(xf @ W1[e] + b1[e])
                ye = h @ W2[e] + b2[e]
                out = out + combine[:, e][:, None].astype(xf.dtype) * ye
            return out.reshape(b, s, d)
        key = jax.random.key(seed)
        k0, k1, k2, k3 = jax.random.split(key, 4)
        return {'x': jax.random.normal(k0, (B, S, D), dtype=jnp.float32), 'Wg': jax.random.normal(k1, (D, E), dtype=jnp.float32) * 0.02, 'W1': jax.random.normal(k2, (E, D, H), dtype=jnp.float32) * 0.02, 'b1': jnp.zeros((E, H), dtype=jnp.float32), 'W2': jax.random.normal(k3, (E, H, D), dtype=jnp.float32) * 0.02, 'b2': jnp.zeros((E, D), dtype=jnp.float32)}
    _L0_ffn_all = _L0_ffn_setup()
    _L0_ffn_in = {k: v for k, v in _L0_ffn_all.items() if k in ('Wg', 'W1', 'b1', 'W2', 'b2')}
    del _L0_ffn_all

    def _L1_cond_setup():
        import jax, jax.numpy as jnp
        import numpy as np
        B, S, D, H = (4, 256, 256, 16)
        DH = D // H
        K_SPARSE = 32
        LAMBDA_MAX, ALPHA = (10.0, 5.0)
        SPARSE_THRESHOLD = 1.0
        key = jax.random.key(seed)
        ks = jax.random.split(key, 12)
        x = jax.random.normal(ks[0], (B, S, D), dtype=jnp.float32)
        prior_mask = jax.random.bernoulli(ks[1], 0.1, (S, S))
        prior_indices = jax.random.randint(ks[2], (S, K_SPARSE), 0, S)
        prior_index_mask = jax.random.bernoulli(ks[3], 0.9, (S, K_SPARSE))
        prior_index_mask = prior_index_mask.at[:, 0].set(True)
        u_prev = jax.random.normal(ks[4], (B, 1), dtype=jnp.float32)
        sc = 1.0 / np.sqrt(D)
        Wq = jax.random.normal(ks[5], (D, D), dtype=jnp.float32) * sc
        Wk = jax.random.normal(ks[6], (D, D), dtype=jnp.float32) * sc
        Wv = jax.random.normal(ks[7], (D, D), dtype=jnp.float32) * sc
        Wo = jax.random.normal(ks[8], (D, D), dtype=jnp.float32) * sc
        bq = jnp.zeros((D,), jnp.float32)
        bk = jnp.zeros((D,), jnp.float32)
        bv = jnp.zeros((D,), jnp.float32)
        bo = jnp.zeros((D,), jnp.float32)
        return {'x': x, 'prior_mask': prior_mask, 'prior_indices': prior_indices, 'prior_index_mask': prior_index_mask, 'u_prev': u_prev, 'Wq': Wq, 'bq': bq, 'Wk': Wk, 'bk': bk, 'Wv': Wv, 'bv': bv, 'Wo': Wo, 'bo': bo}
    _L1_cond_all = _L1_cond_setup()
    _L1_cond_in = {k: v for k, v in _L1_cond_all.items() if k in ('Wq', 'bq', 'Wk', 'bk', 'Wv', 'bv', 'Wo', 'bo')}
    del _L1_cond_all

    def _L1_attn_setup():
        import jax, jax.numpy as jnp
        import numpy as np
        LOCAL_RADIUS = 127
        TOKENS_PER_BLOCK = 16
        NEG = -1000000000.0

        def _concat_3_blocks(x):
            p = jnp.pad(x, [(0, 0), (1, 1), (0, 0), (0, 0), (0, 0)])
            return jnp.concatenate([p[:, :-2], p[:, 1:-1], p[:, 2:]], axis=2)

        def _softmax_with_extra_logit(x, axis=-1):
            m = jnp.maximum(jax.lax.stop_gradient(x.max(axis, keepdims=True)), 0)
            unnorm = jnp.exp(x - m)
            denom = unnorm.sum(axis, keepdims=True) + jnp.exp(-m)
            return unnorm / denom
        key = jax.random.key(seed)
        ks = jax.random.split(key, 5)
        B, L, D, H, dh = (2, 1024, 256, 16, 64)
        return {'x': jax.random.normal(ks[0], (B, L, D), jnp.float32), 'Wq': jax.random.normal(ks[1], (D, H, dh), jnp.float32) * 0.02, 'Wk': jax.random.normal(ks[2], (D, H, dh), jnp.float32) * 0.02, 'Wv': jax.random.normal(ks[3], (D, H, dh), jnp.float32) * 0.02, 'Wo': jax.random.normal(ks[4], (H, dh, D), jnp.float32) * 0.02}
    _L1_attn_all = _L1_attn_setup()
    _L1_attn_in = {k: v for k, v in _L1_attn_all.items() if k in ('Wq', 'Wk', 'Wv', 'Wo')}
    del _L1_attn_all

    def _L1_cond2_setup():
        import jax, jax.numpy as jnp
        import numpy as np
        LN_EPS = 1e-05
        key = jax.random.key(seed)
        ks = jax.random.split(key, 8)
        B, S, H, A, L = (32, 512, 256, 64, 10)
        return {'hidden_states': jax.random.normal(ks[0], (B, S, H), dtype=jnp.float32), 'language_ids': jax.random.randint(ks[1], (B,), 0, L, dtype=jnp.int64), 'W1': jax.random.normal(ks[2], (L, H, A), dtype=jnp.float32) * (1.0 / np.sqrt(H)), 'b1': jnp.zeros((L, A), dtype=jnp.float32), 'W2': jax.random.normal(ks[3], (L, A, H), dtype=jnp.float32) * (1.0 / np.sqrt(A)), 'b2': jnp.zeros((L, H), dtype=jnp.float32), 'gamma': jnp.ones((L, H), dtype=jnp.float32), 'beta': jnp.zeros((L, H), dtype=jnp.float32)}
    _L1_cond2_all = _L1_cond2_setup()
    _L1_cond2_in = {k: v for k, v in _L1_cond2_all.items() if k in ('W1', 'b1', 'W2', 'b2', 'gamma', 'beta')}
    del _L1_cond2_all

    def _L1_ffn_setup():
        import jax, jax.numpy as jnp
        import numpy as np
        DIM = 256

        def _reference_tuple_inner(x, W_r, W_k, W_v, mu_r, mu_k):
            B, T, C = x.shape
            x_prev = jnp.concatenate([jnp.zeros((B, 1, C), x.dtype), x[:, :-1, :]], axis=1)
            xr = mu_r * x + (1.0 - mu_r) * x_prev
            xk = mu_k * x + (1.0 - mu_k) * x_prev
            r = jax.nn.sigmoid(jnp.einsum('btc,dc->btd', xr, W_r))
            k = jnp.einsum('btc,dc->btd', xk, W_k)
            k_act = jnp.square(jax.nn.relu(k))
            out = r * jnp.einsum('btc,dc->btd', k_act, W_v)
            new_state = x[:, -1, :]
            return (out, new_state)
        key = jax.random.key(seed)
        ks = jax.random.split(key, 6)
        B, T, C = (8, 512, DIM)
        x = jax.random.normal(ks[0], (B, T, C), dtype=jnp.float32)
        s = 1.0 / np.sqrt(C)
        W_r = jax.random.uniform(ks[1], (C, C), jnp.float32, -s, s)
        W_k = jax.random.uniform(ks[2], (C, C), jnp.float32, -s, s)
        W_v = jax.random.uniform(ks[3], (C, C), jnp.float32, -s, s)
        mu_r = jax.random.uniform(ks[4], (C,), jnp.float32)
        mu_k = jax.random.uniform(ks[5], (C,), jnp.float32)
        return {'x': x, 'W_r': W_r, 'W_k': W_k, 'W_v': W_v, 'mu_r': mu_r, 'mu_k': mu_k}
    _L1_ffn_all = _L1_ffn_setup()
    _L1_ffn_in = {k: v for k, v in _L1_ffn_all.items() if k in ('W_r', 'W_k', 'W_v', 'mu_r', 'mu_k')}
    del _L1_ffn_all
    return {'x': x, 'itok_B_0_6': itok_B_0_6, 'itok_B_0_7': itok_B_0_7, 'itok_Sx32_0_1023': itok_Sx32_0_1023, 'condB_uprev': condB_uprev, 'itok_B_0_8': itok_B_0_8, 'mask_SxS_bk0': mask_SxS_bk0, 'mask_Sx32_bk1': mask_Sx32_bk1, 'L0_cond_down_w': _L0_cond_in['down_w'], 'L0_cond_down_b': _L0_cond_in['down_b'], 'L0_cond_up_w': _L0_cond_in['up_w'], 'L0_cond_up_b': _L0_cond_in['up_b'], 'L0_cond_ln_g': _L0_cond_in['ln_g'], 'L0_cond_ln_b': _L0_cond_in['ln_b'], 'L0_attn_key': _L0_attn_in['key'], 'L0_attn_value': _L0_attn_in['value'], 'L0_attn_time_maa_x': _L0_attn_in['time_maa_x'], 'L0_attn_time_maa_w': _L0_attn_in['time_maa_w'], 'L0_attn_time_maa_k': _L0_attn_in['time_maa_k'], 'L0_attn_time_maa_v': _L0_attn_in['time_maa_v'], 'L0_attn_time_maa_r': _L0_attn_in['time_maa_r'], 'L0_attn_time_maa_w1': _L0_attn_in['time_maa_w1'], 'L0_attn_time_maa_w2': _L0_attn_in['time_maa_w2'], 'L0_attn_time_decay': _L0_attn_in['time_decay'], 'L0_attn_time_decay_w1': _L0_attn_in['time_decay_w1'], 'L0_attn_time_decay_w2': _L0_attn_in['time_decay_w2'], 'L0_attn_time_faaaa': _L0_attn_in['time_faaaa'], 'L0_attn_W_r': _L0_attn_in['W_r'], 'L0_attn_W_k': _L0_attn_in['W_k'], 'L0_attn_W_v': _L0_attn_in['W_v'], 'L0_attn_W_o': _L0_attn_in['W_o'], 'L0_attn_ln_w': _L0_attn_in['ln_w'], 'L0_attn_ln_b': _L0_attn_in['ln_b'], 'L0_cond2_W1': _L0_cond2_in['W1'], 'L0_cond2_b1': _L0_cond2_in['b1'], 'L0_cond2_W2': _L0_cond2_in['W2'], 'L0_cond2_b2': _L0_cond2_in['b2'], 'L0_cond2_We': _L0_cond2_in['We'], 'L0_cond2_be': _L0_cond2_in['be'], 'L0_ffn_Wg': _L0_ffn_in['Wg'], 'L0_ffn_W1': _L0_ffn_in['W1'], 'L0_ffn_b1': _L0_ffn_in['b1'], 'L0_ffn_W2': _L0_ffn_in['W2'], 'L0_ffn_b2': _L0_ffn_in['b2'], 'L1_cond_Wq': _L1_cond_in['Wq'], 'L1_cond_bq': _L1_cond_in['bq'], 'L1_cond_Wk': _L1_cond_in['Wk'], 'L1_cond_bk': _L1_cond_in['bk'], 'L1_cond_Wv': _L1_cond_in['Wv'], 'L1_cond_bv': _L1_cond_in['bv'], 'L1_cond_Wo': _L1_cond_in['Wo'], 'L1_cond_bo': _L1_cond_in['bo'], 'L1_attn_Wq': _L1_attn_in['Wq'], 'L1_attn_Wk': _L1_attn_in['Wk'], 'L1_attn_Wv': _L1_attn_in['Wv'], 'L1_attn_Wo': _L1_attn_in['Wo'], 'L1_cond2_W1': _L1_cond2_in['W1'], 'L1_cond2_b1': _L1_cond2_in['b1'], 'L1_cond2_W2': _L1_cond2_in['W2'], 'L1_cond2_b2': _L1_cond2_in['b2'], 'L1_cond2_gamma': _L1_cond2_in['gamma'], 'L1_cond2_beta': _L1_cond2_in['beta'], 'L1_ffn_W_r': _L1_ffn_in['W_r'], 'L1_ffn_W_k': _L1_ffn_in['W_k'], 'L1_ffn_W_v': _L1_ffn_in['W_v'], 'L1_ffn_mu_r': _L1_ffn_in['mu_r'], 'L1_ffn_mu_k': _L1_ffn_in['mu_k']}

def reference(x, itok_B_0_6, itok_B_0_7, itok_Sx32_0_1023, condB_uprev, itok_B_0_8, mask_SxS_bk0, mask_Sx32_bk1, L0_cond_down_w, L0_cond_down_b, L0_cond_up_w, L0_cond_up_b, L0_cond_ln_g, L0_cond_ln_b, L0_attn_key, L0_attn_value, L0_attn_time_maa_x, L0_attn_time_maa_w, L0_attn_time_maa_k, L0_attn_time_maa_v, L0_attn_time_maa_r, L0_attn_time_maa_w1, L0_attn_time_maa_w2, L0_attn_time_decay, L0_attn_time_decay_w1, L0_attn_time_decay_w2, L0_attn_time_faaaa, L0_attn_W_r, L0_attn_W_k, L0_attn_W_v, L0_attn_W_o, L0_attn_ln_w, L0_attn_ln_b, L0_cond2_W1, L0_cond2_b1, L0_cond2_W2, L0_cond2_b2, L0_cond2_We, L0_cond2_be, L0_ffn_Wg, L0_ffn_W1, L0_ffn_b1, L0_ffn_W2, L0_ffn_b2, L1_cond_Wq, L1_cond_bq, L1_cond_Wk, L1_cond_bk, L1_cond_Wv, L1_cond_bv, L1_cond_Wo, L1_cond_bo, L1_attn_Wq, L1_attn_Wk, L1_attn_Wv, L1_attn_Wo, L1_cond2_W1, L1_cond2_b1, L1_cond2_W2, L1_cond2_b2, L1_cond2_gamma, L1_cond2_beta, L1_ffn_W_r, L1_ffn_W_k, L1_ffn_W_v, L1_ffn_mu_r, L1_ffn_mu_k):
    import jax
    import jax.numpy as jnp

    def _L0_cond_ref(hidden, profile_ids, down_w, down_b, up_w, up_b, ln_g, ln_b):
        import jax, jax.numpy as jnp
        import numpy as np
        N_PROFILES = 8
        HIDDEN = 256
        BOTTLENECK = 128
        EPS = 1e-05
        Wd = down_w[profile_ids]
        bd = down_b[profile_ids][:, None]
        Wu = up_w[profile_ids]
        bu = up_b[profile_ids][:, None]
        g = ln_g[profile_ids][:, None]
        b = ln_b[profile_ids][:, None]
        z = jax.nn.relu(jnp.einsum('bsh,bhk->bsk', hidden, Wd) + bd)
        y = hidden + jnp.einsum('bsk,bkh->bsh', z, Wu) + bu
        mu = jnp.mean(y, axis=-1, keepdims=True)
        var = jnp.mean(jnp.square(y - mu), axis=-1, keepdims=True)
        return (y - mu) * jax.lax.rsqrt(var + EPS) * g + b

    def _L0_attn_ref(query, key, value, time_maa_x, time_maa_w, time_maa_k, time_maa_v, time_maa_r, time_maa_w1, time_maa_w2, time_decay, time_decay_w1, time_decay_w2, time_faaaa, W_r, W_k, W_v, W_o, ln_w, ln_b):
        import jax, jax.numpy as jnp
        import numpy as np
        B, T, C = (4, 256, 256)
        HEAD = 64
        H = C // HEAD
        LORA_MIX = 32
        LORA_DECAY = 64
        LN_EPS = 0.00064

        def _wkv6(r, k, v, w, u):
            rT = jnp.moveaxis(r, 1, 0)
            kT = jnp.moveaxis(k, 1, 0)
            vT = jnp.moveaxis(v, 1, 0)
            wT = jnp.moveaxis(w, 1, 0)

            def step(S, inputs):
                rt, kt, vt, wt = inputs
                kv = kt[..., :, None] * vt[..., None, :]
                y = jnp.einsum('bhi,bhij->bhj', rt, S + u[None, :, :, None] * kv)
                S = wt[..., :, None] * S + kv
                return (S, y)
            S0 = jnp.zeros((r.shape[0], H, HEAD, HEAD), r.dtype)
            _, yT = jax.lax.scan(step, S0, (rT, kT, vT, wT))
            return jnp.moveaxis(yT, 0, 1)

        def _tmix_forward(x, time_maa_x, time_maa_w, time_maa_k, time_maa_v, time_maa_r, time_maa_w1, time_maa_w2, time_decay, time_decay_w1, time_decay_w2, time_faaaa, W_r, W_k, W_v, W_o, ln_w, ln_b):
            b, t, c = x.shape
            xshift = jnp.pad(x, ((0, 0), (1, 0), (0, 0)))[:, :t]
            xx = xshift - x
            xxx = x + xx * time_maa_x
            m = jnp.tanh(xxx @ time_maa_w1).reshape(b, t, 4, LORA_MIX)
            m = jnp.einsum('btfl,flc->fbtc', m, time_maa_w2)
            mw, mk, mv, mr = (m[0], m[1], m[2], m[3])
            xw = x + xx * (time_maa_w + mw)
            xk = x + xx * (time_maa_k + mk)
            xv = x + xx * (time_maa_v + mv)
            xr = x + xx * (time_maa_r + mr)
            r = (xr @ W_r).reshape(b, t, H, HEAD)
            k = (xk @ W_k).reshape(b, t, H, HEAD)
            v = (xv @ W_v).reshape(b, t, H, HEAD)
            ww = time_decay + jnp.tanh(xw @ time_decay_w1) @ time_decay_w2
            w = jnp.exp(-jnp.exp(ww)).reshape(b, t, H, HEAD)
            y = _wkv6(r, k, v, w, time_faaaa)
            mean = y.mean(-1, keepdims=True)
            var = y.var(-1, keepdims=True)
            yn = ((y - mean) * jax.lax.rsqrt(var + LN_EPS)).reshape(b, t, c)
            yn = yn * ln_w + ln_b
            return yn @ W_o
        return _tmix_forward(query, time_maa_x, time_maa_w, time_maa_k, time_maa_v, time_maa_r, time_maa_w1, time_maa_w2, time_decay, time_decay_w1, time_decay_w2, time_faaaa, W_r, W_k, W_v, W_o, ln_w, ln_b)

    def _L0_cond2_ref(x, indices, W1, b1, W2, b2, We, be):
        import jax, jax.numpy as jnp
        import numpy as np
        IN, HID, OUT, PART, E = (256, 1024, 256, 64, 8)
        B, N = (16, 512)
        h = jax.nn.gelu(jnp.einsum('bni,ih->bnh', x, W1) + b1, approximate=False)
        shared_x = jnp.einsum('bnh,ho->bno', h, W2) + b2
        We_sel = We[indices]
        be_sel = be[indices]
        expert_x = jnp.einsum('bnh,bhp->bnp', h, We_sel) + be_sel[:, None, :]
        return jnp.concatenate([shared_x, expert_x], axis=-1)

    def _L0_ffn_ref(x, Wg, W1, b1, W2, b2):
        import jax, jax.numpy as jnp
        import numpy as np
        E = 8
        TOP_K = 2
        B, S, D = (2, 1024, 256)
        H = 1024
        CAPACITY = 512

        def _moe(x, Wg, W1, b1, W2, b2):
            b, s, d = x.shape
            xf = x.reshape(b * s, d)
            logits = xf.astype(jnp.float32) @ Wg.astype(jnp.float32)
            probs = jax.nn.softmax(logits, axis=-1)
            vals, idx = jax.lax.top_k(probs, TOP_K)
            w = vals / (jnp.sum(vals, axis=-1, keepdims=True) + 1e-09)
            counts = jnp.zeros((E,), dtype=jnp.int32)
            combine = jnp.zeros((b * s, E), dtype=jnp.float32)
            for k in range(TOP_K):
                oh = jax.nn.one_hot(idx[:, k], E, dtype=jnp.int32)
                pos = jnp.cumsum(oh, axis=0) - 1 + counts[None, :]
                keep = (oh == 1) & (pos < CAPACITY)
                counts = counts + jnp.sum(keep.astype(jnp.int32), axis=0)
                combine = combine + w[:, k][:, None] * keep.astype(jnp.float32)
            out = jnp.zeros_like(xf)
            for e in range(E):
                h = jax.nn.gelu(xf @ W1[e] + b1[e])
                ye = h @ W2[e] + b2[e]
                out = out + combine[:, e][:, None].astype(xf.dtype) * ye
            return out.reshape(b, s, d)
        return _moe(x, Wg, W1, b1, W2, b2)

    def _L1_cond_ref(x, prior_mask, prior_indices, prior_index_mask, u_prev, Wq, bq, Wk, bk, Wv, bv, Wo, bo):
        import jax, jax.numpy as jnp
        import numpy as np
        B, S, D, H = (4, 256, 256, 16)
        DH = D // H
        K_SPARSE = 32
        LAMBDA_MAX, ALPHA = (10.0, 5.0)
        SPARSE_THRESHOLD = 1.0
        Bb, Ss, Dd = x.shape
        scale = 1.0 / jnp.sqrt(jnp.asarray(DH, x.dtype))

        def proj(W, b):
            return (x @ W.T + b).reshape(Bb, Ss, H, DH).transpose(0, 2, 1, 3)
        Q, K, V = (proj(Wq, bq), proj(Wk, bk), proj(Wv, bv))
        lam = LAMBDA_MAX * jnp.exp(-ALPHA * u_prev.reshape(Bb))
        use_sparse = lam >= SPARSE_THRESHOLD
        scores = jnp.einsum('bhqd,bhkd->bhqk', Q, K) * scale
        prior_bias = jnp.where(prior_mask[:Ss, :Ss], 0.0, -1.0).astype(x.dtype)
        bias = lam[:, None, None, None] * prior_bias[None, None]
        dense_out = jnp.einsum('bhqk,bhkd->bhqd', jax.nn.softmax(scores + bias, axis=-1), V)
        idx = prior_indices[:Ss]
        Kg = K[:, :, idx]
        Vg = V[:, :, idx]
        s_scores = jnp.einsum('bhsd,bhskd->bhsk', Q, Kg) * scale
        s_scores = jnp.where(prior_index_mask[:Ss][None, None], s_scores, jnp.asarray(-jnp.inf, x.dtype))
        sparse_out = jnp.einsum('bhsk,bhskd->bhsd', jax.nn.softmax(s_scores, axis=-1), Vg)
        out = jnp.where(use_sparse[:, None, None, None], sparse_out, dense_out)
        out = out.transpose(0, 2, 1, 3).reshape(Bb, Ss, Dd)
        return out @ Wo.T + bo

    def _L1_attn_ref(x, Wq, Wk, Wv, Wo):
        import jax, jax.numpy as jnp
        import numpy as np
        LOCAL_RADIUS = 127
        TOKENS_PER_BLOCK = 16
        NEG = -1000000000.0

        def _concat_3_blocks(x):
            p = jnp.pad(x, [(0, 0), (1, 1), (0, 0), (0, 0), (0, 0)])
            return jnp.concatenate([p[:, :-2], p[:, 1:-1], p[:, 2:]], axis=2)

        def _softmax_with_extra_logit(x, axis=-1):
            m = jnp.maximum(jax.lax.stop_gradient(x.max(axis, keepdims=True)), 0)
            unnorm = jnp.exp(x - m)
            denom = unnorm.sum(axis, keepdims=True) + jnp.exp(-m)
            return unnorm / denom
        B, L, D = x.shape
        H, dh = (Wq.shape[1], Wq.shape[2])
        bl = LOCAL_RADIUS + 1
        nb = L // bl
        G = L // TOKENS_PER_BLOCK
        q = jnp.einsum('bld,dhk->blhk', x, Wq) / jnp.sqrt(jnp.asarray(dh, x.dtype))
        k = jnp.einsum('bld,dhk->blhk', x, Wk)
        v = jnp.einsum('bld,dhk->blhk', x, Wv)
        block_ids = jnp.arange(L) // TOKENS_PER_BLOCK
        one_hot = jax.nn.one_hot(block_ids, G, dtype=x.dtype)
        g = jnp.einsum('bld,lg->bgd', x, one_hot)
        side_k = jnp.einsum('bgd,dhk->bghk', g, Wk)
        side_v = jnp.einsum('bgd,dhk->bghk', g, Wv)
        qb = q.reshape(B, nb, bl, H, dh)
        kb = _concat_3_blocks(k.reshape(B, nb, bl, H, dh))
        vb = _concat_3_blocks(v.reshape(B, nb, bl, H, dh))
        k_cat = jnp.concatenate([kb, jnp.broadcast_to(side_k[:, None], (B, nb, G, H, dh))], axis=2)
        v_cat = jnp.concatenate([vb, jnp.broadcast_to(side_v[:, None], (B, nb, G, H, dh))], axis=2)
        logits = jnp.einsum('bnqhd,bnkhd->bnhqk', qb, k_cat)
        q_idx = jnp.arange(bl)[:, None]
        k_idx = jnp.arange(3 * bl)[None, :]
        rel = k_idx - bl - q_idx
        b_idx = jnp.arange(nb)[:, None, None]
        k_pos = (b_idx - 1) * bl + k_idx
        valid = (jnp.abs(rel) <= LOCAL_RADIUS) & (k_pos >= 0) & (k_pos < L)
        local_bias = jnp.where(valid, 0.0, NEG).astype(logits.dtype)
        side_bias = jnp.zeros((nb, bl, G), logits.dtype)
        bias = jnp.concatenate([local_bias, side_bias], axis=-1)
        logits = logits + bias[None, :, None]
        probs = _softmax_with_extra_logit(logits, axis=-1)
        y = jnp.einsum('bnhqk,bnkhd->bnqhd', probs, v_cat)
        y = y.reshape(B, L, H, dh)
        return jnp.einsum('blhk,hkd->bld', y, Wo)

    def _L1_cond2_ref(hidden_states, language_ids, W1, b1, W2, b2, gamma, beta):
        import jax, jax.numpy as jnp
        import numpy as np
        LN_EPS = 1e-05
        w1 = W1[language_ids]
        w2 = W2[language_ids]
        h = jnp.einsum('bsh,bha->bsa', hidden_states, w1) + b1[language_ids][:, None, :]
        h = jax.nn.relu(h)
        adapted = jnp.einsum('bsa,bah->bsh', h, w2) + b2[language_ids][:, None, :]
        x = hidden_states + adapted
        mean = jnp.mean(x, axis=-1, keepdims=True)
        var = jnp.mean(jnp.square(x - mean), axis=-1, keepdims=True)
        normed = (x - mean) * jax.lax.rsqrt(var + LN_EPS)
        return normed * gamma[language_ids][:, None, :] + beta[language_ids][:, None, :]

    def _L1_ffn_ref(x, W_r, W_k, W_v, mu_r, mu_k):
        import jax, jax.numpy as jnp
        import numpy as np
        DIM = 256

        def _reference_tuple_inner(x, W_r, W_k, W_v, mu_r, mu_k):
            B, T, C = x.shape
            x_prev = jnp.concatenate([jnp.zeros((B, 1, C), x.dtype), x[:, :-1, :]], axis=1)
            xr = mu_r * x + (1.0 - mu_r) * x_prev
            xk = mu_k * x + (1.0 - mu_k) * x_prev
            r = jax.nn.sigmoid(jnp.einsum('btc,dc->btd', xr, W_r))
            k = jnp.einsum('btc,dc->btd', xk, W_k)
            k_act = jnp.square(jax.nn.relu(k))
            out = r * jnp.einsum('btc,dc->btd', k_act, W_v)
            new_state = x[:, -1, :]
            return (out, new_state)
        return _reference_tuple_inner(x, W_r, W_k, W_v, mu_r, mu_k)[0]
    x = x + _L0_attn_ref(_L0_cond_ref(x, itok_B_0_6, L0_cond_down_w, L0_cond_down_b, L0_cond_up_w, L0_cond_up_b, L0_cond_ln_g, L0_cond_ln_b), L0_attn_key, L0_attn_value, L0_attn_time_maa_x, L0_attn_time_maa_w, L0_attn_time_maa_k, L0_attn_time_maa_v, L0_attn_time_maa_r, L0_attn_time_maa_w1, L0_attn_time_maa_w2, L0_attn_time_decay, L0_attn_time_decay_w1, L0_attn_time_decay_w2, L0_attn_time_faaaa, L0_attn_W_r, L0_attn_W_k, L0_attn_W_v, L0_attn_W_o, L0_attn_ln_w, L0_attn_ln_b)
    x = x + _L0_ffn_ref(_L0_cond2_ref(x, itok_B_0_7, L0_cond2_W1, L0_cond2_b1, L0_cond2_W2, L0_cond2_b2, L0_cond2_We, L0_cond2_be), L0_ffn_Wg, L0_ffn_W1, L0_ffn_b1, L0_ffn_W2, L0_ffn_b2)
    x = x + _L1_attn_ref(_L1_cond_ref(x, mask_SxS_bk0, itok_Sx32_0_1023, mask_Sx32_bk1, condB_uprev[:, None], L1_cond_Wq, L1_cond_bq, L1_cond_Wk, L1_cond_bk, L1_cond_Wv, L1_cond_bv, L1_cond_Wo, L1_cond_bo), L1_attn_Wq, L1_attn_Wk, L1_attn_Wv, L1_attn_Wo)
    x = x + _L1_ffn_ref(_L1_cond2_ref(x, itok_B_0_8, L1_cond2_W1, L1_cond2_b1, L1_cond2_W2, L1_cond2_b2, L1_cond2_gamma, L1_cond2_beta), L1_ffn_W_r, L1_ffn_W_k, L1_ffn_W_v, L1_ffn_mu_r, L1_ffn_mu_k)
    return x

_drawn_inputs = setup_inputs


def setup_inputs(seed=0):
    import zlib

    import numpy as np

    out = dict(_drawn_inputs(seed))
    spreads = {'L0_cond_ln_g': (1.0, 0.2),
     'L0_cond_ln_b': (0.0, 0.1),
     'L0_attn_ln_w': (1.0, 0.2),
     'L0_attn_ln_b': (0.0, 0.1),
     'L0_ffn_b1': (0.0, 0.362),
     'L0_ffn_b2': (0.0, 0.1),
     'L1_cond_bq': (0.0, 0.8),
     'L1_cond_bk': (0.0, 0.8),
     'L1_cond_bv': (0.0, 0.1),
     'L1_cond_bo': (0.0, 0.1),
     'L1_cond2_b1': (0.0, 0.8),
     'L1_cond2_b2': (0.0, 0.8),
     'L1_cond2_gamma': (1.0, 0.6),
     'L1_cond2_beta': (0.0, 0.716)}
    factors = {'L0_cond_down_b': 7.544,
     'L0_cond_up_b': 4.7,
     'L0_attn_time_maa_x': 8.0,
     'L0_attn_time_maa_w': 8.0,
     'L0_attn_time_decay_w1': 8.0,
     'L0_attn_time_decay_w2': 7.905,
     'L0_attn_time_faaaa': 3.414,
     'L0_cond2_b1': 3.878,
     'L0_cond2_be': 3.513,
     'L0_ffn_W1': 4.177,
     'L1_cond_Wq': 4.316,
     'L1_cond_Wk': 3.063,
     'L1_attn_Wq': 6.11,
     'L1_attn_Wk': 5.961,
     'L1_ffn_mu_r': 6.013}
    for name, (base, spread) in spreads.items():
        noise = np.random.default_rng([zlib.crc32(name.encode()), seed]).standard_normal(out[name].shape)
        drawn = base * np.exp(spread * noise) if base else spread * noise
        out[name] = jnp.asarray(drawn.astype(out[name].dtype))
    for name, factor in factors.items():
        out[name] = (out[name] * factor).astype(out[name].dtype)
    return out
```

```python
from contextlib import ExitStack

import numpy as np

import concourse.bass as bass
from concourse import mybir

F32 = mybir.dt.float32
BF16 = mybir.dt.bfloat16
I32 = mybir.dt.int32
U32 = mybir.dt.uint32
U8 = mybir.dt.uint8
ALU = mybir.AluOpType
ACT = mybir.ActivationFunctionType
AX = mybir.AxisListType

P = 128
B = 2
S = 1024
D = 256
N = B * S
NT = N // P
TB_ = S // P
E = 8
FH = 1024
CAP = 512
ENG = ("pe", "act", "dve", "pool", "sp")


class Prog:

    def __init__(self, nc, ctx):
        self.nc, self.ctx = nc, ctx
        self.q = {e: [] for e in ENG}
        self.n = {}
        self.seen = {e: {} for e in ENG}
        self.sem = {}
        self.k = 0
        self.bar = []
        self.phase("p0")

    def new_sem(self, name):
        self.k += 1
        s = self.ctx.enter_context(self.nc.semaphore(f"{name}_{self.k}"))
        self.n[s] = 0
        return s

    def phase(self, name):
        for e in ("pe", "act", "dve", "pool"):
            self.sem[e] = self.new_sem(f"{name}_{e}")

    def wait(self, e, *hs):
        for h in hs:
            if h is None:
                continue
            if isinstance(h, list):
                self.wait(e, *h)
                continue
            s, v = h
            if self.seen[e].get(s, 0) < v:
                self.seen[e][s] = v
                self.q[e].append(lambda eng, s=s, v=v: eng.wait_ge(s, v))

    def op(self, e, fn, *waits, inc=True):
        self.wait(e, *waits)
        if not inc:
            self.q[e].append(lambda eng: fn(eng))
            return None
        s = self.sem[e]
        self.n[s] += 1
        self.q[e].append(lambda eng, s=s: fn(eng).then_inc(s, 1))
        return (s, self.n[s])

    def dma(self, e, sem, fn, *waits):
        self.wait(e, *waits)
        self.n[sem] += 16
        self.q[e].append(lambda eng, s=sem: fn(eng).then_inc(s, 16))
        return (sem, self.n[sem])

    def barrier(self, name):
        last = [(self.sem[e], self.n[self.sem[e]]) for e in ("pe", "act", "dve", "pool")]
        last = [h for h in last if h[1]]
        self.bar = last
        for e in ("pe", "act", "dve", "pool"):
            self.wait(e, *last)
        self.phase(name)
        return last


class Arena:

    def __init__(self, t, size):
        self.t, self.size, self.lo, self.hi = t, size, 0, size

    def up(self, n, dt=F32):
        a, self.lo = self.lo, self.lo + n
        assert self.lo <= self.hi, (self.lo, self.hi)
        v = self.t[:, a:a + n]
        return v if dt == F32 else v.bitcast(dt)

    def down(self, n):
        self.hi -= n
        assert self.lo <= self.hi, (self.lo, self.hi)
        return self.t[:, self.hi:self.hi + n]


CV = ["maa_x", "maa_w", "maa_k", "maa_v", "maa_r", "decay", "faaaa", "ln_w", "ln_b", "bq", "bk", "mu_r", "mu_k", "bo"]
CIDX = {n: 2 * i for i, n in enumerate(CV)}
CB1 = 2 * len(CV)
NCV = CB1 + 8 + 64


def build(nc, a, out, dbg=None):
    with ExitStack() as ctx:
        pr = Prog(nc, ctx)
        op, dma = pr.op, pr.dma
        WORDS = 52600
        arena = Arena(ctx.enter_context(nc.sbuf_tensor("arena", [P, WORDS], F32)), WORDS)
        PS = ctx.enter_context(nc.psum_tensor("PS", [P, 8, 512], F32))
        bank_free = [[] for _ in range(8)]
        bank_at = [0]

        def bank():
            i = bank_at[0]
            bank_at[0] = (i + 1) % 8
            return i, bank_free[i]

        def mm(out_, lhsT, rhs, start, stop, waits=(), inc=None):
            return op("pe", lambda e: e.matmul(out_, lhsT, rhs, start=start, stop=stop), *waits,
                      inc=stop if inc is None else inc)

        ident = arena.up(P)
        headb = arena.up(P)
        triu = arena.up(P)
        onesm = arena.up(P)
        cvec = arena.up(NCV)
        X = arena.up(NT * D).rearrange("p (t c) -> p t c", t=NT)
        s_c = pr.new_sem("s_c")
        h_cst = [dma("sp", s_c, lambda e: e.dma_start(ident, a["k_ident"])),
                 dma("sp", s_c, lambda e: e.dma_start(cvec, a["cvec"])),
                 dma("sp", s_c, lambda e: e.dma_start(headb, a["k_headb"])),
                 dma("sp", s_c, lambda e: e.dma_start(triu, a["k_triu"]))][-1]

        def cv(name, c):
            i = CIDX[name] + c
            return cvec[:, i:i + 1]

        kslot = arena.up(24)
        dma("sp", s_c, lambda e: e.dma_start(kslot, a["k_slot"]))
        ids = arena.up(8).bitcast(I32)
        h_ids = dma("sp", s_c, lambda e: e.dma_start(ids[0:1, 0:6], a["ids"]))
        h_cst = h_ids
        h_ones = op("pool", lambda e: e.memset(onesm, 1.0))
        regs = {}

        def load_id(i, n):
            def f(e):
                regs[i] = e.value_load(ids[0:1, i:i + 1], min_val=0, max_val=n - 1)
            pr.wait("sp", h_ids)
            pr.q["sp"].append(f)

        def load(sem, dst, src, *waits):
            return dma("sp", sem, lambda e: e.dma_start(dst, src), *waits)

        def load_by(sem, dst, src_of, i, *waits):
            return dma("sp", sem, lambda e: e.dma_start(dst, src_of(regs[i])), *waits)

        def kmaj(name, c=2):
            return a[name].rearrange("(c p) n -> p c n", c=c)

        base0 = arena.lo
        Xg = nc.dram_tensor("xg", (2 * E * CAP, D), F32, kind="Internal").ap()
        Ye = nc.dram_tensor("ye", (E * CAP, D), F32, kind="Internal").ap()
        s_x = pr.new_sem("s_x")

        def adapter(tag, bi, K, n_ids, idx0, down, down_b, up, up_b, gb, srcT, dstT, waits, wb):
            sem = pr.new_sem("s_ad")
            wd, wu, small, bub, zT, xb, y, st = wb
            load_id(idx0 + bi, n_ids)
            load_by(sem, wd, lambda r: a[down].rearrange("e (c p) k -> e p c k", c=2)[bass.ds(r, 1)].rearrange("e p c k -> (e p) c k"), idx0 + bi, *waits)
            load_by(sem, wu[0:K], lambda r: a[up][bass.ds(r, 1)].rearrange("e k h -> (e k) h"), idx0 + bi)
            load_by(sem, small, lambda r: a[gb][bass.ds(r, 1)].rearrange("e p c -> (e p) c"), idx0 + bi)
            h_w = load_by(sem, bub, lambda r: a[up_b][bass.ds(r, 1)].rearrange("e h -> (e h)").partition_broadcast(P), idx0 + bi)
            xs = X[:, TB_ * bi:TB_ * bi + TB_, :]
            h_xb = op("pool", lambda e: e.tensor_tensor(xb, xs, bub.unsqueeze(1).broadcast_to([P, TB_, D]), ALU.add), h_w, *waits)
            hz = []
            for n in range(2):
                i, fr = bank()
                for c in range(2):
                    h = mm(PS[0:K, i, :], wd[:, c, :], srcT[:, c, 512 * n:512 * n + 512], c == 0, c == 1, [h_w, fr, waits])
                h = op("act", lambda e, i=i, n=n: e.activation(zT[0:K, 512 * n:512 * n + 512], PS[0:K, i, :], ACT.Relu, bias=small[0:K, 4:5]), h)
                bank_free[i] = [h]
                hz.append(h)
            hy = []
            for t in range(TB_):
                i, fr = bank()
                h = mm(PS[:, i, 0:D], zT[0:K, P * t:P * t + P], wu[0:K, :], True, True, [hz[t // 4], fr])
                h = op("dve", lambda e, i=i, t=t: e.tensor_tensor(y[:, t, :], PS[:, i, 0:D], xb[:, t, :], ALU.add), h, h_xb)
                bank_free[i] = [h]
                h = op("dve", lambda e, t=t: e.bn_stats(st[:, 6 * t:6 * t + 6], y[:, t, :]), h)
                hy.append(h)
            mv = st[:, 48:64].rearrange("p (t k) -> p t k", k=2)
            for t in range(TB_):
                h = op("dve", lambda e, t=t: e.bn_aggr(mv[:, t, :], st[:, 6 * t:6 * t + 6]), hy[t])
            h = op("dve", lambda e: e.tensor_scalar(st[:, 64:72], mv[:, :, 1], 1e-5, None, ALU.add), h)
            h = op("act", lambda e: e.activation(st[:, 72:80], st[:, 64:72], ACT.Sqrt), h)
            h = op("dve", lambda e: e.reciprocal(st[:, 80:88], st[:, 72:80]), h)
            hn = []
            for t in range(TB_):
                h2 = op("dve", lambda e, t=t: e.tensor_scalar(y[:, t, :], y[:, t, :], mv[:, t, 0:1], st[:, 80 + t:81 + t], ALU.subtract, ALU.mult), h)
                hn.append(h2)
            last = []
            for c in range(2):
                for g in range(2):
                    i, fr = bank()
                    for j in range(4):
                        t = 4 * g + j
                        h = op("pe", lambda e, i=i, j=j, t=t, c=c: e.transpose(PS[:, i, P * j:P * j + P], y[:, t, P * c:P * c + P], ident), hn[t], fr, h_cst, inc=(j == 3))
                    h = op("act", lambda e, i=i, c=c, g=g: e.activation(dstT[:, c, 512 * g:512 * g + 512], PS[:, i, :], ACT.Identity, bias=small[:, 2 + c:3 + c], scale=small[:, c:c + 1]), h)
                    bank_free[i] = [h]
                    last.append(h)
            return last

        def adapter_space(K):
            return (arena.up(2 * K).rearrange("p (c k) -> p c k", c=2), arena.up(D), arena.up(8)[:, 0:5], arena.up(D),
                    arena.up(S), arena.up(TB_ * D).rearrange("p (t c) -> p t c", t=TB_),
                    arena.up(TB_ * D).rearrange("p (t c) -> p t c", t=TB_), arena.up(96))

        def to_T(src, dst, waits, eng="act"):
            last = []
            for g in range(2):
                for c in range(2):
                    i, fr = bank()
                    for j in range(4):
                        t = 4 * g + j
                        h = op("pe", lambda e, i=i, j=j, t=t, c=c: e.transpose(PS[:, i, P * j:P * j + P], src[:, t, P * c:P * c + P], ident), fr, waits, inc=(j == 3))
                    if eng == "act":
                        h = op("act", lambda e, i=i, c=c, g=g: e.copy(dst[:, c, 512 * g:512 * g + 512], PS[:, i, :]), h)
                    else:
                        h = op("dve", lambda e, i=i, c=c, g=g: e.tensor_copy(dst[:, c, 512 * g:512 * g + 512], PS[:, i, :]), h)
                    bank_free[i] = [h]
                    last.append(h)
            return last

        def finish():
            last = [(pr.sem[e], pr.n[pr.sem[e]]) for e in ("pe", "act", "dve", "pool") if pr.n[pr.sem[e]]] or pr.bar
            s_o = pr.new_sem("s_o")
            for b in range(B):
                h = dma("sp", s_o, lambda e, b=b: e.dma_start(out.rearrange("(t p) c -> p t c", p=P)[:, TB_ * b:TB_ * b + TB_, :], X[:, TB_ * b:TB_ * b + TB_, :]), last)
            pr.wait("sp", h)
            with nc.Block() as block:
                for name, eng in (("sync", "sp"), ("tensor", "pe"), ("scalar", "act"), ("vector", "dve"), ("gpsimd", "pool")):
                    def run(e, items=pr.q[eng]):
                        for it in items:
                            it(e)
                    {"sync": block.sync, "tensor": block.tensor, "scalar": block.scalar, "vector": block.vector, "gpsimd": block.gpsimd}[name](run)

        hi0 = arena.hi
        W1c = arena.down(2 * FH).rearrange("p (c n) -> p c n", c=2)
        Wc = [arena.down(8 * D).rearrange("p (f n) -> p f n", f=8) for _ in range(B)]
        bc = [arena.down(D) for _ in range(B)]
        Wg = arena.down(16).rearrange("p (c n) -> p c n", c=2)
        mark = arena.lo
        w1 = arena.up(2 * P).rearrange("p (c n) -> p c n", c=2)
        w2 = arena.up(D)
        dw1 = arena.up(2 * 64).rearrange("p (c n) -> p c n", c=2)
        dw2 = arena.up(D)
        Wr, Wk, Wv, Wo = (arena.up(2 * D).rearrange("p (c n) -> p c n", c=2) for _ in range(4))
        hT2 = [arena.up(2 * S).rearrange("p (c s) -> p c s", c=2) for _ in range(B)]
        mark2 = arena.lo
        s_w = pr.new_sem("s_w")
        for b in range(B):
            h_x = load(s_x, hT2[b], a["xT"].rearrange("(c p) n -> p c n", c=2)[:, :, S * b:S * b + S])
            h_x = load(s_x, X[:, TB_ * b:TB_ * b + TB_, :], a["x"].rearrange("(t p) c -> p t c", p=P)[:, TB_ * b:TB_ * b + TB_, :])
        wA = adapter_space(P)
        h_a = [h_x]
        for b in range(B):
            h_a = adapter("a", b, P, 8, 0, "L0_cond_down_w", None, "L0_cond_up_w", "L0_cond_up_b", "gb0", hT2[b], hT2[b], h_a, wA)
            if b == 0:
                load(s_w, w1, kmaj("L0_attn_time_maa_w1"))
                load(s_w, w2, a["L0_attn_time_maa_w2"])
                load(s_w, dw1, kmaj("L0_attn_time_decay_w1"))
                load(s_w, dw2[0:64], a["L0_attn_time_decay_w2"])
                for w_, n_ in ((Wr, "r"), (Wk, "k"), (Wv, "v"), (Wo, "o")):
                    h_w = load(s_w, w_, kmaj("L0_attn_W_" + n_))
        s_wc = pr.new_sem("s_wc")
        load(s_wc, W1c, kmaj("L0_cond2_W1"))
        for b in range(B):
            load_id(2 + b, E)
            load(s_wc, Wc[b][:, :, 0:192], a["L0_cond2_W2"].rearrange("(f p) n -> p f n", f=8))
            load_by(s_wc, Wc[b][:, :, 192:256], lambda r: a["L0_cond2_We"].rearrange("e (f p) n -> e p f n", f=8)[bass.ds(r, 1)].rearrange("e p f n -> (e p) f n"), 2 + b)
            load(s_wc, bc[b][:, 0:192], a["L0_cond2_b2"].partition_broadcast(P))
            load_by(s_wc, bc[b][:, 192:256], lambda r: a["L0_cond2_be"][bass.ds(r, 1)].rearrange("e n -> (e n)").partition_broadcast(P), 2 + b)
        h_wc = load(s_wc, Wg, kmaj("L0_ffn_Wg"))
        pr.barrier("b")
        arena.lo = mark2

        def full():
            return arena.up(2 * S).rearrange("p (c s) -> p c s", c=2)

        xx, tmp, xf = full(), full(), full()
        rT, kT, vT, wT, yl = full(), full(), full(), full(), full()
        vtok = arena.up(TB_ * D).rearrange("p (t c) -> p t c", t=TB_)
        mT = arena.up(S)
        Gb = tmp
        rg = xx
        tp2 = [arena.up(512) for _ in range(4)]
        tp_free = [[] for _ in range(4)]
        KR, RR = full(), full()
        rp = full()
        Wb = arena.up(P)
        PB = arena.up(P)
        TD = arena.up(16).rearrange("p (c n) -> p c n", c=2)
        KD = [arena.up(S) for _ in range(2)]
        AT = arena.up(16 * P).rearrange("p (n h t) -> p n h t", n=8, h=2)
        KE = mT
        St = arena.up(2 * 9 * 64).rearrange("p (c n j) -> p c n j", c=2, n=9)
        ytok, rpp = xf.rearrange("p c s -> p (c s)").rearrange("p (t c) -> p t c", t=TB_), RR
        st = arena.up(6 * 32 + 2 * 32 + 96)
        h0 = [op("dve", lambda e: e.memset(AT[:, :, :, 0:16], 0.0))]
        h0b = None

        hprev = []
        for b in range(B):
            hT = hT2[b]
            h1 = op("dve", lambda e, hT=hT: e.tensor_tensor(xx[:, :, 1:S], hT[:, :, 0:S - 1], hT[:, :, 1:S], ALU.subtract), hprev)
            h2 = op("dve", lambda e, hT=hT: e.tensor_scalar(xx[:, :, 0:1], hT[:, :, 0:1], -1.0, None, ALU.mult))
            hx = []
            for c in range(2):
                hx.append(op("dve", lambda e, c=c, hT=hT: e.scalar_tensor_tensor(out=tmp[:, c], in0=xx[:, c], scalar=cv("maa_x", c), in1=hT[:, c], op0=ALU.mult, op1=ALU.add), h1, h2, h_cst))
            hm = []
            for n in range(2):
                i, fr = bank()
                for c in range(2):
                    h = mm(PS[:, i, :], w1[:, c, :], tmp[:, c, 512 * n:512 * n + 512], c == 0, c == 1, [h_w, fr, hx])
                h = op("act", lambda e, i=i, n=n: e.activation(mT[:, 512 * n:512 * n + 512], PS[:, i, :], ACT.Tanh), h)
                bank_free[i] = [h]
                hm.append(h)
            hxf_rd = [hx]
            bufs = [tmp, xf]
            rd = [[hm], [hprev]]
            ek = {}
            for q, (f, nm) in enumerate(((0, "w"), (1, "k"), (2, "v"), (3, "r"))):
                dst = bufs[q % 2]
                hf = []
                for c in range(2):
                    for n in range(2):
                        i, fr = bank()
                        sl = slice(512 * n, 512 * n + 512)
                        h = mm(PS[:, i, :], w2[32 * f:32 * f + 32, P * c:P * c + P], mT[32 * f:32 * f + 32, sl], True, True, [fr, hm])
                        h = op("dve", lambda e, i=i, c=c, sl=sl, dst=dst, nm=nm: e.scalar_tensor_tensor(out=dst[:, c, sl], in0=PS[:, i, :], scalar=cv("maa_" + nm, c), in1=xx[:, c, sl], op0=ALU.add, op1=ALU.mult), h, rd[q % 2])
                        bank_free[i] = [h]
                        h = op("pool", lambda e, c=c, sl=sl, dst=dst, hT=hT: e.tensor_tensor(dst[:, c, sl], dst[:, c, sl], hT[:, c, sl], ALU.add), h)
                        hf.append(h)
                if nm == "w":
                    hw2 = []
                    for n in range(2):
                        sl = slice(512 * n, 512 * n + 512)
                        i, fr = bank()
                        for c in range(2):
                            h = mm(PS[0:64, i, :], dw1[:, c, :], dst[:, c, sl], c == 0, c == 1, [fr, hf])
                        h = op("act", lambda e, i=i, sl=sl: e.activation(yl[0:64, 0, sl], PS[0:64, i, :], ACT.Tanh), h, hprev)
                        bank_free[i] = [h]
                        hw2.append(h)
                    rd[q % 2] = [hw2]
                    hw = []
                    for c in range(2):
                        for n in range(2):
                            sl = slice(512 * n, 512 * n + 512)
                            i, fr = bank()
                            h = mm(PS[:, i, :], dw2[0:64, P * c:P * c + P], yl[0:64, 0, sl], True, True, [fr, hw2[n]])
                            h = op("act", lambda e, i=i, c=c, sl=sl: e.activation(wT[:, c, sl], PS[:, i, :], ACT.Exp, bias=cv("decay", c)), h)
                            bank_free[i] = [h]
                            h = op("act", lambda e, c=c, sl=sl: e.activation(wT[:, c, sl], wT[:, c, sl], ACT.Exp, scale=-1.0), h)
                            hw.append(h)
                    continue
                Wm = {"k": Wk, "v": Wv, "r": Wr}[nm]
                dT = {"k": kT, "v": vT, "r": rT}[nm]
                hh = []
                for c in range(2):
                    for n in range(2):
                        sl = slice(512 * n, 512 * n + 512)
                        i, fr = bank()
                        for k in range(2):
                            h = mm(PS[:, i, :], Wm[:, k, P * c:P * c + P], dst[:, k, sl], k == 0, k == 1, [fr, hf])
                        h = op("act", lambda e, i=i, c=c, sl=sl, dT=dT: e.copy(dT[:, c, sl], PS[:, i, :]), h, hprev)
                        bank_free[i] = [h]
                        hh.append(h)
                if nm == "v":
                    for t in range(0, TB_, 2):
                        i, fr = bank()
                        for j in range(2):
                            for k in range(2):
                                h = mm(PS[:, i, D * j:D * j + D], dst[:, k, P * (t + j):P * (t + j) + P], Wm[:, k, :], k == 0, k == 1, [fr, hf])
                        h = op("act", lambda e, i=i, t=t: e.copy(vtok[:, t:t + 2, :], PS[:, i, :].rearrange("p (a c) -> p a c", a=2)), h, hprev)
                        bank_free[i] = [h]
                        hh.append(h)
                rd[q % 2] = [hh]
                ek[nm] = hh
            hk, hv, hr = ek["k"], ek["v"], ek["r"]
            w4, r4, k4, v4 = (z.rearrange("p c (m l) -> p (c m) l", l=16) for z in (wT, rT, kT, vT))
            KR4, RR4, rp4 = (z.rearrange("p c (m l) -> p (c m) l", l=16) for z in (KR, RR, rp))
            h = op("dve", lambda e: e.memset(RR4[:, :, 0:1], 1.0), hprev)
            hR = op("pool", lambda e: e.memset(KR4[:, :, 15:16], 1.0), hprev)
            for j in range(1, 16):
                h = op("dve", lambda e, j=j: e.tensor_tensor(RR4[:, :, j:j + 1], RR4[:, :, j - 1:j], w4[:, :, j - 1:j], ALU.mult), h, hw)
                hR = op("pool", lambda e, j=j: e.tensor_tensor(KR4[:, :, 15 - j:16 - j], KR4[:, :, 16 - j:17 - j], w4[:, :, 16 - j:17 - j], ALU.mult), hR, hw)
            hWb = op("dve", lambda e: e.tensor_tensor(Wb.unsqueeze(2), RR4[:, :, 15:16], w4[:, :, 15:16], ALU.mult), h)
            hKR = op("pool", lambda e: e.tensor_tensor(KR, KR, kT, ALU.mult), hR, hk)
            hrp = op("dve", lambda e: e.tensor_tensor(rp, RR, rT, ALU.mult), h, hr)
            Wb4 = Wb.rearrange("p (c n a) -> p c n a", c=2, a=8)
            PB4 = PB.rearrange("p (c n a) -> p c n a", c=2, a=8)
            h = op("dve", lambda e: e.memset(PB4[:, :, :, 0:1], 1.0), hprev)
            for j in range(1, 8):
                h = op("dve", lambda e, j=j: e.tensor_tensor(PB4[:, :, :, j:j + 1], PB4[:, :, :, j - 1:j], Wb4[:, :, :, j - 1:j], ALU.mult), h, hWb)
            hTD = op("dve", lambda e: e.tensor_tensor(TD.unsqueeze(3), PB4[:, :, :, 7:8], Wb4[:, :, :, 7:8], ALU.mult), h)
            hrpp = op("dve", lambda e: e.tensor_tensor(RR4, rp4, PB.unsqueeze(2).broadcast_to([P, P, 16]), ALU.mult), h, hrp)

            hG = op("act", lambda e: e.copy(Gb, kT), hk, rd[0], rd[1])
            for c in range(2):
                hrg = op("dve", lambda e, c=c: e.scalar_tensor_tensor(out=rg[:, c], in0=rT[:, c], scalar=cv("faaaa", c), in1=kT[:, c], op0=ALU.mult, op1=ALU.mult), hr, hk, hf)
            G4, rg4, y4 = (z.rearrange("p c (m l) -> p (c m) l", l=16) for z in (Gb, rg, yl))
            h_rgrd = []
            hyl = [None] * 4
            for dl in range(16):
                L = 16 - dl
                if dl:
                    hrg = op("pool", lambda e, dl=dl, L=L: e.tensor_tensor(rg4[:, :, 0:L], r4[:, :, dl:16], G4[:, :, 0:L], ALU.mult), hG, h_rgrd)
                    if dl < 15:
                        hG = op("dve", lambda e, dl=dl, L=L: e.tensor_tensor(G4[:, :, 0:L - 1], G4[:, :, 0:L - 1], w4[:, :, dl:15], ALU.mult), hrg, hw)
                h_rgrd = []
                for g in range(4):
                    i, fr = bank()
                    ms = slice(32 * g, 32 * g + 32)
                    pv = PS[:, i, 0:32 * L].rearrange("p (m l) -> p m l", l=L)
                    h = mm(PS[:, i, 0:32 * L], headb, rg4[:, ms, 0:L], True, True, [fr, hrg, h_cst])
                    h_rgrd.append(h)
                    if dl == 0:
                        h = op("dve", lambda e, pv=pv, ms=ms: e.tensor_tensor(y4[:, ms, :], pv, v4[:, ms, :], ALU.mult), h, hv, hw)
                        bank_free[i] = [h]
                        hyl[g] = h
                        continue
                    tb = tp2[g][:, 0:32 * L].rearrange("p (m l) -> p m l", l=L)
                    h = op("dve", lambda e, pv=pv, ms=ms, tb=tb, L=L: e.tensor_tensor(tb, pv, v4[:, ms, 0:L], ALU.mult), h, tp_free[g])
                    bank_free[i] = [h]
                    h = op("pool", lambda e, ms=ms, tb=tb, dl=dl: e.tensor_tensor(y4[:, ms, dl:16], y4[:, ms, dl:16], tb, ALU.add), h, hyl[g])
                    hyl[g] = h
                    tp_free[g] = [h]

            hSt = []
            hy = []
            KRn = KR.rearrange("p c (n s) -> p c n s", n=8)
            for c in range(2):
                KDv = [z.rearrange("p (n s) -> p n s", n=8) for z in KD]
                hz = [op("pool", lambda e, z=z: e.memset(z, 0.0), h_kd if (b or c) else []) for z in KD]
                kd_rd = [[hz[0]], [hz[1]]]
                hkd = None
                banks = [bank() for _ in range(4)]
                for q in range(1, 9):
                    cur, old = KDv[q % 2], KDv[(q - 1) % 2]
                    h1 = op("act", lambda e, cur=cur, q=q, c=c: e.copy(cur[:, :, 16 * (q - 1):16 * q], KRn[:, c, :, 16 * (q - 1):16 * q]), hKR, kd_rd[q % 2])
                    h2 = None
                    if q > 1:
                        h2 = op("dve", lambda e, cur=cur, old=old, q=q, c=c: e.tensor_tensor(cur[:, :, 0:16 * (q - 1)], old[:, :, 0:16 * (q - 1)], Wb4[:, c, :, q - 1:q].broadcast_to([P, 8, 16 * (q - 1)]), ALU.mult), hkd, kd_rd[q % 2], hWb)
                    hkd = [h1, h2]
                    if q == 8:
                        break
                    for n in range(8):
                        for hh_ in range(2):
                            i, fr = banks[2 * (n // 4) + hh_]
                            col = P * (n % 4) + 16 * q
                            rows = slice(64 * hh_, 64 * hh_ + 64)
                            h = mm(PS[:, i, col:col + 16], cur[rows, n, :], rp[rows, c, P * n + 16 * q:P * n + 16 * q + 16], True, True, [fr, hkd, hrp], inc=(n == 7 and hh_ == 1))
                    kd_rd[q % 2] = [h, h2]
                    kd_rd[(q - 1) % 2] = kd_rd[(q - 1) % 2] + [h2]
                hAT = []
                for k in range(4):
                    i = banks[k][0]
                    h3 = op("act", lambda e, i=i, k=k: e.copy(AT[:, 4 * (k // 2):4 * (k // 2) + 4, k % 2, 16:P], PS[:, i, :].rearrange("p (n t) -> p n t", n=4)[:, :, 16:P]), h, hSt, hy)
                    bank_free[i] = [h3]
                    hAT.append(h3)
                hKE = []
                for g in range(2):
                    i, fr = bank()
                    for j in range(4):
                        n = 4 * g + j
                        h = op("pe", lambda e, i=i, j=j, n=n: e.transpose(PS[:, i, P * j:P * j + P], KDv[0][:, n, :], ident), fr, hkd, inc=(j == 3))
                    h_kd = [h]
                    h = op("act", lambda e, i=i, g=g: e.copy(KE[:, 512 * g:512 * g + 512], PS[:, i, :]), h, hSt)
                    bank_free[i] = [h]
                    hKE.append(h)
                i, fr = bank()
                for n in range(8):
                    for hh_ in range(2):
                        ch = P * c + 64 * hh_
                        h = mm(PS[64 * hh_:64 * hh_ + 64, i, 64 * n:64 * n + 64], KE[:, P * n + 64 * hh_:P * n + 64 * hh_ + 64], vtok[:, n, ch:ch + 64], True, True, [fr, hKE, hv], inc=(n == 7 and hh_ == 1))
                hs = op("dve", lambda e, c=c: e.memset(St[:, c, 0, :], 0.0), hy)
                for n in range(7):
                    hs = op("dve", lambda e, c=c, n=n, i=i: e.scalar_tensor_tensor(out=St[:, c, n + 1, :], in0=St[:, c, n, :], scalar=TD[:, c, n:n + 1], in1=PS[:, i, 64 * n:64 * n + 64], op0=ALU.mult, op1=ALU.add), h, hs, hTD)
                bank_free[i] = [hs]
                hSt = [h, hs]
                hy = []
                for hh_ in range(2):
                    i, fr = bank()
                    rows = slice(64 * hh_, 64 * hh_ + 64)
                    ch = P * c + 64 * hh_
                    for t in range(8):
                        o = PS[:, i, 64 * t:64 * t + 64]
                        mm(o, AT[:, t, hh_, :], vtok[:, t, ch:ch + 64], True, False, [fr, hAT, hs, hyl, hrpp, h0])
                        mm(o, RR[rows, c, P * t:P * t + P], St[rows, c, t, :], False, False)
                        h = mm(o, yl[:, c, P * t:P * t + P], ident[:, 64 * hh_:64 * hh_ + 64], False, True, inc=(t == 7))
                    h2 = op("act", lambda e, i=i, ch=ch: e.copy(ytok[:, :, ch:ch + 64], PS[:, i, :].rearrange("p (j x) -> p j x", j=8)), h, rd[1])
                    bank_free[i] = [h2]
                    hy.append(h2)
                hy_all = hy if c == 0 else hy_all + hy
            yg = ytok.rearrange("p t (h j) -> p (t h) j", j=64)
            mv = st[:, 192:256].rearrange("p (g k) -> p g k", k=2)
            for g in range(32):
                h = op("dve", lambda e, g=g: e.bn_stats(st[:, 6 * g:6 * g + 6], yg[:, g, :]), hy_all)
            for g in range(32):
                h = op("dve", lambda e, g=g: e.bn_aggr(mv[:, g, :], st[:, 6 * g:6 * g + 6]), h if g == 0 else None)
            h = op("dve", lambda e: e.tensor_scalar(st[:, 256:288], mv[:, :, 1], 0.00064, None, ALU.add), h)
            h = op("act", lambda e: e.activation(st[:, 288:320], st[:, 256:288], ACT.Sqrt), h)
            h = op("dve", lambda e: e.reciprocal(st[:, 320:352], st[:, 288:320]), h)
            h = op("dve", lambda e: e.tensor_tensor(yg, yg, mv[:, :, 0:1].broadcast_to([P, 32, 64]), ALU.subtract), h)
            h = op("dve", lambda e: e.tensor_tensor(yg, yg, st[:, 320:352].unsqueeze(2).broadcast_to([P, 32, 64]), ALU.mult), h)
            hyn = h
            hT_n = []
            for c in range(2):
                for g in range(2):
                    i, fr = bank()
                    for j in range(4):
                        t = 4 * g + j
                        h = op("pe", lambda e, i=i, j=j, t=t, c=c: e.transpose(PS[:, i, P * j:P * j + P], ytok[:, t, P * c:P * c + P], ident), fr, hyn, inc=(j == 3))
                    h = op("act", lambda e, i=i, c=c, g=g: e.activation(tmp[:, c, 512 * g:512 * g + 512], PS[:, i, :], ACT.Identity, bias=cv("ln_b", c), scale=cv("ln_w", c)), h, hG, hrg)
                    bank_free[i] = [h]
                    hT_n.append(h)
            for t in range(0, TB_, 2):
                i, fr = bank()
                for j in range(2):
                    for k in range(2):
                        h = mm(PS[:, i, D * j:D * j + D], tmp[:, k, P * (t + j):P * (t + j) + P], Wo[:, k, :], k == 0, k == 1, [fr, hT_n])
                xs = X[:, TB_ * b + t:TB_ * b + t + 2, :]
                h = op("dve", lambda e, i=i, xs=xs: e.tensor_tensor(xs, xs, PS[:, i, :].rearrange("p (a c) -> p a c", a=2), ALU.add), h)
                bank_free[i] = [h]
            hprev = [(pr.sem[e], pr.n[pr.sem[e]]) for e in ("pe", "act", "dve", "pool")]
        bar = pr.barrier("c")
        if dbg == "x0":
            return finish()

        arena.lo = base0
        CN = arena.up(4 * S).bitcast(BF16).rearrange("p (t k) -> p t k", t=TB_)
        PM = arena.up(2 * S).bitcast(U8).rearrange("p (t k) -> p t k", t=TB_)
        e_mark = arena.lo
        C1 = arena.up(NT * D).rearrange("p (t c) -> p t c", t=NT)
        c_mark = arena.lo
        b2e = arena.up(E * D)
        s_b2 = pr.new_sem("s_b2")
        h_wc = [h_wc, load(s_b2, b2e, a["L0_ffn_b2"].rearrange("e c -> (e c)").partition_broadcast(P), bar)]
        NEX = 2
        exw = [(arena.up(2 * FH).rearrange("p (c n) -> p c n", c=2), arena.up(8 * D).rearrange("p (f n) -> p f n", f=8)) for _ in range(NEX)]
        h_ex = {}
        s_ex = [pr.new_sem("s_ex") for _ in range(NEX)]

        def get_w(e_, waits=()):
            load(s_ex[e_ % NEX], exw[e_ % NEX][0], a["L0_ffn_W1"][e_].rearrange("(c p) n -> p c n", c=2), *waits)
            h_ex[e_] = load(s_ex[e_ % NEX], exw[e_ % NEX][1], a["L0_ffn_W2"][e_].rearrange("(f p) n -> p f n", f=8))

        for e_ in range(NEX):
            get_w(e_, [bar])
        zt = arena.up(2048)
        iota = arena.up(S)
        pki = arena.up(TB_ * 32).bitcast(I32).rearrange("p (t j) -> p t j", t=TB_)
        pkf = arena.up(TB_ * 32).rearrange("p (t j) -> p t j", t=TB_)
        pkm = arena.up(TB_ * 8).bitcast(U8).rearrange("p (t j) -> p t j", t=TB_)
        hit = arena.up(S // 2).bitcast(BF16)
        pkmf = arena.up(TB_ * 32).rearrange("p (t j) -> p t j", t=TB_)
        s_pk = pr.new_sem("s_pk")
        load(s_pk, iota, a["k_iota"])
        load(s_pk, pki, a["idx"].rearrange("(t p) j -> p t j", p=P))
        load(s_pk, pkm, a["imask"].rearrange("(t p) j -> p t j", p=P))
        h_pk = load(s_pk, PM, a["pmask"].rearrange("(t p) k -> p t k", p=P))
        h = op("pool", lambda e: e.tensor_copy(pkf, pki), h_pk)
        h = op("pool", lambda e: e.tensor_scalar(pkf, pkf, 1.0, None, ALU.add), h)
        h2 = op("pool", lambda e: e.tensor_copy(pkmf, pkm), h_pk)
        h = op("pool", lambda e: e.tensor_tensor(pkf, pkf, pkmf, ALU.mult), h, h2)
        h = op("pool", lambda e: e.tensor_scalar(pkf, pkf, 1.0, None, ALU.subtract), h)
        h_pkf = h

        def count(eng, t, j, h):
            col = pkf[:, t, j:j + 1]
            if j == 0:
                return op(eng, lambda e: e.tensor_scalar(CN[:, t, :], iota, col, None, ALU.is_equal), h_pkf)
            if eng == "dve":
                return op(eng, lambda e: e.scalar_tensor_tensor(out=CN[:, t, :], in0=iota, scalar=col, in1=CN[:, t, :], op0=ALU.is_equal, op1=ALU.add), h)
            h = op(eng, lambda e: e.tensor_scalar(hit, iota, col, None, ALU.is_equal), h)
            return op(eng, lambda e: e.tensor_tensor(CN[:, t, :], CN[:, t, :], hit, ALU.add), h)

        cn_h = [None] * TB_
        cn_work = {"pool": [(t, j) for t in range(2) for j in range(32)], "dve": [(t, j) for t in range(2, 8) for j in range(32)]}

        def pump(eng, n):
            for _ in range(min(n, len(cn_work[eng]))):
                t, j = cn_work[eng].pop(0)
                cn_h[t] = count(eng, t, j, cn_h[t])

        pump("pool", 200)
        h = op("dve", lambda e: e.memset(zt, 0.0))
        s_z = pr.new_sem("s_z")
        for j in range(4):
            h_zero = dma("act", s_z, lambda e, j=j: e.dma_start(Xg[1024 * j:1024 * j + 1024, :].rearrange("(p r) c -> p (r c)", p=P), zt), h)
        xT1 = [arena.up(2 * S).rearrange("p (c s) -> p c s", c=2) for _ in range(B)]
        hb = [arena.up(8 * 512).rearrange("p (f s) -> p f s", f=8) for _ in range(2)]
        hb_rd = [[], []]
        xT_h = [to_T(X[:, TB_ * b:TB_ * b + TB_, :], xT1[b], [], "dve") for b in range(B)]

        def mlp_hidden(src, s0, w, bias, func, dst, waits):
            last = None
            for f in range(8):
                i, fr = bank()
                for k in range(2):
                    h = mm(PS[:, i, :], w[:, k, P * f:P * f + P], src[:, k, s0:s0 + 512], k == 0, k == 1, [fr, waits])
                last = op("act", lambda e, i=i, f=f: e.activation(dst[:, f, :], PS[:, i, :], func, bias=cvec[:, bias + f:bias + f + 1]), h)
                bank_free[i] = [last]
            return last

        def mlp_out(src, w, bias, dst, waits, dwaits):
            hs_ = []
            for t in range(0, 4, 2):
                i, fr = bank()
                for j in range(2):
                    for f in range(8):
                        h = mm(PS[:, i, D * j:D * j + D], src[:, f, P * (t + j):P * (t + j) + P], w[:, f, :], f == 0, f == 7, [fr, waits])
                h2 = op("dve", lambda e, i=i, t=t: e.tensor_tensor(dst[:, t:t + 2, :], PS[:, i, :].rearrange("p (a c) -> p a c", a=2), bias.unsqueeze(1).broadcast_to([P, 2, D]), ALU.add), h, dwaits)
                bank_free[i] = [h2]
                hs_.append(h2)
            return h, hs_

        pend = None
        hC = []
        for q in range(5):
            pump("dve", 26)
            if q < 4:
                b, n = q // 2, q % 2
                hh = mlp_hidden(xT1[b], 512 * n, W1c, CB1, ACT.Gelu, hb[q % 2], [h_wc, xT_h[b], hb_rd[q % 2]])
            if pend is not None:
                pq, ph = pend
                hp, hs_ = mlp_out(hb[pq % 2], Wc[pq // 2], bc[pq // 2], C1[:, 4 * pq:4 * pq + 4, :], [ph], [h_wc])
                hb_rd[pq % 2] = [hp]
                hC += hs_
            pend = (q, hh) if q < 4 else None

        xr0, xr1 = (z.rearrange("p c s -> p (c s)") for z in xT1)
        hT_ = [to_T(C1[:, TB_ * b:TB_ * b + TB_, :], xT1[b], [hC], "dve") for b in range(B)]
        rt = arena.up(1600)
        at = [0]

        def ra(n):
            at[0] += n
            return rt[:, at[0] - n:at[0]]

        def v8(z):
            return z.rearrange("p (t e) -> p t e", e=8)

        PR, M8, OH, PQ = ra(128), ra(128), ra(256), ra(256)
        IX = ra(128).bitcast(U32)
        IXF = ra(32).rearrange("p (k t) -> p k t", k=2)
        BS = ra(256)
        s1, s2, wk, posk, keep, sl, tk = (ra(32).rearrange("p (k t) -> p k t", k=2) for _ in range(7))
        cnt = ra(8)
        WK = ra(32).rearrange("p (k t) -> p k t", k=2)
        SI = ra(32).bitcast(I32).rearrange("p (k t) -> p k t", k=2)
        GI = ra(32).bitcast(I32).rearrange("p (k t) -> p k t", k=2)
        i, fr = bank()
        for t in range(NT):
            for k in range(2):
                h = mm(PS[:, i, 8 * t:8 * t + 8], xT1[t // 8][:, k, P * (t % 8):P * (t % 8) + P], Wg[:, k, :], k == 0, k == 1, [fr, hT_, h_wc], inc=(t == NT - 1 and k == 1))
        LG = v8(PS[:, i, 0:128])

        def dv(fn, *w):
            return op("dve", fn, *w)

        mx = s1.rearrange("p k t -> p (k t)")[:, 0:16]
        sm = s2.rearrange("p k t -> p (k t)")[:, 0:16]
        h = dv(lambda e: e.tensor_reduce(mx, LG, AX.X, ALU.max), h)
        h = dv(lambda e: e.tensor_tensor(v8(PR), LG, mx.unsqueeze(2).broadcast_to([P, 16, 8]), ALU.subtract), h)
        bank_free[i] = [h]
        h = op("act", lambda e: e.activation(PR, PR, ACT.Exp), h)
        h = dv(lambda e: e.tensor_reduce(sm, v8(PR), AX.X, ALU.add), h)
        h = dv(lambda e: e.reciprocal(mx, sm), h)
        h = dv(lambda e: e.tensor_tensor(v8(PR), v8(PR), mx.unsqueeze(2).broadcast_to([P, 16, 8]), ALU.mult), h)
        for t in range(NT):
            h2 = dv(lambda e, t=t: e.max(v8(M8)[:, t, :], v8(PR)[:, t, :]), h)
        for t in range(NT):
            h3 = dv(lambda e, t=t: e.max_index(IX[:, 8 * t:8 * t + 8], v8(M8)[:, t, :], v8(PR)[:, t, :]), h2)
        M8k = v8(M8)[:, :, 0:2].rearrange("p t k -> p k t")
        h = dv(lambda e: e.tensor_copy(IXF, v8(IX)[:, :, 0:2].rearrange("p t k -> p k t")), h3)
        iota8 = kslot[:, 0:8]
        OHv = OH.rearrange("p (k t e) -> p k t e", k=2, t=16)
        for k in range(2):
            hoh = dv(lambda e, k=k: e.tensor_tensor(OHv[:, k], iota8.unsqueeze(1).broadcast_to([P, 16, 8]), IXF[:, k, :].unsqueeze(2).broadcast_to([P, 16, 8]), ALU.is_equal), h, h_wc)
        h = dv(lambda e: e.tensor_tensor(s1[:, 0, :], M8k[:, 0, :], M8k[:, 1, :], ALU.add), h2)
        h = dv(lambda e: e.tensor_scalar(s1[:, 0, :], s1[:, 0, :], 1e-9, None, ALU.add), h)
        h = dv(lambda e: e.reciprocal(s2[:, 0, :], s1[:, 0, :]), h)
        hwk = dv(lambda e: e.tensor_tensor(wk, M8k, s2[:, 0:1, :].broadcast_to([P, 2, 16]), ALU.mult), h)
        i, fr = bank()
        h = mm(PS[:, i, 0:256], triu, OH, True, True, [fr, hoh])
        h = mm(PS[:, i, 256:512], onesm, OH, True, True)
        BSv = BS.rearrange("p (k t e) -> p k t e", k=2, t=16)
        TOT = PS[:, i, 256:512].rearrange("p (k t e) -> p k t e", k=2, t=16)
        PQv = PQ.rearrange("p (k t e) -> p k t e", k=2, t=16)
        h0_ = dv(lambda e: e.memset(BSv[:, :, 0, :], -1.0), h)
        for t in range(1, NT):
            h0_ = dv(lambda e, t=t: e.tensor_tensor(BSv[:, :, t, :], BSv[:, :, t - 1, :], TOT[:, :, t - 1, :], ALU.add), h0_)
        h1 = dv(lambda e: e.tensor_tensor(cnt, BSv[:, 0, 15, :], TOT[:, 0, 15, :], ALU.add), h0_)
        h1 = dv(lambda e: e.tensor_scalar(cnt, cnt, 1.0, float(CAP), ALU.add, ALU.min), h1)
        h2 = dv(lambda e, i=i: e.tensor_tensor(PQ, PS[:, i, 0:256], BS, ALU.add), h0_)
        bank_free[i] = [h2]
        h2 = dv(lambda e: e.tensor_tensor(PQv[:, 1], PQv[:, 1], cnt.unsqueeze(1).broadcast_to([P, 16, 8]), ALU.add), h2, h1)
        h2 = dv(lambda e: e.tensor_tensor(PQ, PQ, OH, ALU.mult), h2)
        h2 = dv(lambda e: e.tensor_reduce(posk, PQv, AX.X, ALU.add), h2)
        h3 = dv(lambda e: e.tensor_scalar(keep, posk, float(CAP), None, ALU.is_lt), h2)
        h4 = dv(lambda e: e.scalar_tensor_tensor(out=sl, in0=IXF, scalar=float(CAP), in1=posk, op0=ALU.mult, op1=ALU.add), h2)
        hWK = dv(lambda e: e.tensor_tensor(WK, wk, keep, ALU.mult), hwk, h3)
        h5 = dv(lambda e: e.tensor_tensor(sl, sl, keep, ALU.mult), h3, h4)
        hGI = dv(lambda e: e.tensor_copy(GI, sl), h5)
        trash = kslot[:, 8:24]
        h6 = dv(lambda e: e.tensor_scalar(tk, keep, -1.0, 1.0, ALU.mult, ALU.add), h3)
        for k in range(2):
            h7 = dv(lambda e, k=k: e.tensor_scalar(s1[:, k, :], trash, float(N * k), None, ALU.add), h)
        h7 = dv(lambda e: e.tensor_tensor(tk, tk, s1, ALU.mult), h6, h7)
        h7 = dv(lambda e: e.tensor_tensor(sl, sl, tk, ALU.add), h7, hGI)
        hSI = dv(lambda e: e.tensor_copy(SI, sl), h7)
        s_sc = pr.new_sem("s_sc")
        for k in range(2):
            for t in range(NT):
                h_sc = dma("pool", s_sc, lambda e, k=k, t=t: e.indirect_dma_start(
                    Xg[:, :], bass.IndirectOffsetOnAxis(ap=SI[:, k, t:t + 1].bitcast(U32), axis=0), C1[:, t, :], None), hSI, hC, h_zero)

        xg = [arena.up(4 * D).rearrange("p (t c) -> p t c", t=4) for _ in range(2)]
        xgT = [xr0[:, 1024 * j:1024 * j + 1024].rearrange("p (c s) -> p c s", c=2) for j in range(2)]
        ye = [xr1[:, 1024 * j:1024 * j + 1024].rearrange("p (t c) -> p t c", t=4) for j in range(2)]
        xg_rd, xgT_rd, ye_rd = [[]] * 3, [[]] * 2, [[]] * 2
        s_xg = [pr.new_sem("s_xg") for _ in range(2)]
        s_ye = [pr.new_sem("s_ye") for _ in range(2)]
        hb_rd = [[(pr.sem["pe"], pr.n[pr.sem["pe"]])]] * 2
        h_yst = []
        h_xg = {}

        def get_x(e_):
            h_xg[e_] = load(s_xg[e_ % 2], xg[e_ % 2], Xg[CAP * e_:CAP * e_ + CAP, :].rearrange("(t p) c -> p t c", p=P), h_sc, xg_rd[e_ % 2])

        for e_ in range(2):
            get_x(e_)
        pend = None
        for e_ in range(E + 1):
            pump("dve", 10)
            if e_ < E:
                u = e_ % 2
                T_ = []
                for c in range(2):
                    i, fr = bank()
                    for j in range(4):
                        h = op("pe", lambda e, i=i, j=j, c=c, u=u: e.transpose(PS[:, i, P * j:P * j + P], xg[u][:, j, P * c:P * c + P], ident), fr, h_xg[e_], inc=(j == 3))
                    h2 = op("dve", lambda e, i=i, c=c, e_=e_: e.tensor_copy(xgT[e_ % 2][:, c, :], PS[:, i, :]), h, xgT_rd[e_ % 2])
                    bank_free[i] = [h2]
                    T_.append(h2)
                xg_rd[u] = [h]
                if e_ + 2 < E:
                    get_x(e_ + 2)
                w1e, w2e = exw[e_ % NEX]
                hh = mlp_hidden(xgT[e_ % 2], 0, w1e, CB1 + 8 + 8 * e_, ACT.Gelu_apprx_tanh, hb[e_ % 2], [h_ex[e_], T_, hb_rd[e_ % 2]])
                xgT_rd[e_ % 2] = [(pr.sem["pe"], pr.n[pr.sem["pe"]])]
            if pend is not None:
                pe_, ph = pend
                hp, hs_ = mlp_out(hb[pe_ % 2], exw[pe_ % NEX][1], b2e[:, D * pe_:D * pe_ + D], ye[pe_ % 2], [ph], [h_wc, ye_rd[pe_ % 2]])
                hb_rd[pe_ % 2] = [hp]
                h = load(s_ye[pe_ % 2], Ye[CAP * pe_:CAP * pe_ + CAP, :].rearrange("(t p) c -> p t c", p=P), ye[pe_ % 2], hs_)
                ye_rd[pe_ % 2] = [h]
                h_yst.append(h)
                if pe_ + NEX < E:
                    get_w(pe_ + NEX, [hp])
            pend = (e_, hh) if e_ < E else None
        gt = [zt[:, D * j:D * j + D] for j in range(8)]
        s_g = [pr.new_sem("s_g") for _ in range(8)]
        gt_rd = [[] for _ in range(8)]
        hx_ = [None] * NT
        for j in range(2 * NT):
            t, k, u = j // 2, j % 2, j % 8
            h = dma("pool", s_g[u], lambda e, k=k, t=t, u=u: e.indirect_dma_start(
                gt[u], None, Ye[:, :], bass.IndirectOffsetOnAxis(ap=GI[:, k, t:t + 1].bitcast(U32), axis=0)), h_yst, gt_rd[u], hGI)
            h = dv(lambda e, k=k, t=t, u=u: e.scalar_tensor_tensor(out=X[:, t, :], in0=gt[u], scalar=WK[:, k, t:t + 1], in1=X[:, t, :], op0=ALU.mult, op1=ALU.add), h, hx_[t], hWK)
            hx_[t] = h
            gt_rd[u] = [h]
        pr.barrier("e")
        if dbg == "x1":
            return finish()

        def phase_e():
            arena.lo = e_mark
            arena.hi = hi0
            FP = [nc.dram_tensor(f"parts{k}", (3, D, S), BF16, kind="Internal").ap() for k in range(4)]
            Wq4, Wk4, Wv4, Wo4 = (arena.up(2 * D).rearrange("p (c n) -> p c n", c=2) for _ in range(4))
            bvb = arena.up(D)
            xT4 = arena.up(2 * S).rearrange("p (c s) -> p c s", c=2)
            K6 = [arena.up(8 * S).bitcast(BF16).rearrange("p (h s) -> p h s", h=16) for _ in range(2)]
            Q6 = [arena.up(8 * P).bitcast(BF16).rearrange("p (h s) -> p h s", h=16) for _ in range(2)]
            V4 = [arena.up(TB_ * 272).rearrange("p (t h j) -> p t h j", t=TB_, h=16) for _ in range(2)]
            X4T = [arena.down(2 * S).rearrange("p (c s) -> p c s", c=2) for _ in range(2)]
            Oc = arena.up(2 * S).rearrange("p (t c) -> p t c", t=TB_)
            Ab = [arena.up(S) for _ in range(2)]
            Sb = [arena.up(S) for _ in range(3)]
            Pt = [arena.up(S) for _ in range(3)]
            mr = arena.up(8)
            rc = arena.up(16)
            ub = arena.up(8)
            s_e = pr.new_sem("s_e")
            ebar = pr.bar
            for w_, n_ in ((Wq4, "Wq"), (Wk4, "Wk"), (Wv4, "Wv"), (Wo4, "Wo")):
                load(s_e, w_, kmaj("L1_cond_" + n_), ebar)
            load(s_e, ub[:, 0:B], a["u"].rearrange("o b -> (o b)").partition_broadcast(P))
            h_we = load(s_e, bvb, a["L1_cond_bv"].partition_broadcast(P))
            h = op("act", lambda e: e.activation(ub[:, 2:4], ub[:, 0:2], ACT.Exp, scale=-5.0), h_we)
            h = op("pool", lambda e: e.tensor_scalar(ub[:, 2:4], ub[:, 2:4], 10.0, None, ALU.mult), h)
            h1 = op("pool", lambda e: e.tensor_scalar(ub[:, 4:6], ub[:, 2:4], 1.0, None, ALU.is_ge), h)
            h = op("pool", lambda e: e.tensor_scalar(ub[:, 2:4], ub[:, 2:4], 1.0, None, ALU.min), h1)
            h = op("pool", lambda e: e.tensor_scalar(ub[:, 6:8], ub[:, 4:6], -1.0, 1.0, ALU.mult, ALU.add), h)
            h_u = op("pool", lambda e: e.tensor_tensor(ub[:, 6:8], ub[:, 6:8], ub[:, 2:4], ALU.mult), h)
            SP_, LD_ = ub[:, 4:6], ub[:, 6:8]
            h_one = [op("pool", lambda e, v=v: e.memset(v[:, :, :, 16:17], 1.0)) for v in V4]
            QF = X4T[0]
            HM = X4T[1].rearrange("p c s -> p (c s)").bitcast(BF16).rearrange("p (k c s) -> p k c s", k=2, c=2)
            LO = Oc.rearrange("p t c -> p (t c)")[:, 0:S].bitcast(BF16).rearrange("p (c s) -> p c s", c=2)
            s_fp = [pr.new_sem("s_fp") for _ in range(4)]
            s_k6 = [pr.new_sem("s_k6") for _ in range(2)]
            s_q6 = [pr.new_sem("s_q6") for _ in range(2)]
            h_fp, h_k6 = {}, []
            stg = []
            xt_rd = []
            for b in range(B):
                hx4 = to_T(X[:, TB_ * b:TB_ * b + TB_, :], xT4, [xt_rd], "act")
                for kq in range(2):
                    w_, bias, sc = ((Wq4, "bq", -0.25), (Wk4, "bk", 1.0))[kq]
                    hq = []
                    for c in range(2):
                        for n in range(2):
                            sl = slice(512 * n, 512 * n + 512)
                            i, fr = bank()
                            for k in range(2):
                                h = mm(PS[:, i, :], w_[:, k, P * c:P * c + P], xT4[:, k, sl], k == 0, k == 1, [fr, hx4, h_we])
                            h = dv(lambda e, i=i, c=c, sl=sl, bias=bias, sc=sc: e.tensor_scalar(QF[:, c, sl], PS[:, i, :], cv(bias, c), sc, ALU.add, ALU.mult), h, stg)
                            bank_free[i] = [h]
                            hq.append(h)
                    h = op("act", lambda e: e.copy(HM[:, 0], QF), hq, stg)
                    h = dv(lambda e: e.tensor_tensor(QF, QF, HM[:, 0], ALU.subtract), h)
                    h = op("act", lambda e: e.copy(HM[:, 1], QF), h)
                    h = dv(lambda e: e.tensor_tensor(LO, QF, HM[:, 1], ALU.subtract), h, stg)
                    j = 2 * b + kq
                    for part, src in ((0, HM[:, 0]), (1, HM[:, 1]), (2, LO)):
                        hd = dma("sp", s_fp[j], lambda e, j=j, part=part, src=src: e.dma_start(FP[j][part].rearrange("(c p) s -> p c s", p=P), src), h)
                    h_fp[j] = hd
                    stg = [hd]
                    if kq:
                        for g, part in enumerate((0, 1, 0, 2, 0, 1)):
                            hk6 = dma("sp", s_k6[b], lambda e, j=j, g=g, part=part, b=b: e.dma_start(K6[b][16 * g:16 * g + 16], FP[j][part].rearrange("(h r) s -> r h s", r=16)), hd)
                        h_k6.append(hk6)
                for t in range(0, TB_, 2):
                    i, fr = bank()
                    for j in range(2):
                        for k in range(2):
                            h = mm(PS[:, i, D * j:D * j + D], xT4[:, k, P * (t + j):P * (t + j) + P], Wv4[:, k, :], k == 0, k == 1, [fr, hx4, h_we])
                    xt_rd = [h]
                    hV = dv(lambda e, i=i, t=t, b=b: e.tensor_tensor(V4[b][:, t:t + 2, :, 0:16], PS[:, i, :].rearrange("p (a h j) -> p a h j", a=2, h=16), bvb.rearrange("p (h j) -> p h j", h=16).unsqueeze(1).broadcast_to([P, 2, 16, 16]), ALU.add), h)
                    bank_free[i] = [hV]
            pr.barrier("e2")
            SBK, PBK, OBK = [(0, 1), (2, 3)], [4, 5, 6], 7
            s_fr, p_fr, o_fr = [[], []], [[], [], []], []
            sb_fr, pt_fr, ab_fr = [[], [], []], [[], [], []], [[], []]
            q_fr = [[], []]
            h_q6, h_ab = {}, {}

            def get_q(m):
                b, t = m // TB_, m % TB_
                for g, part in enumerate((0, 0, 1, 0, 2, 1)):
                    h_q6[m] = dma("sp", s_q6[m % 2], lambda e, g=g, part=part, b=b, t=t, m=m: e.dma_start(
                        Q6[m % 2][16 * g:16 * g + 16], FP[2 * b][part].rearrange("(h r) s -> r h s", r=16)[:, :, P * t:P * t + P]), q_fr[m % 2], h_fp[2 * b])

            def bias(m):
                b, t = m // TB_, m % TB_
                A, T = Ab[m % 2], Tb
                c_ = CN[:, t, :]
                hh = op("pool", lambda e: e.tensor_scalar(A, c_, 1.0, None, ALU.max), ab_fr[m % 2])
                hh = op("act", lambda e: e.activation(A, A, ACT.Ln), hh)
                h2 = op("pool", lambda e: e.tensor_scalar(T, c_, 1.0, None, ALU.min), h_ab.get(m - 1))
                h2 = op("pool", lambda e: e.tensor_scalar(T, T, 1.0, -1e30, ALU.subtract, ALU.mult), h2)
                hh = op("pool", lambda e: e.tensor_tensor(A, T, A, ALU.subtract), h2, hh)
                hh = op("pool", lambda e: e.tensor_scalar(A, A, SP_[:, b:b + 1], None, ALU.mult), hh, h_u)
                h2 = op("pool", lambda e: e.tensor_scalar(T, PM[:, t, :], -1.0, 1.0, ALU.mult, ALU.add), hh)
                h2 = op("pool", lambda e: e.tensor_scalar(T, T, LD_[:, b:b + 1], None, ALU.mult), h2)
                h_ab[m] = op("pool", lambda e: e.tensor_tensor(A, A, T, ALU.add), h2)

            Tb = xT4[:, 0, :]
            Tb1 = X4T[1]
            Tb2 = K6[0].rearrange("p h s -> p (h s)").bitcast(F32)[:, 0:2 * S].rearrange("p (c s) -> p c s", c=2)
            items = [(m, h_) for m in range(B * TB_) for h_ in range(16)]
            st_ = {}
            get_q(0)
            get_q(1)
            bias(0)
            hx_prev = None

            def scores(z):
                m, h_ = items[z]
                b = m // TB_
                bk = SBK[z % 2]
                for n in range(2):
                    h = mm(PS[:, bk[n], :], Q6[m % 2][0:96, h_, :], K6[b][0:96, h_, 512 * n:512 * n + 512], True, True, [s_fr[z % 2], h_q6[m], h_k6[b]], inc=(n == 1))
                if h_ == 15:
                    q_fr[m % 2] = [h]
                    if m + 2 < B * TB_:
                        get_q(m + 2)
                ps = PS[:, bk[0]:bk[0] + 2, :].rearrange("p a s -> p (a s)")
                sbt, acc = Sb[z % 3], mr[:, z % 4:z % 4 + 1]
                h = dv(lambda e: e.tensor_tensor_reduce(sbt, ps, Ab[m % 2], 1.0, 3e38, ALU.add, ALU.min, acc), h, sb_fr[z % 3], h_ab[m], mr_rd.get(z - 4))
                s_fr[z % 2] = [h]
                if h_ == 15:
                    ab_fr[m % 2] = [h]
                h = op("act", lambda e: e.activation(sbt, sbt, ACT.Exp, bias=acc, scale=-1.0), h)
                mr_rd[z] = h
                st_[z] = h

            def turn(z):
                sbt, ptt = Sb[z % 3], Pt[z % 3]
                hs_ = []
                for g in range(2):
                    u = (2 * z + g) % 3
                    i = PBK[u]
                    for j in range(4):
                        k = 4 * g + j
                        h = op("pe", lambda e, i=i, j=j, k=k: e.transpose(PS[:, i, P * j:P * j + P], sbt[:, P * k:P * k + P], ident), p_fr[u], st_[z], inc=(j == 3))
                    eng = "dve" if (g == 0 and z % 8 != 7) else "act"
                    if eng == "dve":
                        h2 = dv(lambda e, i=i: e.tensor_copy(ptt[:, 0:512], PS[:, i, :]), h, pt_fr[z % 3])
                    else:
                        h2 = op("act", lambda e, i=i, g=g: e.copy(ptt[:, 512 * g:512 * g + 512], PS[:, i, :]), h, pt_fr[z % 3])
                    p_fr[u] = [h2]
                    hs_.append(h2)
                sb_fr[z % 3] = [h]
                st_[z] = hs_

            def values(z):
                nonlocal o_fr
                m, h_ = items[z]
                b, t = m // TB_, m % TB_
                o = PS[:, OBK, 17 * h_:17 * h_ + 17]
                for k in range(8):
                    h = mm(o, Pt[z % 3][:, P * k:P * k + P], V4[b][:, k, h_, :], k == 0, k == 7, [st_[z], o_fr])
                pt_fr[z % 3] = [h]
                if h_ == 15:
                    ov = PS[:, OBK, 0:272].rearrange("p (h j) -> p h j", h=16)
                    h = dv(lambda e: e.reciprocal(rc, ov[:, :, 16]), h)
                    h = dv(lambda e: e.tensor_tensor(Oc[:, t, :].rearrange("p (h j) -> p h j", h=16), ov[:, :, 0:16], rc.unsqueeze(2).broadcast_to([P, 16, 16]), ALU.mult), h, oc_fr)
                    o_fr = [h]
                    return h

            mr_rd = {}
            oc_fr = []
            hx4T = []
            NZ = len(items)
            for z in range(NZ + 2):
                if z < NZ:
                    if items[z][1] == 4 and items[z][0] + 1 < B * TB_:
                        bias(items[z][0] + 1)
                    scores(z)
                if 1 <= z <= NZ:
                    turn(z - 1)
                if z >= 2:
                    h = values(z - 2)
                    m, h_ = items[z - 2]
                    if h_ == 15 and m % TB_ == TB_ - 1:
                        b = m // TB_
                        Ot = (Tb2 if b else Tb1)
                        last = []
                        for g in range(2):
                            for c in range(2):
                                u = 2
                                i = 6
                                for j in range(4):
                                    t = 4 * g + j
                                    h2 = op("pe", lambda e, i=i, j=j, t=t, c=c: e.transpose(PS[:, i, P * j:P * j + P], Oc[:, t, P * c:P * c + P], ident), p_fr[2], h, inc=(j == 3))
                                h3 = op("act", lambda e, i=i, c=c, g=g, Ot=Ot: e.copy(Ot[:, c, 512 * g:512 * g + 512], PS[:, i, :]), h2)
                                p_fr[2] = [h3]
                                last.append(h3)
                        oc_fr = [h2]
                        for c in range(2):
                            for n in range(2):
                                for k in range(2):
                                    h2 = mm(PS[:, 6, :], Wo4[:, k, P * c:P * c + P], Ot[:, k, 512 * n:512 * n + 512], k == 0, k == 1, [p_fr[2], last])
                                h3 = op("act", lambda e, c=c, n=n, b=b: e.activation(X4T[b][:, c, 512 * n:512 * n + 512], PS[:, 6, :], ACT.Identity, bias=cv("bo", c)), h2)
                                p_fr[2] = [h3]
                                hx4T.append(h3)
            return X4T

        X4T = phase_e()
        pr.barrier("f")
        if dbg == "c2":
            hh = []
            for b in range(B):
                for t in range(TB_):
                    for c in range(2):
                        i, fr = bank()
                        h = op("pe", lambda e, i=i, t=t, c=c, b=b: e.transpose(PS[:, i, 0:P], X4T[b][:, c, P * t:P * t + P], ident), fr)
                        h = dv(lambda e, i=i, t=t, c=c, b=b: e.tensor_copy(X[:, TB_ * b + t, P * c:P * c + P], PS[:, i, 0:P]), h)
                        bank_free[i] = [h]
            return finish()

        def phase_f():
            arena.lo = base0
            fbar = pr.bar
            Wq5, Wk5, Wv5 = (arena.up(2 * FH).rearrange("p (c n) -> p c n", c=2) for _ in range(3))
            Wo5 = arena.up(8 * D).rearrange("p (f n) -> p f n", f=8)
            qT, kT5 = (arena.up(8 * S).rearrange("p (f s) -> p f s", f=8) for _ in range(2))
            v5 = arena.up(8 * FH).rearrange("p (t n) -> p t n", t=8)
            sk = arena.up(8 * 64).rearrange("p (f g) -> p f g", f=8)
            sv = arena.up(FH)
            gT = arena.up(2 * 64).rearrange("p (c g) -> p c g", c=2)
            band = arena.up(768)
            Sb = [arena.up(449) for _ in range(3)]
            Se = [arena.up(321) for _ in range(2)]
            Pb = [arena.up(512) for _ in range(3)]
            Pt = [arena.up(512) for _ in range(2)]
            sm = arena.up(32)
            mr = arena.up(8)
            yk = arena.up(FH)
            yT = arena.up(FH).rearrange("p (f s) -> p f s", f=8)
            s_f = pr.new_sem("s_f")
            for w_, n_ in ((Wq5, "Wq"), (Wk5, "Wk"), (Wv5, "Wv")):
                load(s_f, w_, kmaj("L1_attn_" + n_), fbar)
            load(s_f, band, a["k_band"])
            h_w5 = load(s_f, Wo5, a["L1_attn_Wo"].rearrange("(f p) n -> p f n", f=8))
            hz = [op("pool", lambda e, z=z: e.memset(z, 0.0)) for z in Sb + Se + Pb + [sv]]
            hz = [hz[-1]]
            proj_rd = []
            bfree = {i: [] for i in range(8)}
            y_fr, yk_rd, yT_rd = [[], []], [], []
            sb_fr, se_fr, pb_fr, pt_fr = [[], [], []], [[], []], [[], [], []], [[], []]
            sm_rd = [[], []]
            ring = [0]

            def pbank():
                i = 3 + ring[0] % 3
                ring[0] += 1
                return i

            for b in range(B):
                xb_ = X4T[b]
                h_g = dv(lambda e, xb_=xb_: e.tensor_reduce(gT, xb_.rearrange("p c (g l) -> p c g l", l=16), AX.X, ALU.add), proj_rd)
                hp = []
                cyc = [0]

                def nb():
                    i = cyc[0] % 8
                    cyc[0] += 1
                    return i

                for w_, dst, sc in ((Wq5, qT, -0.125), (Wk5, kT5, 1.0)):
                    for f in range(8):
                        for n in range(2):
                            i = nb()
                            for k in range(2):
                                h = mm(PS[:, i, :], w_[:, k, P * f:P * f + P], xb_[:, k, 512 * n:512 * n + 512], k == 0, k == 1, [bfree[i], h_w5])
                            o = dst[:, f, 512 * n:512 * n + 512]
                            if cyc[0] % 2:
                                h = op("act", lambda e, i=i, o=o, sc=sc: e.mul(o, PS[:, i, :], sc), h, proj_rd)
                            else:
                                h = dv(lambda e, i=i, o=o, sc=sc: e.tensor_scalar(o, PS[:, i, :], sc, None, ALU.mult), h, proj_rd)
                            bfree[i] = [h]
                            hp.append(h)
                for t in range(8):
                    for n in range(2):
                        i = nb()
                        for k in range(2):
                            h = mm(PS[:, i, :], xb_[:, k, P * t:P * t + P], Wv5[:, k, 512 * n:512 * n + 512], k == 0, k == 1, [bfree[i], h_w5])
                        o = v5[:, t, 512 * n:512 * n + 512]
                        if cyc[0] % 2:
                            h = op("act", lambda e, i=i, o=o: e.copy(o, PS[:, i, :]), h, proj_rd)
                        else:
                            h = dv(lambda e, i=i, o=o: e.tensor_copy(o, PS[:, i, :]), h, proj_rd)
                        bfree[i] = [h]
                        hp.append(h)
                i = nb()
                for f in range(8):
                    for k in range(2):
                        h = mm(PS[:, i, 64 * f:64 * f + 64], Wk5[:, k, P * f:P * f + P], gT[:, k, :], k == 0, k == 1, [bfree[i], h_g])
                h = dv(lambda e, i=i: e.tensor_copy(sk, PS[:, i, :].rearrange("p (f g) -> p f g", f=8)), h, proj_rd)
                bfree[i] = [h]
                hp.append(h)
                for n in range(2):
                    i = nb()
                    for k in range(2):
                        h = mm(PS[0:64, i, :], gT[:, k, :], Wv5[:, k, 512 * n:512 * n + 512], k == 0, k == 1, [bfree[i], h_g])
                    h = dv(lambda e, i=i, n=n: e.tensor_copy(sv[0:64, 512 * n:512 * n + 512], PS[0:64, i, :]), h, proj_rd, hz)
                    bfree[i] = [h]
                    hp.append(h)
                all_b = [x for v_ in bfree.values() for x in v_]
                state = {}
                items = [(t, h_) for t in range(8) for h_ in range(16)]

                def geom(t):
                    k0 = max(t - 1, 0)
                    k1 = min(t + 2, 8)
                    return k0, k1, P * (k1 - k0)

                def scores(z):
                    t, h_ = items[z]
                    k0, k1, nk = geom(t)
                    i = z % 3
                    rows = slice(64 * (h_ % 2), 64 * (h_ % 2) + 64)
                    f = h_ // 2
                    mm(PS[:, i, 0:nk], qT[rows, f, P * t:P * t + P], kT5[rows, f, P * k0:P * k1], True, True, [bfree[i], hp], inc=False)
                    h = mm(PS[:, i, nk:nk + 64], qT[rows, f, P * t:P * t + P], sk[rows, f, :], True, True)
                    w = nk + 64
                    if nk == 384:
                        sbt, frs, u, bnd = Sb[z % 3], sb_fr, z % 3, band[:, 0:448]
                    else:
                        sbt, frs, u = Se[z % 2], se_fr, z % 2
                        bnd = band[:, 128:448] if t == 0 else band[:, 448:768]
                    acc = mr[:, z % 8:z % 8 + 1]
                    pbt = Pb[z % 3]
                    smc = sm[:, 16 * (t % 2) + h_:16 * (t % 2) + h_ + 1]
                    h = dv(lambda e: e.tensor_tensor_reduce(sbt[:, 0:w], PS[:, i, 0:w], bnd, 1.0, 0.0, ALU.add, ALU.min, acc), h, frs[u], hz, state.get(("e", z - 8)))
                    bfree[i] = [h]
                    h = op("act", lambda e: e.activation(pbt[:, 0:w + 1], sbt[:, 0:w + 1], ACT.Exp, bias=acc, scale=-1.0, accum_out=smc), h, pb_fr[z % 3], sm_rd[t % 2] if h_ == 0 else None)
                    frs[u] = [h]
                    state["e", z] = h

                def turn(z):
                    t, h_ = items[z]
                    k0, k1, nk = geom(t)
                    nj = k1 - k0 + 1
                    i = pbank()
                    pbt, ptt = Pb[z % 3], Pt[z % 2]
                    for j in range(nj):
                        h = op("pe", lambda e, j=j: e.transpose(PS[:, i, P * j:P * j + P], pbt[:, P * j:P * j + P], ident), bfree[i], state["e", z], inc=(j == nj - 1))
                    pb_fr[z % 3] = [h]
                    if z % 2:
                        h = op("act", lambda e: e.copy(ptt[:, 0:P * nj], PS[:, i, 0:P * nj]), h, pt_fr[z % 2])
                    else:
                        h = dv(lambda e: e.tensor_copy(ptt[:, 0:P * nj], PS[:, i, 0:P * nj]), h, pt_fr[z % 2])
                    bfree[i] = [h]
                    state["t", z] = h

                def values(z):
                    nonlocal yk_rd, yT_rd
                    t, h_ = items[z]
                    k0, k1, nk = geom(t)
                    nj = k1 - k0 + 1
                    i = 6 + h_ // 8
                    o = PS[:, i, 64 * (h_ % 8):64 * (h_ % 8) + 64]
                    for j in range(nj):
                        rhs = v5[:, k0 + j, 64 * h_:64 * h_ + 64] if j < nj - 1 else sv[:, 64 * h_:64 * h_ + 64]
                        h = mm(o, Pt[z % 2][:, P * j:P * j + P], rhs, j == 0, j == nj - 1, [state["t", z], bfree[i]])
                    pt_fr[z % 2] = [h]
                    if h_ % 8 < 7:
                        return
                    g = h_ // 8
                    rr = sm[:, 16 * (t % 2) + 8 * g:16 * (t % 2) + 8 * g + 8]
                    h2 = dv(lambda e: e.reciprocal(rr, rr), state["e", z])
                    h = dv(lambda e: e.tensor_tensor(yk[:, 512 * g:512 * g + 512].rearrange("p (h j) -> p h j", h=8), PS[:, i, :].rearrange("p (h j) -> p h j", h=8), rr.unsqueeze(2).broadcast_to([P, 8, 64]), ALU.mult), h, h2, yk_rd if g == 0 else None)
                    bfree[i] = [h]
                    state["y", g] = h
                    if g == 0:
                        return
                    sm_rd[t % 2] = [h]
                    last = []
                    for gg in range(2):
                        ii = pbank()
                        for j in range(4):
                            h = op("pe", lambda e, ii=ii, j=j, gg=gg: e.transpose(PS[:, ii, P * j:P * j + P], yk[:, 512 * gg + P * j:512 * gg + P * j + P], ident), bfree[ii], state["y", 0], state["y", 1], inc=(j == 3))
                        h3 = op("act", lambda e, ii=ii, gg=gg: e.copy(yT[:, 4 * gg:4 * gg + 4, :], PS[:, ii, :].rearrange("p (f s) -> p f s", f=4)), h, yT_rd)
                        bfree[ii] = [h3]
                        last.append(h3)
                    yk_rd = [h]
                    ii = pbank()
                    for k in range(8):
                        h = mm(PS[:, ii, 0:D], yT[:, k, :], Wo5[:, k, :], k == 0, k == 7, [bfree[ii], last])
                    yT_rd = [h]
                    xs = X[:, TB_ * b + t, :]
                    h = dv(lambda e: e.tensor_tensor(xs, xs, PS[:, ii, 0:D], ALU.add), h)
                    bfree[ii] = [h]

                NZ = len(items)
                for z in range(NZ + 2):
                    if z < NZ:
                        scores(z)
                    if 1 <= z <= NZ:
                        turn(z - 1)
                    if z >= 2:
                        values(z - 2)
                proj_rd = [(pr.sem[e], pr.n[pr.sem[e]]) for e in ("pe", "act", "dve")]

        phase_f()
        pr.barrier("g")
        if dbg == "x2":
            return finish()

        def phase_g():
            arena.lo, arena.hi = base0, hi0
            gbar = pr.bar
            Wr7, Wk7, Wv7 = (arena.up(2 * D).rearrange("p (c n) -> p c n", c=2) for _ in range(3))
            s_h = pr.new_sem("s_h")
            for w_, n_ in ((Wr7, "r"), (Wk7, "k"), (Wv7, "v")):
                h_w7 = load(s_h, w_, kmaj("L1_ffn_W_" + n_), gbar)
            om = arena.up(4)
            for q, nm in enumerate(("mu_r", "mu_k")):
                i0 = CIDX[nm]
                h_om = dv(lambda e, q=q, i0=i0: e.tensor_scalar(om[:, 2 * q:2 * q + 2], cvec[:, i0:i0 + 2], -1.0, 1.0, ALU.mult, ALU.add))
            hT = [arena.up(2 * S).rearrange("p (c s) -> p c s", c=2) for _ in range(B)]
            xr, xk, ka = ([arena.up(2 * S).rearrange("p (c s) -> p c s", c=2) for _ in range(1)][0] for _ in range(3))
            R = arena.up(TB_ * D).rearrange("p (t c) -> p t c", t=TB_)
            wB = [adapter_space(64) for _ in range(B)]
            hc = []
            for b in range(B):
                hx = to_T(X[:, TB_ * b:TB_ * b + TB_, :], hT[b], [])
                hc.append(adapter("g", b, 64, 10, 4, "L1_cond2_W1", None, "L1_cond2_W2", "L1_cond2_b2", "gb1", hT[b], hT[b], [hx, gbar], wB[b]))
            prev = []
            for b in range(B):
                hh = []
                for q, (dst, nm) in enumerate(((xr, "mu_r"), (xk, "mu_k"))):
                    for c in range(2):
                        h = dv(lambda e, dst=dst, c=c, nm=nm, b=b: e.tensor_scalar(dst[:, c], hT[b][:, c], cv(nm, c), None, ALU.mult), hc[b], prev)
                        h = dv(lambda e, dst=dst, c=c, q=q, b=b: e.scalar_tensor_tensor(out=dst[:, c, 1:S], in0=hT[b][:, c, 0:S - 1], scalar=om[:, 2 * q + c:2 * q + c + 1], in1=dst[:, c, 1:S], op0=ALU.mult, op1=ALU.add), h, h_om)
                        hh.append(h)
                hk = []
                for c in range(2):
                    for n in range(2):
                        i, fr = bank()
                        for k in range(2):
                            h = mm(PS[:, i, :], Wk7[:, k, P * c:P * c + P], xk[:, k, 512 * n:512 * n + 512], k == 0, k == 1, [fr, hh, h_w7])
                        o = ka[:, c, 512 * n:512 * n + 512]
                        h = op("act", lambda e, i=i, o=o: e.activation(o, PS[:, i, :], ACT.Relu), h, prev)
                        bank_free[i] = [h]
                        hk.append(op("pool", lambda e, o=o: e.tensor_tensor(o, o, o, ALU.mult), h))
                hr = []
                for t in range(0, TB_, 2):
                    i, fr = bank()
                    for j in range(2):
                        for k in range(2):
                            h = mm(PS[:, i, D * j:D * j + D], xr[:, k, P * (t + j):P * (t + j) + P], Wr7[:, k, :], k == 0, k == 1, [fr, hh, h_w7])
                    h = op("act", lambda e, i=i, t=t: e.activation(R[:, t:t + 2, :], PS[:, i, :].rearrange("p (a c) -> p a c", a=2), ACT.Sigmoid), h, prev)
                    bank_free[i] = [h]
                    hr.append(h)
                for t in range(0, TB_, 2):
                    i, fr = bank()
                    for j in range(2):
                        for k in range(2):
                            h = mm(PS[:, i, D * j:D * j + D], ka[:, k, P * (t + j):P * (t + j) + P], Wv7[:, k, :], k == 0, k == 1, [fr, hk])
                    xs = X[:, TB_ * b + t:TB_ * b + t + 2, :]
                    h = dv(lambda e, i=i, t=t: e.tensor_tensor(R[:, t:t + 2, :], R[:, t:t + 2, :], PS[:, i, :].rearrange("p (a c) -> p a c", a=2), ALU.mult), h, hr[t // 2])
                    bank_free[i] = [h]
                    h = op("pool", lambda e, t=t, xs=xs: e.tensor_tensor(xs, xs, R[:, t:t + 2, :], ALU.add), h)
                prev = [(pr.sem[e], pr.n[pr.sem[e]]) for e in ("pe", "act", "dve", "pool")]

        phase_g()
        finish()


def layouts(i):
    f = {k: np.asarray(v) for k, v in i.items()}
    a = {}
    a["x"] = f["x"].reshape(N, D)
    a["xT"] = f["x"].reshape(N, D).T
    a["ids"] = np.concatenate([f["itok_B_0_6"], f["itok_B_0_7"], f["itok_B_0_8"]]).reshape(1, 6)
    a["u"] = f["condB_uprev"].reshape(1, B)
    a["idx"] = f["itok_Sx32_0_1023"]
    a["imask"] = f["mask_Sx32_bk1"]
    a["pmask"] = f["mask_SxS_bk0"]

    def col(v):
        return v.reshape(-1, P).T

    vecs = {"maa_x": "L0_attn_time_maa_x", "maa_w": "L0_attn_time_maa_w", "maa_k": "L0_attn_time_maa_k",
            "maa_v": "L0_attn_time_maa_v", "maa_r": "L0_attn_time_maa_r", "decay": "L0_attn_time_decay",
            "faaaa": "L0_attn_time_faaaa", "ln_w": "L0_attn_ln_w", "ln_b": "L0_attn_ln_b",
            "bq": "L1_cond_bq", "bk": "L1_cond_bk", "mu_r": "L1_ffn_mu_r", "mu_k": "L1_ffn_mu_k", "bo": "L1_cond_bo"}
    a["cvec"] = np.concatenate([col(f[vecs[n]].reshape(-1)) for n in CV]
                               + [col(f["L0_cond2_b1"]), col(f["L0_ffn_b1"].reshape(-1))], axis=1)

    def gb(g, b, bd):
        e = g.shape[0]
        pad = np.zeros((e, P, 1), np.float32)
        pad[:, :bd.shape[1], 0] = bd
        return np.concatenate([g.reshape(e, 2, P).transpose(0, 2, 1), b.reshape(e, 2, P).transpose(0, 2, 1), pad], axis=2)

    a["gb0"] = gb(f["L0_cond_ln_g"], f["L0_cond_ln_b"], f["L0_cond_down_b"])
    a["gb1"] = gb(f["L1_cond2_gamma"], f["L1_cond2_beta"], f["L1_cond2_b1"])
    for n in ("L0_cond_down_w", "L0_cond_up_w", "L0_cond_up_b", "L0_attn_time_maa_w1", "L0_attn_time_decay_w1",
              "L0_attn_time_decay_w2", "L0_attn_W_r", "L0_attn_W_k", "L0_attn_W_v", "L0_attn_W_o",
              "L0_cond2_W1", "L0_cond2_W2", "L0_cond2_b2", "L0_cond2_We", "L0_cond2_be", "L0_ffn_Wg",
              "L0_ffn_W1", "L0_ffn_W2", "L0_ffn_b2", "L1_cond_bv", "L1_cond2_W1",
              "L1_cond2_W2", "L1_cond2_b2"):
        a[n] = f[n]
    a["L0_attn_time_maa_w2"] = f["L0_attn_time_maa_w2"].reshape(P, D)
    for n in ("Wq", "Wk", "Wv", "Wo"):
        a["L1_cond_" + n] = f["L1_cond_" + n].T
        w = f["L1_attn_" + n]
        a["L1_attn_" + n] = w.reshape(1024, 256) if n == "Wo" else w.reshape(256, 1024)
    for n in ("W_r", "W_k", "W_v"):
        a["L1_ffn_" + n] = f["L1_ffn_" + n].T
    i = np.arange(P)
    a["k_ident"] = np.eye(P, dtype=np.float32)
    a["k_headb"] = (i[:, None] // 64 == i[None, :] // 64).astype(np.float32)
    a["k_triu"] = (i[:, None] <= i[None, :]).astype(np.float32)
    NEG = np.float32(-1e9)
    z = np.zeros((P, P), np.float32)
    prev = np.where(i[None, :] > i[:, None], np.float32(0), -NEG)
    nxt = np.where(i[None, :] < i[:, None], np.float32(0), -NEG)
    a["k_band"] = np.concatenate([prev, z, nxt, z[:, :64], prev, z, z[:, :64]], axis=1).astype(np.float32)
    a["k_iota"] = np.broadcast_to(np.arange(S, dtype=np.float32), (P, S))
    a["k_slot"] = np.concatenate([np.broadcast_to(np.arange(8, dtype=np.float32), (P, 8)),
                                  np.arange(N, dtype=np.float32).reshape(NT, P).T + E * CAP], axis=1)
    return {k: np.ascontiguousarray(v) for k, v in a.items()}


def kernel(**inputs):
    import concourse.bacc as _bacc
    from concourse.bass_utils import run_bass_kernel_spmd as _run

    nc = _bacc.Bacc("TRN2", target_bir_lowering=False, num_devices=1)
    arrays, aps = {}, {}
    for name, v in layouts(inputs).items():
        arrays[f"in_{name}"] = v
        aps[name] = nc.dram_tensor(f"in_{name}", v.shape, mybir.dt.from_np(v.dtype), kind="ExternalInput").ap()
    out = nc.dram_tensor("out_0", (N, D), F32, kind="ExternalOutput").ap()
    build(nc, aps, out)
    r = _run(nc, [arrays], core_ids=[0])
    return r.results[0]["out_0"].reshape(B, S, D)
```

```python
from contextlib import ExitStack

import numpy as np

import concourse.bass as bass
from concourse import mybir

F32 = mybir.dt.float32
BF16 = mybir.dt.bfloat16
I32 = mybir.dt.int32
U32 = mybir.dt.uint32
U8 = mybir.dt.uint8
ALU = mybir.AluOpType
ACT = mybir.ActivationFunctionType
AX = mybir.AxisListType

P = 128
B = 2
S = 1024
D = 256
N = B * S
NT = N // P
TB_ = S // P
E = 8
FH = 1024
CAP = 512
ENG = ("pe", "act", "dve", "pool", "sp")


class Prog:

    def __init__(self, nc, ctx):
        self.nc, self.ctx = nc, ctx
        self.q = {e: [] for e in ENG}
        self.n = {}
        self.seen = {e: {} for e in ENG}
        self.sem = {}
        self.k = 0
        self.bar = []
        self.phase("p0")

    def new_sem(self, name):
        self.k += 1
        s = self.ctx.enter_context(self.nc.semaphore(f"{name}_{self.k}"))
        self.n[s] = 0
        return s

    def phase(self, name):
        for e in ("pe", "act", "dve", "pool"):
            self.sem[e] = self.new_sem(f"{name}_{e}")

    def wait(self, e, *hs):
        for h in hs:
            if h is None:
                continue
            if isinstance(h, list):
                self.wait(e, *h)
                continue
            s, v = h
            if self.seen[e].get(s, 0) < v:
                self.seen[e][s] = v
                self.q[e].append(lambda eng, s=s, v=v: eng.wait_ge(s, v))

    def op(self, e, fn, *waits, inc=True):
        self.wait(e, *waits)
        if not inc:
            self.q[e].append(lambda eng: fn(eng))
            return None
        s = self.sem[e]
        self.n[s] += 1
        self.q[e].append(lambda eng, s=s: fn(eng).then_inc(s, 1))
        return (s, self.n[s])

    def dma(self, e, sem, fn, *waits):
        self.wait(e, *waits)
        self.n[sem] += 16
        self.q[e].append(lambda eng, s=sem: fn(eng).then_inc(s, 16))
        return (sem, self.n[sem])

    def barrier(self, name):
        last = [(self.sem[e], self.n[self.sem[e]]) for e in ("pe", "act", "dve", "pool")]
        last = [h for h in last if h[1]]
        self.bar = last
        for e in ("pe", "act", "dve", "pool"):
            self.wait(e, *last)
        self.phase(name)
        return last


class Arena:

    def __init__(self, t, size):
        self.t, self.size, self.lo, self.hi = t, size, 0, size

    def up(self, n, dt=F32):
        a, self.lo = self.lo, self.lo + n
        assert self.lo <= self.hi, (self.lo, self.hi)
        v = self.t[:, a:a + n]
        return v if dt == F32 else v.bitcast(dt)

    def down(self, n):
        self.hi -= n
        assert self.lo <= self.hi, (self.lo, self.hi)
        return self.t[:, self.hi:self.hi + n]


CV = ["maa_x", "maa_w", "maa_k", "maa_v", "maa_r", "decay", "faaaa", "ln_w", "ln_b", "bq", "bk", "mu_r", "mu_k", "bo"]
CIDX = {n: 2 * i for i, n in enumerate(CV)}
CB1 = 2 * len(CV)
NCV = CB1 + 8 + 64


def build(nc, a, out, dbg=None):
    with ExitStack() as ctx:
        pr = Prog(nc, ctx)
        op, dma = pr.op, pr.dma
        WORDS = 52600
        arena = Arena(ctx.enter_context(nc.sbuf_tensor("arena", [P, WORDS], F32)), WORDS)
        PS = ctx.enter_context(nc.psum_tensor("PS", [P, 8, 512], F32))
        bank_free = [[] for _ in range(8)]
        bank_at = [0]

        def bank():
            i = bank_at[0]
            bank_at[0] = (i + 1) % 8
            return i, bank_free[i]

        def mm(out_, lhsT, rhs, start, stop, waits=(), inc=None):
            return op("pe", lambda e: e.matmul(out_, lhsT, rhs, start=start, stop=stop), *waits,
                      inc=stop if inc is None else inc)

        ident = arena.up(P)
        headb = arena.up(P)
        triu = arena.up(P)
        onesm = arena.up(P)
        cvec = arena.up(NCV)
        X = arena.up(NT * D).rearrange("p (t c) -> p t c", t=NT)
        s_c = pr.new_sem("s_c")
        h_cst = [dma("sp", s_c, lambda e: e.dma_start(ident, a["k_ident"])),
                 dma("sp", s_c, lambda e: e.dma_start(cvec, a["cvec"])),
                 dma("sp", s_c, lambda e: e.dma_start(headb, a["k_headb"])),
                 dma("sp", s_c, lambda e: e.dma_start(triu, a["k_triu"]))][-1]

        def cv(name, c):
            i = CIDX[name] + c
            return cvec[:, i:i + 1]

        kslot = arena.up(24)
        dma("sp", s_c, lambda e: e.dma_start(kslot, a["k_slot"]))
        ids = arena.up(8).bitcast(I32)
        h_ids = dma("sp", s_c, lambda e: e.dma_start(ids[0:1, 0:6], a["ids"]))
        h_cst = h_ids
        h_ones = op("pool", lambda e: e.memset(onesm, 1.0))
        regs = {}

        def load_id(i, n):
            def f(e):
                regs[i] = e.value_load(ids[0:1, i:i + 1], min_val=0, max_val=n - 1)
            pr.wait("sp", h_ids)
            pr.q["sp"].append(f)

        def load(sem, dst, src, *waits):
            return dma("sp", sem, lambda e: e.dma_start(dst, src), *waits)

        def load_by(sem, dst, src_of, i, *waits):
            return dma("sp", sem, lambda e: e.dma_start(dst, src_of(regs[i])), *waits)

        def kmaj(name, c=2):
            return a[name].rearrange("(c p) n -> p c n", c=c)

        base0 = arena.lo
        Xg = nc.dram_tensor("xg", (2 * E * CAP, D), F32, kind="Internal").ap()
        Ye = nc.dram_tensor("ye", (E * CAP, D), F32, kind="Internal").ap()
        s_x = pr.new_sem("s_x")

        def adapter(tag, bi, K, n_ids, idx0, down, down_b, up, up_b, gb, srcT, dstT, waits, wb):
            sem = pr.new_sem("s_ad")
            wd, wu, small, bub, zT, xb, y, st = wb
            load_id(idx0 + bi, n_ids)
            load_by(sem, wd, lambda r: a[down].rearrange("e (c p) k -> e p c k", c=2)[bass.ds(r, 1)].rearrange("e p c k -> (e p) c k"), idx0 + bi, *waits)
            load_by(sem, wu[0:K], lambda r: a[up][bass.ds(r, 1)].rearrange("e k h -> (e k) h"), idx0 + bi)
            load_by(sem, small, lambda r: a[gb][bass.ds(r, 1)].rearrange("e p c -> (e p) c"), idx0 + bi)
            h_w = load_by(sem, bub, lambda r: a[up_b][bass.ds(r, 1)].rearrange("e h -> (e h)").partition_broadcast(P), idx0 + bi)
            xs = X[:, TB_ * bi:TB_ * bi + TB_, :]
            h_xb = op("pool", lambda e: e.tensor_tensor(xb, xs, bub.unsqueeze(1).broadcast_to([P, TB_, D]), ALU.add), h_w, *waits)
            hz = []
            for n in range(2):
                i, fr = bank()
                for c in range(2):
                    h = mm(PS[0:K, i, :], wd[:, c, :], srcT[:, c, 512 * n:512 * n + 512], c == 0, c == 1, [h_w, fr, waits])
                h = op("act", lambda e, i=i, n=n: e.activation(zT[0:K, 512 * n:512 * n + 512], PS[0:K, i, :], ACT.Relu, bias=small[0:K, 4:5]), h)
                bank_free[i] = [h]
                hz.append(h)
            hy = []
            for t in range(TB_):
                i, fr = bank()
                h = mm(PS[:, i, 0:D], zT[0:K, P * t:P * t + P], wu[0:K, :], True, True, [hz[t // 4], fr])
                h = op("dve", lambda e, i=i, t=t: e.tensor_tensor(y[:, t, :], PS[:, i, 0:D], xb[:, t, :], ALU.add), h, h_xb)
                bank_free[i] = [h]
                h = op("dve", lambda e, t=t: e.bn_stats(st[:, 6 * t:6 * t + 6], y[:, t, :]), h)
                hy.append(h)
            mv = st[:, 48:64].rearrange("p (t k) -> p t k", k=2)
            for t in range(TB_):
                h = op("dve", lambda e, t=t: e.bn_aggr(mv[:, t, :], st[:, 6 * t:6 * t + 6]), hy[t])
            h = op("dve", lambda e: e.tensor_scalar(st[:, 64:72], mv[:, :, 1], 1e-5, None, ALU.add), h)
            h = op("act", lambda e: e.activation(st[:, 72:80], st[:, 64:72], ACT.Sqrt), h)
            h = op("dve", lambda e: e.reciprocal(st[:, 80:88], st[:, 72:80]), h)
            hn = []
            for t in range(TB_):
                h2 = op("dve", lambda e, t=t: e.tensor_scalar(y[:, t, :], y[:, t, :], mv[:, t, 0:1], st[:, 80 + t:81 + t], ALU.subtract, ALU.mult), h)
                hn.append(h2)
            last = []
            for c in range(2):
                for g in range(2):
                    i, fr = bank()
                    for j in range(4):
                        t = 4 * g + j
                        h = op("pe", lambda e, i=i, j=j, t=t, c=c: e.transpose(PS[:, i, P * j:P * j + P], y[:, t, P * c:P * c + P], ident), hn[t], fr, h_cst, inc=(j == 3))
                    h = op("act", lambda e, i=i, c=c, g=g: e.activation(dstT[:, c, 512 * g:512 * g + 512], PS[:, i, :], ACT.Identity, bias=small[:, 2 + c:3 + c], scale=small[:, c:c + 1]), h)
                    bank_free[i] = [h]
                    last.append(h)
            return last

        def adapter_space(K):
            return (arena.up(2 * K).rearrange("p (c k) -> p c k", c=2), arena.up(D), arena.up(8)[:, 0:5], arena.up(D),
                    arena.up(S), arena.up(TB_ * D).rearrange("p (t c) -> p t c", t=TB_),
                    arena.up(TB_ * D).rearrange("p (t c) -> p t c", t=TB_), arena.up(96))

        def to_T(src, dst, waits, eng="act"):
            last = []
            for g in range(2):
                for c in range(2):
                    i, fr = bank()
                    for j in range(4):
                        t = 4 * g + j
                        h = op("pe", lambda e, i=i, j=j, t=t, c=c: e.transpose(PS[:, i, P * j:P * j + P], src[:, t, P * c:P * c + P], ident), fr, waits, inc=(j == 3))
                    if eng == "act":
                        h = op("act", lambda e, i=i, c=c, g=g: e.copy(dst[:, c, 512 * g:512 * g + 512], PS[:, i, :]), h)
                    else:
                        h = op("dve", lambda e, i=i, c=c, g=g: e.tensor_copy(dst[:, c, 512 * g:512 * g + 512], PS[:, i, :]), h)
                    bank_free[i] = [h]
                    last.append(h)
            return last

        def finish():
            last = [(pr.sem[e], pr.n[pr.sem[e]]) for e in ("pe", "act", "dve", "pool") if pr.n[pr.sem[e]]] or pr.bar
            s_o = pr.new_sem("s_o")
            for b in range(B):
                h = dma("sp", s_o, lambda e, b=b: e.dma_start(out.rearrange("(t p) c -> p t c", p=P)[:, TB_ * b:TB_ * b + TB_, :], X[:, TB_ * b:TB_ * b + TB_, :]), last)
            pr.wait("sp", h)
            with nc.Block() as block:
                for name, eng in (("sync", "sp"), ("tensor", "pe"), ("scalar", "act"), ("vector", "dve"), ("gpsimd", "pool")):
                    def run(e, items=pr.q[eng]):
                        for it in items:
                            it(e)
                    {"sync": block.sync, "tensor": block.tensor, "scalar": block.scalar, "vector": block.vector, "gpsimd": block.gpsimd}[name](run)

        hi0 = arena.hi
        W1c = arena.down(2 * FH).rearrange("p (c n) -> p c n", c=2)
        Wc = [arena.down(8 * D).rearrange("p (f n) -> p f n", f=8) for _ in range(B)]
        bc = [arena.down(D) for _ in range(B)]
        Wg = arena.down(16).rearrange("p (c n) -> p c n", c=2)
        mark = arena.lo
        w1 = arena.up(2 * P).rearrange("p (c n) -> p c n", c=2)
        w2 = arena.up(D)
        dw1 = arena.up(2 * 64).rearrange("p (c n) -> p c n", c=2)
        dw2 = arena.up(D)
        Wr, Wk, Wv, Wo = (arena.up(2 * D).rearrange("p (c n) -> p c n", c=2) for _ in range(4))
        hT2 = [arena.up(2 * S).rearrange("p (c s) -> p c s", c=2) for _ in range(B)]
        mark2 = arena.lo
        s_w = pr.new_sem("s_w")
        for b in range(B):
            h_x = load(s_x, hT2[b], a["xT"].rearrange("(c p) n -> p c n", c=2)[:, :, S * b:S * b + S])
            h_x = load(s_x, X[:, TB_ * b:TB_ * b + TB_, :], a["x"].rearrange("(t p) c -> p t c", p=P)[:, TB_ * b:TB_ * b + TB_, :])
        wA = adapter_space(P)
        h_a = [h_x]
        for b in range(B):
            h_a = adapter("a", b, P, 8, 0, "L0_cond_down_w", None, "L0_cond_up_w", "L0_cond_up_b", "gb0", hT2[b], hT2[b], h_a, wA)
            if b == 0:
                load(s_w, w1, kmaj("L0_attn_time_maa_w1"))
                load(s_w, w2, a["L0_attn_time_maa_w2"])
                load(s_w, dw1, kmaj("L0_attn_time_decay_w1"))
                load(s_w, dw2[0:64], a["L0_attn_time_decay_w2"])
                for w_, n_ in ((Wr, "r"), (Wk, "k"), (Wv, "v"), (Wo, "o")):
                    h_w = load(s_w, w_, kmaj("L0_attn_W_" + n_))
        s_wc = pr.new_sem("s_wc")
        load(s_wc, W1c, kmaj("L0_cond2_W1"))
        for b in range(B):
            load_id(2 + b, E)
            load(s_wc, Wc[b][:, :, 0:192], a["L0_cond2_W2"].rearrange("(f p) n -> p f n", f=8))
            load_by(s_wc, Wc[b][:, :, 192:256], lambda r: a["L0_cond2_We"].rearrange("e (f p) n -> e p f n", f=8)[bass.ds(r, 1)].rearrange("e p f n -> (e p) f n"), 2 + b)
            load(s_wc, bc[b][:, 0:192], a["L0_cond2_b2"].partition_broadcast(P))
            load_by(s_wc, bc[b][:, 192:256], lambda r: a["L0_cond2_be"][bass.ds(r, 1)].rearrange("e n -> (e n)").partition_broadcast(P), 2 + b)
        h_wc = load(s_wc, Wg, kmaj("L0_ffn_Wg"))
        pr.barrier("b")
        arena.lo = mark2

        def full():
            return arena.up(2 * S).rearrange("p (c s) -> p c s", c=2)

        xx, tmp, xf = full(), full(), full()
        rT, kT, vT, wT, yl = full(), full(), full(), full(), full()
        vtok = arena.up(TB_ * D).rearrange("p (t c) -> p t c", t=TB_)
        mT = arena.up(S)
        Gb = tmp
        rg = xx
        tp2 = [arena.up(512) for _ in range(4)]
        tp_free = [[] for _ in range(4)]
        KR, RR = full(), full()
        rp = full()
        Wb = arena.up(P)
        PB = arena.up(P)
        TD = arena.up(16).rearrange("p (c n) -> p c n", c=2)
        KD = [arena.up(S) for _ in range(2)]
        AT = arena.up(16 * P).rearrange("p (n h t) -> p n h t", n=8, h=2)
        KE = mT
        St = arena.up(2 * 9 * 64).rearrange("p (c n j) -> p c n j", c=2, n=9)
        ytok, rpp = xf.rearrange("p c s -> p (c s)").rearrange("p (t c) -> p t c", t=TB_), RR
        st = arena.up(6 * 32 + 2 * 32 + 96)
        h0 = [op("dve", lambda e: e.memset(AT[:, :, :, 0:16], 0.0))]
        h0b = None

        hprev = []
        for b in range(B):
            hT = hT2[b]
            h1 = op("dve", lambda e, hT=hT: e.tensor_tensor(xx[:, :, 1:S], hT[:, :, 0:S - 1], hT[:, :, 1:S], ALU.subtract), hprev)
            h2 = op("dve", lambda e, hT=hT: e.tensor_scalar(xx[:, :, 0:1], hT[:, :, 0:1], -1.0, None, ALU.mult))
            hx = []
            for c in range(2):
                hx.append(op("dve", lambda e, c=c, hT=hT: e.scalar_tensor_tensor(out=tmp[:, c], in0=xx[:, c], scalar=cv("maa_x", c), in1=hT[:, c], op0=ALU.mult, op1=ALU.add), h1, h2, h_cst))
            hm = []
            for n in range(2):
                i, fr = bank()
                for c in range(2):
                    h = mm(PS[:, i, :], w1[:, c, :], tmp[:, c, 512 * n:512 * n + 512], c == 0, c == 1, [h_w, fr, hx])
                h = op("act", lambda e, i=i, n=n: e.activation(mT[:, 512 * n:512 * n + 512], PS[:, i, :], ACT.Tanh), h)
                bank_free[i] = [h]
                hm.append(h)
            hxf_rd = [hx]
            bufs = [tmp, xf]
            rd = [[hm], [hprev]]
            ek = {}
            for q, (f, nm) in enumerate(((0, "w"), (1, "k"), (2, "v"), (3, "r"))):
                dst = bufs[q % 2]
                hf = []
                for c in range(2):
                    for n in range(2):
                        i, fr = bank()
                        sl = slice(512 * n, 512 * n + 512)
                        h = mm(PS[:, i, :], w2[32 * f:32 * f + 32, P * c:P * c + P], mT[32 * f:32 * f + 32, sl], True, True, [fr, hm])
                        h = op("dve", lambda e, i=i, c=c, sl=sl, dst=dst, nm=nm: e.scalar_tensor_tensor(out=dst[:, c, sl], in0=PS[:, i, :], scalar=cv("maa_" + nm, c), in1=xx[:, c, sl], op0=ALU.add, op1=ALU.mult), h, rd[q % 2])
                        bank_free[i] = [h]
                        h = op("pool", lambda e, c=c, sl=sl, dst=dst, hT=hT: e.tensor_tensor(dst[:, c, sl], dst[:, c, sl], hT[:, c, sl], ALU.add), h)
                        hf.append(h)
                if nm == "w":
                    hw2 = []
                    for n in range(2):
                        sl = slice(512 * n, 512 * n + 512)
                        i, fr = bank()
                        for c in range(2):
                            h = mm(PS[0:64, i, :], dw1[:, c, :], dst[:, c, sl], c == 0, c == 1, [fr, hf])
                        h = op("act", lambda e, i=i, sl=sl: e.activation(yl[0:64, 0, sl], PS[0:64, i, :], ACT.Tanh), h, hprev)
                        bank_free[i] = [h]
                        hw2.append(h)
                    rd[q % 2] = [hw2]
                    hw = []
                    for c in range(2):
                        for n in range(2):
                            sl = slice(512 * n, 512 * n + 512)
                            i, fr = bank()
                            h = mm(PS[:, i, :], dw2[0:64, P * c:P * c + P], yl[0:64, 0, sl], True, True, [fr, hw2[n]])
                            h = op("act", lambda e, i=i, c=c, sl=sl: e.activation(wT[:, c, sl], PS[:, i, :], ACT.Exp, bias=cv("decay", c)), h)
                            bank_free[i] = [h]
                            h = op("act", lambda e, c=c, sl=sl: e.activation(wT[:, c, sl], wT[:, c, sl], ACT.Exp, scale=-1.0), h)
                            hw.append(h)
                    continue
                Wm = {"k": Wk, "v": Wv, "r": Wr}[nm]
                dT = {"k": kT, "v": vT, "r": rT}[nm]
                hh = []
                for c in range(2):
                    for n in range(2):
                        sl = slice(512 * n, 512 * n + 512)
                        i, fr = bank()
                        for k in range(2):
                            h = mm(PS[:, i, :], Wm[:, k, P * c:P * c + P], dst[:, k, sl], k == 0, k == 1, [fr, hf])
                        h = op("act", lambda e, i=i, c=c, sl=sl, dT=dT: e.copy(dT[:, c, sl], PS[:, i, :]), h, hprev)
                        bank_free[i] = [h]
                        hh.append(h)
                if nm == "v":
                    for t in range(0, TB_, 2):
                        i, fr = bank()
                        for j in range(2):
                            for k in range(2):
                                h = mm(PS[:, i, D * j:D * j + D], dst[:, k, P * (t + j):P * (t + j) + P], Wm[:, k, :], k == 0, k == 1, [fr, hf])
                        h = op("act", lambda e, i=i, t=t: e.copy(vtok[:, t:t + 2, :], PS[:, i, :].rearrange("p (a c) -> p a c", a=2)), h, hprev)
                        bank_free[i] = [h]
                        hh.append(h)
                rd[q % 2] = [hh]
                ek[nm] = hh
            hk, hv, hr = ek["k"], ek["v"], ek["r"]
            w4, r4, k4, v4 = (z.rearrange("p c (m l) -> p (c m) l", l=16) for z in (wT, rT, kT, vT))
            KR4, RR4, rp4 = (z.rearrange("p c (m l) -> p (c m) l", l=16) for z in (KR, RR, rp))
            h = op("dve", lambda e: e.memset(RR4[:, :, 0:1], 1.0), hprev)
            hR = op("pool", lambda e: e.memset(KR4[:, :, 15:16], 1.0), hprev)
            for j in range(1, 16):
                h = op("dve", lambda e, j=j: e.tensor_tensor(RR4[:, :, j:j + 1], RR4[:, :, j - 1:j], w4[:, :, j - 1:j], ALU.mult), h, hw)
                hR = op("pool", lambda e, j=j: e.tensor_tensor(KR4[:, :, 15 - j:16 - j], KR4[:, :, 16 - j:17 - j], w4[:, :, 16 - j:17 - j], ALU.mult), hR, hw)
            hWb = op("dve", lambda e: e.tensor_tensor(Wb.unsqueeze(2), RR4[:, :, 15:16], w4[:, :, 15:16], ALU.mult), h)
            hKR = op("pool", lambda e: e.tensor_tensor(KR, KR, kT, ALU.mult), hR, hk)
            hrp = op("dve", lambda e: e.tensor_tensor(rp, RR, rT, ALU.mult), h, hr)
            Wb4 = Wb.rearrange("p (c n a) -> p c n a", c=2, a=8)
            PB4 = PB.rearrange("p (c n a) -> p c n a", c=2, a=8)
            h = op("dve", lambda e: e.memset(PB4[:, :, :, 0:1], 1.0), hprev)
            for j in range(1, 8):
                h = op("dve", lambda e, j=j: e.tensor_tensor(PB4[:, :, :, j:j + 1], PB4[:, :, :, j - 1:j], Wb4[:, :, :, j - 1:j], ALU.mult), h, hWb)
            hTD = op("dve", lambda e: e.tensor_tensor(TD.unsqueeze(3), PB4[:, :, :, 7:8], Wb4[:, :, :, 7:8], ALU.mult), h)
            hrpp = op("dve", lambda e: e.tensor_tensor(RR4, rp4, PB.unsqueeze(2).broadcast_to([P, P, 16]), ALU.mult), h, hrp)

            hG = op("act", lambda e: e.copy(Gb, kT), hk, rd[0], rd[1])
            for c in range(2):
                hrg = op("dve", lambda e, c=c: e.scalar_tensor_tensor(out=rg[:, c], in0=rT[:, c], scalar=cv("faaaa", c), in1=kT[:, c], op0=ALU.mult, op1=ALU.mult), hr, hk, hf)
            G4, rg4, y4 = (z.rearrange("p c (m l) -> p (c m) l", l=16) for z in (Gb, rg, yl))
            h_rgrd = []
            hyl = [None] * 4
            for dl in range(16):
                L = 16 - dl
                if dl:
                    hrg = op("pool", lambda e, dl=dl, L=L: e.tensor_tensor(rg4[:, :, 0:L], r4[:, :, dl:16], G4[:, :, 0:L], ALU.mult), hG, h_rgrd)
                    if dl < 15:
                        hG = op("dve", lambda e, dl=dl, L=L: e.tensor_tensor(G4[:, :, 0:L - 1], G4[:, :, 0:L - 1], w4[:, :, dl:15], ALU.mult), hrg, hw)
                h_rgrd = []
                for g in range(4):
                    i, fr = bank()
                    ms = slice(32 * g, 32 * g + 32)
                    pv = PS[:, i, 0:32 * L].rearrange("p (m l) -> p m l", l=L)
                    h = mm(PS[:, i, 0:32 * L], headb, rg4[:, ms, 0:L], True, True, [fr, hrg, h_cst])
                    h_rgrd.append(h)
                    if dl == 0:
                        h = op("dve", lambda e, pv=pv, ms=ms: e.tensor_tensor(y4[:, ms, :], pv, v4[:, ms, :], ALU.mult), h, hv, hw)
                        bank_free[i] = [h]
                        hyl[g] = h
                        continue
                    tb = tp2[g][:, 0:32 * L].rearrange("p (m l) -> p m l", l=L)
                    h = op("dve", lambda e, pv=pv, ms=ms, tb=tb, L=L: e.tensor_tensor(tb, pv, v4[:, ms, 0:L], ALU.mult), h, tp_free[g])
                    bank_free[i] = [h]
                    h = op("pool", lambda e, ms=ms, tb=tb, dl=dl: e.tensor_tensor(y4[:, ms, dl:16], y4[:, ms, dl:16], tb, ALU.add), h, hyl[g])
                    hyl[g] = h
                    tp_free[g] = [h]

            hSt = []
            hy = []
            KRn = KR.rearrange("p c (n s) -> p c n s", n=8)
            for c in range(2):
                KDv = [z.rearrange("p (n s) -> p n s", n=8) for z in KD]
                hz = [op("pool", lambda e, z=z: e.memset(z, 0.0), h_kd if (b or c) else []) for z in KD]
                kd_rd = [[hz[0]], [hz[1]]]
                hkd = None
                banks = [bank() for _ in range(4)]
                for q in range(1, 9):
                    cur, old = KDv[q % 2], KDv[(q - 1) % 2]
                    h1 = op("act", lambda e, cur=cur, q=q, c=c: e.copy(cur[:, :, 16 * (q - 1):16 * q], KRn[:, c, :, 16 * (q - 1):16 * q]), hKR, kd_rd[q % 2])
                    h2 = None
                    if q > 1:
                        h2 = op("dve", lambda e, cur=cur, old=old, q=q, c=c: e.tensor_tensor(cur[:, :, 0:16 * (q - 1)], old[:, :, 0:16 * (q - 1)], Wb4[:, c, :, q - 1:q].broadcast_to([P, 8, 16 * (q - 1)]), ALU.mult), hkd, kd_rd[q % 2], hWb)
                    hkd = [h1, h2]
                    if q == 8:
                        break
                    for n in range(8):
                        for hh_ in range(2):
                            i, fr = banks[2 * (n // 4) + hh_]
                            col = P * (n % 4) + 16 * q
                            rows = slice(64 * hh_, 64 * hh_ + 64)
                            h = mm(PS[:, i, col:col + 16], cur[rows, n, :], rp[rows, c, P * n + 16 * q:P * n + 16 * q + 16], True, True, [fr, hkd, hrp], inc=(n == 7 and hh_ == 1))
                    kd_rd[q % 2] = [h, h2]
                    kd_rd[(q - 1) % 2] = kd_rd[(q - 1) % 2] + [h2]
                hAT = []
                for k in range(4):
                    i = banks[k][0]
                    h3 = op("act", lambda e, i=i, k=k: e.copy(AT[:, 4 * (k // 2):4 * (k // 2) + 4, k % 2, 16:P], PS[:, i, :].rearrange("p (n t) -> p n t", n=4)[:, :, 16:P]), h, hSt, hy)
                    bank_free[i] = [h3]
                    hAT.append(h3)
                hKE = []
                for g in range(2):
                    i, fr = bank()
                    for j in range(4):
                        n = 4 * g + j
                        h = op("pe", lambda e, i=i, j=j, n=n: e.transpose(PS[:, i, P * j:P * j + P], KDv[0][:, n, :], ident), fr, hkd, inc=(j == 3))
                    h_kd = [h]
                    h = op("act", lambda e, i=i, g=g: e.copy(KE[:, 512 * g:512 * g + 512], PS[:, i, :]), h, hSt)
                    bank_free[i] = [h]
                    hKE.append(h)
                i, fr = bank()
                for n in range(8):
                    for hh_ in range(2):
                        ch = P * c + 64 * hh_
                        h = mm(PS[64 * hh_:64 * hh_ + 64, i, 64 * n:64 * n + 64], KE[:, P * n + 64 * hh_:P * n + 64 * hh_ + 64], vtok[:, n, ch:ch + 64], True, True, [fr, hKE, hv], inc=(n == 7 and hh_ == 1))
                hs = op("dve", lambda e, c=c: e.memset(St[:, c, 0, :], 0.0), hy)
                for n in range(7):
                    hs = op("dve", lambda e, c=c, n=n, i=i: e.scalar_tensor_tensor(out=St[:, c, n + 1, :], in0=St[:, c, n, :], scalar=TD[:, c, n:n + 1], in1=PS[:, i, 64 * n:64 * n + 64], op0=ALU.mult, op1=ALU.add), h, hs, hTD)
                bank_free[i] = [hs]
                hSt = [h, hs]
                hy = []
                for hh_ in range(2):
                    i, fr = bank()
                    rows = slice(64 * hh_, 64 * hh_ + 64)
                    ch = P * c + 64 * hh_
                    for t in range(8):
                        o = PS[:, i, 64 * t:64 * t + 64]
                        mm(o, AT[:, t, hh_, :], vtok[:, t, ch:ch + 64], True, False, [fr, hAT, hs, hyl, hrpp, h0])
                        mm(o, RR[rows, c, P * t:P * t + P], St[rows, c, t, :], False, False)
                        h = mm(o, yl[:, c, P * t:P * t + P], ident[:, 64 * hh_:64 * hh_ + 64], False, True, inc=(t == 7))
                    h2 = op("act", lambda e, i=i, ch=ch: e.copy(ytok[:, :, ch:ch + 64], PS[:, i, :].rearrange("p (j x) -> p j x", j=8)), h, rd[1])
                    bank_free[i] = [h2]
                    hy.append(h2)
                hy_all = hy if c == 0 else hy_all + hy
            yg = ytok.rearrange("p t (h j) -> p (t h) j", j=64)
            mv = st[:, 192:256].rearrange("p (g k) -> p g k", k=2)
            for g in range(32):
                h = op("dve", lambda e, g=g: e.bn_stats(st[:, 6 * g:6 * g + 6], yg[:, g, :]), hy_all)
            for g in range(32):
                h = op("dve", lambda e, g=g: e.bn_aggr(mv[:, g, :], st[:, 6 * g:6 * g + 6]), h if g == 0 else None)
            h = op("dve", lambda e: e.tensor_scalar(st[:, 256:288], mv[:, :, 1], 0.00064, None, ALU.add), h)
            h = op("act", lambda e: e.activation(st[:, 288:320], st[:, 256:288], ACT.Sqrt), h)
            h = op("dve", lambda e: e.reciprocal(st[:, 320:352], st[:, 288:320]), h)
            h = op("dve", lambda e: e.tensor_tensor(yg, yg, mv[:, :, 0:1].broadcast_to([P, 32, 64]), ALU.subtract), h)
            h = op("dve", lambda e: e.tensor_tensor(yg, yg, st[:, 320:352].unsqueeze(2).broadcast_to([P, 32, 64]), ALU.mult), h)
            hyn = h
            hT_n = []
            for c in range(2):
                for g in range(2):
                    i, fr = bank()
                    for j in range(4):
                        t = 4 * g + j
                        h = op("pe", lambda e, i=i, j=j, t=t, c=c: e.transpose(PS[:, i, P * j:P * j + P], ytok[:, t, P * c:P * c + P], ident), fr, hyn, inc=(j == 3))
                    h = op("act", lambda e, i=i, c=c, g=g: e.activation(tmp[:, c, 512 * g:512 * g + 512], PS[:, i, :], ACT.Identity, bias=cv("ln_b", c), scale=cv("ln_w", c)), h, hG, hrg)
                    bank_free[i] = [h]
                    hT_n.append(h)
            for t in range(0, TB_, 2):
                i, fr = bank()
                for j in range(2):
                    for k in range(2):
                        h = mm(PS[:, i, D * j:D * j + D], tmp[:, k, P * (t + j):P * (t + j) + P], Wo[:, k, :], k == 0, k == 1, [fr, hT_n])
                xs = X[:, TB_ * b + t:TB_ * b + t + 2, :]
                h = op("dve", lambda e, i=i, xs=xs: e.tensor_tensor(xs, xs, PS[:, i, :].rearrange("p (a c) -> p a c", a=2), ALU.add), h)
                bank_free[i] = [h]
            hprev = [(pr.sem[e], pr.n[pr.sem[e]]) for e in ("pe", "act", "dve", "pool")]
        bar = pr.barrier("c")
        if dbg == "x0":
            return finish()

        arena.lo = base0
        CN = arena.up(4 * S).bitcast(BF16).rearrange("p (t k) -> p t k", t=TB_)
        PM = arena.up(2 * S).bitcast(U8).rearrange("p (t k) -> p t k", t=TB_)
        e_mark = arena.lo
        C1 = arena.up(NT * D).rearrange("p (t c) -> p t c", t=NT)
        c_mark = arena.lo
        b2e = arena.up(E * D)
        s_b2 = pr.new_sem("s_b2")
        h_wc = [h_wc, load(s_b2, b2e, a["L0_ffn_b2"].rearrange("e c -> (e c)").partition_broadcast(P), bar)]
        NEX = 2
        exw = [(arena.up(2 * FH).rearrange("p (c n) -> p c n", c=2), arena.up(8 * D).rearrange("p (f n) -> p f n", f=8)) for _ in range(NEX)]
        h_ex = {}
        s_ex = [pr.new_sem("s_ex") for _ in range(NEX)]

        def get_w(e_, waits=()):
            load(s_ex[e_ % NEX], exw[e_ % NEX][0], a["L0_ffn_W1"][e_].rearrange("(c p) n -> p c n", c=2), *waits)
            h_ex[e_] = load(s_ex[e_ % NEX], exw[e_ % NEX][1], a["L0_ffn_W2"][e_].rearrange("(f p) n -> p f n", f=8))

        for e_ in range(NEX):
            get_w(e_, [bar])
        zt = arena.up(2048)
        iota = arena.up(S)
        pki = arena.up(TB_ * 32).bitcast(I32).rearrange("p (t j) -> p t j", t=TB_)
        pkf = arena.up(TB_ * 32).rearrange("p (t j) -> p t j", t=TB_)
        pkm = arena.up(TB_ * 8).bitcast(U8).rearrange("p (t j) -> p t j", t=TB_)
        hit = arena.up(S // 2).bitcast(BF16)
        pkmf = arena.up(TB_ * 32).rearrange("p (t j) -> p t j", t=TB_)
        s_pk = pr.new_sem("s_pk")
        load(s_pk, iota, a["k_iota"])
        load(s_pk, pki, a["idx"].rearrange("(t p) j -> p t j", p=P))
        load(s_pk, pkm, a["imask"].rearrange("(t p) j -> p t j", p=P))
        h_pk = load(s_pk, PM, a["pmask"].rearrange("(t p) k -> p t k", p=P))
        h = op("pool", lambda e: e.tensor_copy(pkf, pki), h_pk)
        h = op("pool", lambda e: e.tensor_scalar(pkf, pkf, 1.0, None, ALU.add), h)
        h2 = op("pool", lambda e: e.tensor_copy(pkmf, pkm), h_pk)
        h = op("pool", lambda e: e.tensor_tensor(pkf, pkf, pkmf, ALU.mult), h, h2)
        h = op("pool", lambda e: e.tensor_scalar(pkf, pkf, 1.0, None, ALU.subtract), h)
        h_pkf = h

        def count(eng, t, j, h):
            col = pkf[:, t, j:j + 1]
            if j == 0:
                return op(eng, lambda e: e.tensor_scalar(CN[:, t, :], iota, col, None, ALU.is_equal), h_pkf)
            if eng == "dve":
                return op(eng, lambda e: e.scalar_tensor_tensor(out=CN[:, t, :], in0=iota, scalar=col, in1=CN[:, t, :], op0=ALU.is_equal, op1=ALU.add), h)
            h = op(eng, lambda e: e.tensor_scalar(hit, iota, col, None, ALU.is_equal), h)
            return op(eng, lambda e: e.tensor_tensor(CN[:, t, :], CN[:, t, :], hit, ALU.add), h)

        cn_h = [None] * TB_
        cn_work = {"pool": [(t, j) for t in range(2) for j in range(32)], "dve": [(t, j) for t in range(2, 8) for j in range(32)]}

        def pump(eng, n):
            for _ in range(min(n, len(cn_work[eng]))):
                t, j = cn_work[eng].pop(0)
                cn_h[t] = count(eng, t, j, cn_h[t])

        pump("pool", 200)
        h = op("dve", lambda e: e.memset(zt, 0.0))
        s_z = pr.new_sem("s_z")
        for j in range(4):
            h_zero = dma("act", s_z, lambda e, j=j: e.dma_start(Xg[1024 * j:1024 * j + 1024, :].rearrange("(p r) c -> p (r c)", p=P), zt), h)
        xT1 = [arena.up(2 * S).rearrange("p (c s) -> p c s", c=2) for _ in range(B)]
        hb = [arena.up(8 * 512).rearrange("p (f s) -> p f s", f=8) for _ in range(2)]
        hb_rd = [[], []]
        xT_h = [to_T(X[:, TB_ * b:TB_ * b + TB_, :], xT1[b], [], "dve") for b in range(B)]

        def mlp_hidden(src, s0, w, bias, func, dst, waits):
            last = None
            for f in range(8):
                i, fr = bank()
                for k in range(2):
                    h = mm(PS[:, i, :], w[:, k, P * f:P * f + P], src[:, k, s0:s0 + 512], k == 0, k == 1, [fr, waits])
                last = op("act", lambda e, i=i, f=f: e.activation(dst[:, f, :], PS[:, i, :], func, bias=cvec[:, bias + f:bias + f + 1]), h)
                bank_free[i] = [last]
            return last

        def mlp_out(src, w, bias, dst, waits, dwaits):
            hs_ = []
            for t in range(0, 4, 2):
                i, fr = bank()
                for j in range(2):
                    for f in range(8):
                        h = mm(PS[:, i, D * j:D * j + D], src[:, f, P * (t + j):P * (t + j) + P], w[:, f, :], f == 0, f == 7, [fr, waits])
                h2 = op("dve", lambda e, i=i, t=t: e.tensor_tensor(dst[:, t:t + 2, :], PS[:, i, :].rearrange("p (a c) -> p a c", a=2), bias.unsqueeze(1).broadcast_to([P, 2, D]), ALU.add), h, dwaits)
                bank_free[i] = [h2]
                hs_.append(h2)
            return h, hs_

        pend = None
        hC = []
        for q in range(5):
            pump("dve", 26)
            if q < 4:
                b, n = q // 2, q % 2
                hh = mlp_hidden(xT1[b], 512 * n, W1c, CB1, ACT.Gelu, hb[q % 2], [h_wc, xT_h[b], hb_rd[q % 2]])
            if pend is not None:
                pq, ph = pend
                hp, hs_ = mlp_out(hb[pq % 2], Wc[pq // 2], bc[pq // 2], C1[:, 4 * pq:4 * pq + 4, :], [ph], [h_wc])
                hb_rd[pq % 2] = [hp]
                hC += hs_
            pend = (q, hh) if q < 4 else None

        xr0, xr1 = (z.rearrange("p c s -> p (c s)") for z in xT1)
        hT_ = [to_T(C1[:, TB_ * b:TB_ * b + TB_, :], xT1[b], [hC], "dve") for b in range(B)]
        rt = arena.up(1600)
        at = [0]

        def ra(n):
            at[0] += n
            return rt[:, at[0] - n:at[0]]

        def v8(z):
            return z.rearrange("p (t e) -> p t e", e=8)

        PR, M8, OH, PQ = ra(128), ra(128), ra(256), ra(256)
        IX = ra(128).bitcast(U32)
        IXF = ra(32).rearrange("p (k t) -> p k t", k=2)
        BS = ra(256)
        s1, s2, wk, posk, keep, sl, tk = (ra(32).rearrange("p (k t) -> p k t", k=2) for _ in range(7))
        cnt = ra(8)
        WK = ra(32).rearrange("p (k t) -> p k t", k=2)
        SI = ra(32).bitcast(I32).rearrange("p (k t) -> p k t", k=2)
        GI = ra(32).bitcast(I32).rearrange("p (k t) -> p k t", k=2)
        i, fr = bank()
        for t in range(NT):
            for k in range(2):
                h = mm(PS[:, i, 8 * t:8 * t + 8], xT1[t // 8][:, k, P * (t % 8):P * (t % 8) + P], Wg[:, k, :], k == 0, k == 1, [fr, hT_, h_wc], inc=(t == NT - 1 and k == 1))
        LG = v8(PS[:, i, 0:128])

        def dv(fn, *w):
            return op("dve", fn, *w)

        mx = s1.rearrange("p k t -> p (k t)")[:, 0:16]
        sm = s2.rearrange("p k t -> p (k t)")[:, 0:16]
        h = dv(lambda e: e.tensor_reduce(mx, LG, AX.X, ALU.max), h)
        h = dv(lambda e: e.tensor_tensor(v8(PR), LG, mx.unsqueeze(2).broadcast_to([P, 16, 8]), ALU.subtract), h)
        bank_free[i] = [h]
        h = op("act", lambda e: e.activation(PR, PR, ACT.Exp), h)
        h = dv(lambda e: e.tensor_reduce(sm, v8(PR), AX.X, ALU.add), h)
        h = dv(lambda e: e.reciprocal(mx, sm), h)
        h = dv(lambda e: e.tensor_tensor(v8(PR), v8(PR), mx.unsqueeze(2).broadcast_to([P, 16, 8]), ALU.mult), h)
        for t in range(NT):
            h2 = dv(lambda e, t=t: e.max(v8(M8)[:, t, :], v8(PR)[:, t, :]), h)
        for t in range(NT):
            h3 = dv(lambda e, t=t: e.max_index(IX[:, 8 * t:8 * t + 8], v8(M8)[:, t, :], v8(PR)[:, t, :]), h2)
        M8k = v8(M8)[:, :, 0:2].rearrange("p t k -> p k t")
        h = dv(lambda e: e.tensor_copy(IXF, v8(IX)[:, :, 0:2].rearrange("p t k -> p k t")), h3)
        iota8 = kslot[:, 0:8]
        OHv = OH.rearrange("p (k t e) -> p k t e", k=2, t=16)
        for k in range(2):
            hoh = dv(lambda e, k=k: e.tensor_tensor(OHv[:, k], iota8.unsqueeze(1).broadcast_to([P, 16, 8]), IXF[:, k, :].unsqueeze(2).broadcast_to([P, 16, 8]), ALU.is_equal), h, h_wc)
        h = dv(lambda e: e.tensor_tensor(s1[:, 0, :], M8k[:, 0, :], M8k[:, 1, :], ALU.add), h2)
        h = dv(lambda e: e.tensor_scalar(s1[:, 0, :], s1[:, 0, :], 1e-9, None, ALU.add), h)
        h = dv(lambda e: e.reciprocal(s2[:, 0, :], s1[:, 0, :]), h)
        hwk = dv(lambda e: e.tensor_tensor(wk, M8k, s2[:, 0:1, :].broadcast_to([P, 2, 16]), ALU.mult), h)
        i, fr = bank()
        h = mm(PS[:, i, 0:256], triu, OH, True, True, [fr, hoh])
        h = mm(PS[:, i, 256:512], onesm, OH, True, True)
        BSv = BS.rearrange("p (k t e) -> p k t e", k=2, t=16)
        TOT = PS[:, i, 256:512].rearrange("p (k t e) -> p k t e", k=2, t=16)
        PQv = PQ.rearrange("p (k t e) -> p k t e", k=2, t=16)
        h0_ = dv(lambda e: e.memset(BSv[:, :, 0, :], -1.0), h)
        for t in range(1, NT):
            h0_ = dv(lambda e, t=t: e.tensor_tensor(BSv[:, :, t, :], BSv[:, :, t - 1, :], TOT[:, :, t - 1, :], ALU.add), h0_)
        h1 = dv(lambda e: e.tensor_tensor(cnt, BSv[:, 0, 15, :], TOT[:, 0, 15, :], ALU.add), h0_)
        h1 = dv(lambda e: e.tensor_scalar(cnt, cnt, 1.0, float(CAP), ALU.add, ALU.min), h1)
        h2 = dv(lambda e, i=i: e.tensor_tensor(PQ, PS[:, i, 0:256], BS, ALU.add), h0_)
        bank_free[i] = [h2]
        h2 = dv(lambda e: e.tensor_tensor(PQv[:, 1], PQv[:, 1], cnt.unsqueeze(1).broadcast_to([P, 16, 8]), ALU.add), h2, h1)
        h2 = dv(lambda e: e.tensor_tensor(PQ, PQ, OH, ALU.mult), h2)
        h2 = dv(lambda e: e.tensor_reduce(posk, PQv, AX.X, ALU.add), h2)
        h3 = dv(lambda e: e.tensor_scalar(keep, posk, float(CAP), None, ALU.is_lt), h2)
        h4 = dv(lambda e: e.scalar_tensor_tensor(out=sl, in0=IXF, scalar=float(CAP), in1=posk, op0=ALU.mult, op1=ALU.add), h2)
        hWK = dv(lambda e: e.tensor_tensor(WK, wk, keep, ALU.mult), hwk, h3)
        h5 = dv(lambda e: e.tensor_tensor(sl, sl, keep, ALU.mult), h3, h4)
        hGI = dv(lambda e: e.tensor_copy(GI, sl), h5)
        trash = kslot[:, 8:24]
        h6 = dv(lambda e: e.tensor_scalar(tk, keep, -1.0, 1.0, ALU.mult, ALU.add), h3)
        for k in range(2):
            h7 = dv(lambda e, k=k: e.tensor_scalar(s1[:, k, :], trash, float(N * k), None, ALU.add), h)
        h7 = dv(lambda e: e.tensor_tensor(tk, tk, s1, ALU.mult), h6, h7)
        h7 = dv(lambda e: e.tensor_tensor(sl, sl, tk, ALU.add), h7, hGI)
        hSI = dv(lambda e: e.tensor_copy(SI, sl), h7)
        s_sc = pr.new_sem("s_sc")
        for k in range(2):
            for t in range(NT):
                h_sc = dma("pool", s_sc, lambda e, k=k, t=t: e.indirect_dma_start(
                    Xg[:, :], bass.IndirectOffsetOnAxis(ap=SI[:, k, t:t + 1].bitcast(U32), axis=0), C1[:, t, :], None), hSI, hC, h_zero)

        xg = [arena.up(4 * D).rearrange("p (t c) -> p t c", t=4) for _ in range(2)]
        xgT = [xr0[:, 1024 * j:1024 * j + 1024].rearrange("p (c s) -> p c s", c=2) for j in range(2)]
        ye = [xr1[:, 1024 * j:1024 * j + 1024].rearrange("p (t c) -> p t c", t=4) for j in range(2)]
        xg_rd, xgT_rd, ye_rd = [[]] * 3, [[]] * 2, [[]] * 2
        s_xg = [pr.new_sem("s_xg") for _ in range(2)]
        s_ye = [pr.new_sem("s_ye") for _ in range(2)]
        hb_rd = [[(pr.sem["pe"], pr.n[pr.sem["pe"]])]] * 2
        h_yst = []
        h_xg = {}

        def get_x(e_):
            h_xg[e_] = load(s_xg[e_ % 2], xg[e_ % 2], Xg[CAP * e_:CAP * e_ + CAP, :].rearrange("(t p) c -> p t c", p=P), h_sc, xg_rd[e_ % 2])

        for e_ in range(2):
            get_x(e_)
        pend = None
        for e_ in range(E + 1):
            pump("dve", 10)
            if e_ < E:
                u = e_ % 2
                T_ = []
                for c in range(2):
                    i, fr = bank()
                    for j in range(4):
                        h = op("pe", lambda e, i=i, j=j, c=c, u=u: e.transpose(PS[:, i, P * j:P * j + P], xg[u][:, j, P * c:P * c + P], ident), fr, h_xg[e_], inc=(j == 3))
                    h2 = op("dve", lambda e, i=i, c=c, e_=e_: e.tensor_copy(xgT[e_ % 2][:, c, :], PS[:, i, :]), h, xgT_rd[e_ % 2])
                    bank_free[i] = [h2]
                    T_.append(h2)
                xg_rd[u] = [h]
                if e_ + 2 < E:
                    get_x(e_ + 2)
                w1e, w2e = exw[e_ % NEX]
                hh = mlp_hidden(xgT[e_ % 2], 0, w1e, CB1 + 8 + 8 * e_, ACT.Gelu_apprx_tanh, hb[e_ % 2], [h_ex[e_], T_, hb_rd[e_ % 2]])
                xgT_rd[e_ % 2] = [(pr.sem["pe"], pr.n[pr.sem["pe"]])]
            if pend is not None:
                pe_, ph = pend
                hp, hs_ = mlp_out(hb[pe_ % 2], exw[pe_ % NEX][1], b2e[:, D * pe_:D * pe_ + D], ye[pe_ % 2], [ph], [h_wc, ye_rd[pe_ % 2]])
                hb_rd[pe_ % 2] = [hp]
                h = load(s_ye[pe_ % 2], Ye[CAP * pe_:CAP * pe_ + CAP, :].rearrange("(t p) c -> p t c", p=P), ye[pe_ % 2], hs_)
                ye_rd[pe_ % 2] = [h]
                h_yst.append(h)
                if pe_ + NEX < E:
                    get_w(pe_ + NEX, [hp])
            pend = (e_, hh) if e_ < E else None
        gt = [zt[:, D * j:D * j + D] for j in range(8)]
        s_g = [pr.new_sem("s_g") for _ in range(8)]
        gt_rd = [[] for _ in range(8)]
        hx_ = [None] * NT
        for j in range(2 * NT):
            t, k, u = j // 2, j % 2, j % 8
            h = dma("pool", s_g[u], lambda e, k=k, t=t, u=u: e.indirect_dma_start(
                gt[u], None, Ye[:, :], bass.IndirectOffsetOnAxis(ap=GI[:, k, t:t + 1].bitcast(U32), axis=0)), h_yst, gt_rd[u], hGI)
            h = dv(lambda e, k=k, t=t, u=u: e.scalar_tensor_tensor(out=X[:, t, :], in0=gt[u], scalar=WK[:, k, t:t + 1], in1=X[:, t, :], op0=ALU.mult, op1=ALU.add), h, hx_[t], hWK)
            hx_[t] = h
            gt_rd[u] = [h]
        pr.barrier("e")
        if dbg == "x1":
            return finish()

        def phase_e():
            arena.lo = e_mark
            arena.hi = hi0
            FP = [nc.dram_tensor(f"parts{k}", (3, D, S), BF16, kind="Internal").ap() for k in range(4)]
            Wall = arena.up(8 * D)
            Wq4, Wk4, Wv4, Wo4 = (Wall[:, 2 * D * j:2 * D * j + 2 * D].rearrange("p (c n) -> p c n", c=2) for j in range(4))
            bvb = arena.up(D)
            xT4 = arena.up(2 * S).rearrange("p (c s) -> p c s", c=2)
            K6 = [arena.up(8 * S).bitcast(BF16).rearrange("p (h s) -> p h s", h=16) for _ in range(2)]
            Q6 = [arena.up(8 * P).bitcast(BF16).rearrange("p (h s) -> p h s", h=16) for _ in range(2)]
            V4 = [arena.up(TB_ * 272).rearrange("p (t h j) -> p t h j", t=TB_, h=16) for _ in range(2)]
            X4T = [arena.down(2 * S).rearrange("p (c s) -> p c s", c=2) for _ in range(2)]
            Oc = arena.up(2 * S).rearrange("p (t c) -> p t c", t=TB_)
            Ab = [arena.up(S) for _ in range(2)]
            Sb = [arena.up(S) for _ in range(3)]
            Pt = [arena.up(S) for _ in range(3)]
            mr = arena.up(8)
            rc = arena.up(16)
            ub = arena.up(8)
            s_e = pr.new_sem("s_e")
            ebar = pr.bar
            for w_, n_ in ((Wq4, "Wq"), (Wk4, "Wk"), (Wv4, "Wv"), (Wo4, "Wo")):
                load(s_e, w_, kmaj("L1_cond_" + n_), ebar)
            load(s_e, ub[:, 0:B], a["u"].rearrange("o b -> (o b)").partition_broadcast(P))
            h_we = load(s_e, bvb, a["L1_cond_bv"].partition_broadcast(P))
            h = op("act", lambda e: e.activation(ub[:, 2:4], ub[:, 0:2], ACT.Exp, scale=-5.0), h_we)
            h = op("pool", lambda e: e.tensor_scalar(ub[:, 2:4], ub[:, 2:4], 10.0, None, ALU.mult), h)
            h1 = op("pool", lambda e: e.tensor_scalar(ub[:, 4:6], ub[:, 2:4], 1.0, None, ALU.is_ge), h)
            h = op("pool", lambda e: e.tensor_scalar(ub[:, 2:4], ub[:, 2:4], 1.0, None, ALU.min), h1)
            h = op("pool", lambda e: e.tensor_scalar(ub[:, 6:8], ub[:, 4:6], -1.0, 1.0, ALU.mult, ALU.add), h)
            h_u = op("pool", lambda e: e.tensor_tensor(ub[:, 6:8], ub[:, 6:8], ub[:, 2:4], ALU.mult), h)
            SP_, LD_ = ub[:, 4:6], ub[:, 6:8]
            h_one = [op("pool", lambda e, v=v: e.memset(v[:, :, :, 16:17], 1.0)) for v in V4]
            QF = X4T[0]
            HM = X4T[1].rearrange("p c s -> p (c s)").bitcast(BF16).rearrange("p (k c s) -> p k c s", k=2, c=2)
            LO = Oc.rearrange("p t c -> p (t c)")[:, 0:S].bitcast(BF16).rearrange("p (c s) -> p c s", c=2)
            s_fp = [pr.new_sem("s_fp") for _ in range(4)]
            s_k6 = [pr.new_sem("s_k6") for _ in range(2)]
            s_q6 = [pr.new_sem("s_q6") for _ in range(2)]
            h_fp, h_k6 = {}, []
            stg = []
            xt_rd = []
            for b in range(B):
                hx4 = to_T(X[:, TB_ * b:TB_ * b + TB_, :], xT4, [xt_rd], "act")
                for kq in range(2):
                    w_, bias, sc = ((Wq4, "bq", -0.25), (Wk4, "bk", 1.0))[kq]
                    hq = []
                    for c in range(2):
                        for n in range(2):
                            sl = slice(512 * n, 512 * n + 512)
                            i, fr = bank()
                            for k in range(2):
                                h = mm(PS[:, i, :], w_[:, k, P * c:P * c + P], xT4[:, k, sl], k == 0, k == 1, [fr, hx4, h_we])
                            h = dv(lambda e, i=i, c=c, sl=sl, bias=bias, sc=sc: e.tensor_scalar(QF[:, c, sl], PS[:, i, :], cv(bias, c), sc, ALU.add, ALU.mult), h, stg)
                            bank_free[i] = [h]
                            hq.append(h)
                    h = op("act", lambda e: e.copy(HM[:, 0], QF), hq, stg)
                    h = dv(lambda e: e.tensor_tensor(QF, QF, HM[:, 0], ALU.subtract), h)
                    h = op("act", lambda e: e.copy(HM[:, 1], QF), h)
                    h = dv(lambda e: e.tensor_tensor(LO, QF, HM[:, 1], ALU.subtract), h, stg)
                    j = 2 * b + kq
                    for part, src in ((0, HM[:, 0]), (1, HM[:, 1]), (2, LO)):
                        hd = dma("sp", s_fp[j], lambda e, j=j, part=part, src=src: e.dma_start(FP[j][part].rearrange("(c p) s -> p c s", p=P), src), h)
                    h_fp[j] = hd
                    stg = [hd]
                    if kq:
                        for g, part in enumerate((0, 1, 0, 2, 0, 1)):
                            hk6 = dma("sp", s_k6[b], lambda e, j=j, g=g, part=part, b=b: e.dma_start(K6[b][16 * g:16 * g + 16], FP[j][part].rearrange("(h r) s -> r h s", r=16)), hd)
                        h_k6.append(hk6)
                for t in range(0, TB_, 2):
                    i, fr = bank()
                    for j in range(2):
                        for k in range(2):
                            h = mm(PS[:, i, D * j:D * j + D], xT4[:, k, P * (t + j):P * (t + j) + P], Wv4[:, k, :], k == 0, k == 1, [fr, hx4, h_we])
                    xt_rd = [h]
                    hV = dv(lambda e, i=i, t=t, b=b: e.tensor_tensor(V4[b][:, t:t + 2, :, 0:16], PS[:, i, :].rearrange("p (a h j) -> p a h j", a=2, h=16), bvb.rearrange("p (h j) -> p h j", h=16).unsqueeze(1).broadcast_to([P, 2, 16, 16]), ALU.add), h)
                    bank_free[i] = [hV]
            pr.barrier("e2")
            SBK, PBK, OBK = [(0, 1), (2, 3)], [4, 5, 6], 7
            s_fr, p_fr = [[], []], [[], [], []]
            h_oz = dv(lambda e: e.memset(PS[:, OBK, :], 0.0), pr.bar)
            p_at = [0]
            OT = Wall[:, 0:512]
            Pt = Pt + [xT4[:, 1, :]]
            sb_fr, pt_fr, ab_fr = [[], [], []], [[] for _ in range(4)], [[], []]
            q_fr = [[], []]
            h_q6, h_ab = {}, {}

            def get_q(m):
                b, t = m // TB_, m % TB_
                for g, part in enumerate((0, 0, 1, 0, 2, 1)):
                    h_q6[m] = dma("sp", s_q6[m % 2], lambda e, g=g, part=part, b=b, t=t, m=m: e.dma_start(
                        Q6[m % 2][16 * g:16 * g + 16], FP[2 * b][part].rearrange("(h r) s -> r h s", r=16)[:, :, P * t:P * t + P]), q_fr[m % 2], h_fp[2 * b])

            def bias(m):
                b, t = m // TB_, m % TB_
                A, T = Ab[m % 2], Tb
                c_ = CN[:, t, :]
                hh = op("pool", lambda e: e.tensor_scalar(A, c_, 1.0, None, ALU.max), ab_fr[m % 2])
                hh = op("act", lambda e: e.activation(A, A, ACT.Ln), hh)
                h2 = op("pool", lambda e: e.tensor_scalar(T, c_, 1.0, None, ALU.min), h_ab.get(m - 1))
                h2 = op("pool", lambda e: e.tensor_scalar(T, T, 1.0, -1e30, ALU.subtract, ALU.mult), h2)
                hh = op("pool", lambda e: e.tensor_tensor(A, T, A, ALU.subtract), h2, hh)
                hh = op("pool", lambda e: e.tensor_scalar(A, A, SP_[:, b:b + 1], None, ALU.mult), hh, h_u)
                h2 = op("pool", lambda e: e.tensor_scalar(T, PM[:, t, :], -1.0, 1.0, ALU.mult, ALU.add), hh)
                h2 = op("pool", lambda e: e.tensor_scalar(T, T, LD_[:, b:b + 1], None, ALU.mult), h2)
                h_ab[m] = op("pool", lambda e: e.tensor_tensor(A, A, T, ALU.add), h2)

            Tb = xT4[:, 0, :]
            Tb1 = X4T[1]
            Tb2 = K6[0].rearrange("p h s -> p (h s)").bitcast(F32)[:, 0:2 * S].rearrange("p (c s) -> p c s", c=2)
            items = [(m, h_) for m in range(B * TB_) for h_ in range(16)]
            st_ = {}
            get_q(0)
            get_q(1)
            bias(0)
            hx_prev = None

            def scores(z):
                m, h_ = items[z]
                b = m // TB_
                bk = SBK[z % 2]
                for n in range(2):
                    h = mm(PS[:, bk[n], :], Q6[m % 2][0:96, h_, :], K6[b][0:96, h_, 512 * n:512 * n + 512], True, True, [s_fr[z % 2], h_q6[m], h_k6[b]], inc=(n == 1))
                if h_ == 15:
                    q_fr[m % 2] = [h]
                    if m + 2 < B * TB_:
                        get_q(m + 2)
                ps = PS[:, bk[0]:bk[0] + 2, :].rearrange("p a s -> p (a s)")
                sbt, acc = Sb[z % 3], mr[:, z % 4:z % 4 + 1]
                h = dv(lambda e: e.tensor_tensor_reduce(sbt, ps, Ab[m % 2], 1.0, 3e38, ALU.add, ALU.min, acc), h, sb_fr[z % 3], h_ab[m], mr_rd.get(z - 4))
                s_fr[z % 2] = [h]
                if h_ == 15:
                    ab_fr[m % 2] = [h]
                h = op("act", lambda e: e.activation(sbt, sbt, ACT.Exp, bias=acc, scale=-1.0), h)
                mr_rd[z] = h
                st_[z] = h

            def turn(z):
                sbt, ptt = Sb[z % 3], Pt[z % 4]
                hs_ = []
                for g in range(2):
                    u = p_at[0] % 3
                    p_at[0] += 1
                    i = PBK[u]
                    for j in range(4):
                        k = 4 * g + j
                        h = op("pe", lambda e, i=i, j=j, k=k: e.transpose(PS[:, i, P * j:P * j + P], sbt[:, P * k:P * k + P], ident), p_fr[u], st_[z], inc=(j == 3))
                    eng = "dve" if (g == 0 and z % 8 != 7) else "act"
                    if eng == "dve":
                        h2 = dv(lambda e, i=i: e.tensor_copy(ptt[:, 0:512], PS[:, i, :]), h, pt_fr[z % 4])
                    else:
                        h2 = op("act", lambda e, i=i, g=g: e.copy(ptt[:, 512 * g:512 * g + 512], PS[:, i, :]), h, pt_fr[z % 4])
                    p_fr[u] = [h2]
                    hs_.append(h2)
                sb_fr[z % 3] = [h]
                st_[z] = hs_

            def values(z):
                nonlocal o_fr, ot_rd
                m, h_ = items[z]
                b, t = m // TB_, m % TB_
                g = h_ // 4
                for k in range(8):
                    for d in range(2):
                        r = 32 * ((h_ + d) % 4)
                        h = mm(PS[r:r + 17, OBK, P * g:P * g + P], V4[b][:, k, h_ + d, :], Pt[(z + d) % 4][:, P * k:P * k + P], k == 0, k == 7, [st_[z], st_[z + 1], o_fr[g]], inc=(k == 7 and d == 1))
                pt_fr[z % 4] = [h]
                pt_fr[(z + 1) % 4] = [h]
                if h_ % 4 == 2:
                    h = op("act", lambda e: e.copy(OT[:, P * g:P * g + P], PS[:, OBK, P * g:P * g + P]), h, ot_rd)
                    o_fr[g] = [h]
                    ot_h.append(h)
                if h_ == 14:
                    u = p_at[0] % 3
                    p_at[0] += 1
                    i = PBK[u]
                    for j in range(4):
                        h = op("pe", lambda e, j=j: e.transpose(PS[:, i, P * j:P * j + P], OT[:, P * j:P * j + P], ident), p_fr[u], ot_h[-4:], inc=(j == 3))
                    ot_rd = [h]
                    ov = PS[:, i, :].rearrange("p (h j) -> p h j", h=16)
                    h = dv(lambda e: e.reciprocal(rc, ov[:, :, 16]), h)
                    h = dv(lambda e: e.tensor_tensor(Oc[:, t, :].rearrange("p (h j) -> p h j", h=16), ov[:, :, 0:16], rc.unsqueeze(2).broadcast_to([P, 16, 16]), ALU.mult), h, oc_fr)
                    p_fr[u] = [h]
                    return h

            ot_rd, ot_h = [], []
            o_fr = [h_oz] * 4
            mr_rd = {}
            oc_fr = []
            hx4T = []
            NZ = len(items)
            for z in range(NZ + 4):
                if z < NZ:
                    if items[z][1] == 4 and items[z][0] + 1 < B * TB_:
                        bias(items[z][0] + 1)
                    scores(z)
                if 2 <= z < NZ + 2:
                    turn(z - 2)
                if z >= 4 and z % 2 == 0:
                    h = values(z - 4)
                    m, h_ = items[z - 4]
                    if h_ == 14 and m % TB_ == TB_ - 1:
                        b = m // TB_
                        Ot = (Tb2 if b else Tb1)
                        last = []
                        for g in range(2):
                            for c in range(2):
                                u = 2
                                i = 6
                                for j in range(4):
                                    t = 4 * g + j
                                    h2 = op("pe", lambda e, i=i, j=j, t=t, c=c: e.transpose(PS[:, i, P * j:P * j + P], Oc[:, t, P * c:P * c + P], ident), p_fr[2], h, inc=(j == 3))
                                h3 = op("act", lambda e, i=i, c=c, g=g, Ot=Ot: e.copy(Ot[:, c, 512 * g:512 * g + 512], PS[:, i, :]), h2)
                                p_fr[2] = [h3]
                                last.append(h3)
                        oc_fr = [h2]
                        for c in range(2):
                            for n in range(2):
                                for k in range(2):
                                    h2 = mm(PS[:, 6, :], Wo4[:, k, P * c:P * c + P], Ot[:, k, 512 * n:512 * n + 512], k == 0, k == 1, [p_fr[2], last])
                                h3 = op("act", lambda e, c=c, n=n, b=b: e.activation(X4T[b][:, c, 512 * n:512 * n + 512], PS[:, 6, :], ACT.Identity, bias=cv("bo", c)), h2)
                                p_fr[2] = [h3]
                                hx4T.append(h3)
            return X4T

        X4T = phase_e()
        pr.barrier("f")
        if dbg == "c2":
            hh = []
            for b in range(B):
                for t in range(TB_):
                    for c in range(2):
                        i, fr = bank()
                        h = op("pe", lambda e, i=i, t=t, c=c, b=b: e.transpose(PS[:, i, 0:P], X4T[b][:, c, P * t:P * t + P], ident), fr)
                        h = dv(lambda e, i=i, t=t, c=c, b=b: e.tensor_copy(X[:, TB_ * b + t, P * c:P * c + P], PS[:, i, 0:P]), h)
                        bank_free[i] = [h]
            return finish()

        def phase_f():
            arena.lo = base0
            fbar = pr.bar
            Wq5, Wk5, Wv5 = (arena.up(2 * FH).rearrange("p (c n) -> p c n", c=2) for _ in range(3))
            Wo5 = arena.up(8 * D).rearrange("p (f n) -> p f n", f=8)
            band = arena.up(768)
            gT = arena.up(B * 2 * 64).rearrange("p (b c g) -> p b c g", b=B, c=2)
            yT = [arena.up(8 * S).rearrange("p (f s) -> p f s", f=8) for _ in range(B)]
            q5, k5, v5 = ([arena.up(S) for _ in range(2)] for _ in range(3))
            sk = [arena.up(64) for _ in range(2)]
            sv = [arena.up(P) for _ in range(2)]
            Sb = [arena.up(449) for _ in range(3)]
            Se = [arena.up(321) for _ in range(2)]
            Pb = [arena.up(512) for _ in range(6)]
            Pt = [arena.up(512) for _ in range(4)]
            sm = arena.up(8)
            mr = arena.up(8)
            s_f = pr.new_sem("s_f")
            for w_, n_ in ((Wk5, "Wk"), (Wq5, "Wq"), (Wv5, "Wv")):
                load(s_f, w_, kmaj("L1_attn_" + n_), fbar)
            load(s_f, band, a["k_band"])
            h_w5 = load(s_f, Wo5, a["L1_attn_Wo"].rearrange("(f p) n -> p f n", f=8))
            hz = [op("pool", lambda e, z=z: e.memset(z, 0.0)) for z in Sb + Se + Pb + sv][-1]
            h_g = [dv(lambda e, b=b: e.tensor_reduce(gT[:, b], X4T[b].rearrange("p c (g l) -> p c g l", l=16), AX.X, ALU.add)) for b in range(B)]
            bfree = {i: [] for i in range(8)}
            units = [(b, f) for b in range(B) for f in range(8)]
            steps = [(u, t) for u in range(len(units)) for t in range(8)]
            u_rdy = [[] for _ in units]
            k_rd, v_rd, y_at = [[], []], [[], []], [[] for _ in range(B)]
            s_fr, se_fr = [[], [], []], [[], []]
            p_fr, pt_fr = [[] for _ in range(6)], [[] for _ in range(4)]
            state = {}

            def chunk(u, c, i=7):
                b, f = units[u]
                r, x_ = u % 2, X4T[b]
                fs = slice(P * f, P * f + P)
                if c < 4:
                    w_, dst, n = (Wk5, k5, c) if c < 2 else (Wq5, q5, c - 2)
                    for k in range(2):
                        h = mm(PS[:, i, :], w_[:, k, fs], x_[:, k, 512 * n:512 * n + 512], k == 0, k == 1, [bfree[i], h_w5])
                    o = dst[r][:, 512 * n:512 * n + 512]
                    if c < 2:
                        h = op("act", lambda e: e.copy(o, PS[:, i, :]), h, k_rd[r])
                    else:
                        h = dv(lambda e: e.tensor_scalar(o, PS[:, i, :], -0.125, None, ALU.mult), h, k_rd[r])
                elif c < 6:
                    for j in range(4):
                        t = 4 * (c - 4) + j
                        for k in range(2):
                            h = mm(PS[:, i, P * j:P * j + P], x_[:, k, P * t:P * t + P], Wv5[:, k, fs], k == 0, k == 1, [bfree[i]], inc=(j == 3 and k == 1))
                    o = v5[r][:, 512 * (c - 4):512 * (c - 4) + 512]
                    h = op("act", lambda e: e.copy(o, PS[:, i, :]), h, v_rd[r])
                elif c == 6:
                    for k in range(2):
                        h = mm(PS[:, i, 0:64], Wk5[:, k, fs], gT[:, b, k, :], k == 0, k == 1, [bfree[i], h_g])
                    h = dv(lambda e: e.tensor_copy(sk[r], PS[:, i, 0:64]), h, k_rd[r])
                else:
                    for k in range(2):
                        h = mm(PS[0:64, i, 0:P], gT[:, b, k, :], Wv5[:, k, fs], k == 0, k == 1, [bfree[i]])
                    h = dv(lambda e: e.tensor_copy(sv[r][0:64, :], PS[0:64, i, 0:P]), h, v_rd[r], hz)
                bfree[i] = [h]
                u_rdy[u].append(h)

            def geom(t):
                k0 = max(t - 1, 0)
                k1 = min(t + 2, 8)
                return k0, k1, P * (k1 - k0)

            def scores(z):
                u, t = steps[z]
                k0, k1, nk = geom(t)
                r = u % 2
                hs = []
                for d in range(2):
                    i = (2 * z + d) % 3
                    rows = slice(64 * d, 64 * d + 64)
                    q_ = q5[r][rows, P * t:P * t + P]
                    mm(PS[:, i, 0:nk], q_, k5[r][rows, P * k0:P * k1], True, True, [bfree[i], u_rdy[u]], inc=False)
                    hs.append(mm(PS[:, i, nk:nk + 64], q_, sk[r][rows, :], True, True))
                if t == 7:
                    k_rd[r] = [hs[-1]]
                w = nk + 64
                hx = []
                for d in range(2):
                    i, x, g = (2 * z + d) % 3, 2 * z + d, 2 * (z % 4) + d
                    if nk == 384:
                        sbt, frs, o, bnd = Sb[x % 3], s_fr, x % 3, band[:, 0:448]
                    else:
                        sbt, frs, o = Se[x % 2], se_fr, x % 2
                        bnd = band[:, 128:448] if t == 0 else band[:, 448:768]
                    pbt, acc, smc = Pb[x % 6], mr[:, g:g + 1], sm[:, g:g + 1]
                    h = dv(lambda e, i=i, sbt=sbt, bnd=bnd, acc=acc: e.tensor_tensor_reduce(sbt[:, 0:w], PS[:, i, 0:w], bnd, 1.0, 0.0, ALU.add, ALU.min, acc), hs[d], frs[o], hz, h_w5, state.get(("e", z - 4)))
                    bfree[i] = [h]
                    h = op("act", lambda e, sbt=sbt, pbt=pbt, acc=acc, smc=smc: e.activation(pbt[:, 0:w + 1], sbt[:, 0:w + 1], ACT.Exp, bias=acc, scale=-1.0, accum_out=smc), h, p_fr[x % 6], state.get(("d", z - 4)))
                    frs[o] = [h]
                    hx.append(h)
                state["e", z] = hx

            def scale(z):
                u, t = steps[z]
                w = geom(t)[2] + 64
                g = 2 * (z % 4)
                h = dv(lambda e: e.reciprocal(sm[:, g:g + 2], sm[:, g:g + 2]), state["e", z])
                hd = []
                for d in range(2):
                    pbt = Pb[(2 * z + d) % 6]
                    hd.append(op("pool", lambda e, pbt=pbt, d=d: e.tensor_scalar(pbt[:, 0:w], pbt[:, 0:w], sm[:, g + d:g + d + 1], 1.0, ALU.mult, ALU.mult), h))
                state["d", z] = hd

            def turn(z):
                u, t = steps[z]
                nj = geom(t)[2] // P + 1
                hs = []
                for d in range(2):
                    i, o = 3 + d, (2 * z + d) % 4
                    pbt, ptt = Pb[(2 * z + d) % 6], Pt[o]
                    for j in range(nj):
                        h = op("pe", lambda e, i=i, j=j, pbt=pbt: e.transpose(PS[:, i, P * j:P * j + P], pbt[:, P * j:P * j + P], ident), bfree[i], state["d", z][d], inc=(j == nj - 1))
                    p_fr[(2 * z + d) % 6] = [h]
                    if d:
                        h = dv(lambda e, i=i, ptt=ptt: e.tensor_copy(ptt[:, 0:P * nj], PS[:, i, 0:P * nj]), h, pt_fr[o])
                    else:
                        h = op("act", lambda e, i=i, ptt=ptt: e.copy(ptt[:, 0:P * nj], PS[:, i, 0:P * nj]), h, pt_fr[o])
                    bfree[i] = [h]
                    hs.append(h)
                state["t", z] = hs

            def values(z):
                u, t = steps[z]
                b, f = units[u]
                r = u % 2
                k0, k1, nk = geom(t)
                nj = k1 - k0 + 1
                n = z // 4
                i = 5 + n % 2
                for j in range(nj):
                    for d in range(2):
                        c = slice(64 * d, 64 * d + 64)
                        w_ = v5[r][:, P * (k0 + j):P * (k0 + j) + P][:, c] if j < nj - 1 else sv[r][:, c]
                        h = mm(PS[c, i, P * (t % 4):P * (t % 4) + P], w_, Pt[(2 * z + d) % 4][:, P * j:P * j + P], j == 0, j == nj - 1, [state["t", z], bfree[i] if t % 4 == 0 else None], inc=(j == nj - 1 and d == 1))
                pt_fr[(2 * z) % 4] = [h]
                pt_fr[(2 * z + 1) % 4] = [h]
                if t == 7:
                    v_rd[r] = [h]
                if t % 4 < 3:
                    return
                o = yT[b][:, f, 512 * (t // 4):512 * (t // 4) + 512]
                h = dv(lambda e: e.tensor_copy(o, PS[:, i, :]), h)
                bfree[i] = [h]
                y_at[b] = [h]

            def project(b, t, i=7):
                for k in range(8):
                    h = mm(PS[:, i, 0:D], yT[b][:, k, P * t:P * t + P], Wo5[:, k, :], k == 0, k == 7, [bfree[i], y_at[b]])
                xs = X[:, TB_ * b + t, :]
                h = dv(lambda e: e.tensor_tensor(xs, xs, PS[:, i, 0:D], ALU.add), h)
                bfree[i] = [h]

            for c in range(8):
                chunk(0, c, c)
            NZ = len(steps)
            for z in range(NZ + 2):
                if 1 <= z <= NZ:
                    scale(z - 1)
                if z < NZ:
                    scores(z)
                if z > 65 and z % 2 == 0 and z < 82:
                    project(0, (z - 66) // 2)
                if 2 <= z:
                    values(z - 2)
                if 1 <= z <= NZ:
                    turn(z - 1)
                if z < NZ and steps[z][0] + 1 < len(units):
                    chunk(steps[z][0] + 1, z % 8)
            for t in range(8):
                project(1, t, t)

        phase_f()
        pr.barrier("g")
        if dbg == "x2":
            return finish()

        def phase_g():
            arena.lo, arena.hi = base0, hi0
            gbar = pr.bar
            Wr7, Wk7, Wv7 = (arena.up(2 * D).rearrange("p (c n) -> p c n", c=2) for _ in range(3))
            s_h = pr.new_sem("s_h")
            for w_, n_ in ((Wr7, "r"), (Wk7, "k"), (Wv7, "v")):
                h_w7 = load(s_h, w_, kmaj("L1_ffn_W_" + n_), gbar)
            om = arena.up(4)
            for q, nm in enumerate(("mu_r", "mu_k")):
                i0 = CIDX[nm]
                h_om = dv(lambda e, q=q, i0=i0: e.tensor_scalar(om[:, 2 * q:2 * q + 2], cvec[:, i0:i0 + 2], -1.0, 1.0, ALU.mult, ALU.add))
            hT = [arena.up(2 * S).rearrange("p (c s) -> p c s", c=2) for _ in range(B)]
            xr, xk, ka = ([arena.up(2 * S).rearrange("p (c s) -> p c s", c=2) for _ in range(1)][0] for _ in range(3))
            R = arena.up(TB_ * D).rearrange("p (t c) -> p t c", t=TB_)
            wB = [adapter_space(64) for _ in range(B)]
            hc = []
            for b in range(B):
                hx = to_T(X[:, TB_ * b:TB_ * b + TB_, :], hT[b], [])
                hc.append(adapter("g", b, 64, 10, 4, "L1_cond2_W1", None, "L1_cond2_W2", "L1_cond2_b2", "gb1", hT[b], hT[b], [hx, gbar], wB[b]))
            prev = []
            for b in range(B):
                hh = []
                for q, (dst, nm) in enumerate(((xr, "mu_r"), (xk, "mu_k"))):
                    for c in range(2):
                        h = dv(lambda e, dst=dst, c=c, nm=nm, b=b: e.tensor_scalar(dst[:, c], hT[b][:, c], cv(nm, c), None, ALU.mult), hc[b], prev)
                        h = dv(lambda e, dst=dst, c=c, q=q, b=b: e.scalar_tensor_tensor(out=dst[:, c, 1:S], in0=hT[b][:, c, 0:S - 1], scalar=om[:, 2 * q + c:2 * q + c + 1], in1=dst[:, c, 1:S], op0=ALU.mult, op1=ALU.add), h, h_om)
                        hh.append(h)
                hk = []
                for c in range(2):
                    for n in range(2):
                        i, fr = bank()
                        for k in range(2):
                            h = mm(PS[:, i, :], Wk7[:, k, P * c:P * c + P], xk[:, k, 512 * n:512 * n + 512], k == 0, k == 1, [fr, hh, h_w7])
                        o = ka[:, c, 512 * n:512 * n + 512]
                        h = op("act", lambda e, i=i, o=o: e.activation(o, PS[:, i, :], ACT.Relu), h, prev)
                        bank_free[i] = [h]
                        hk.append(op("pool", lambda e, o=o: e.tensor_tensor(o, o, o, ALU.mult), h))
                hr = []
                for t in range(0, TB_, 2):
                    i, fr = bank()
                    for j in range(2):
                        for k in range(2):
                            h = mm(PS[:, i, D * j:D * j + D], xr[:, k, P * (t + j):P * (t + j) + P], Wr7[:, k, :], k == 0, k == 1, [fr, hh, h_w7])
                    h = op("act", lambda e, i=i, t=t: e.activation(R[:, t:t + 2, :], PS[:, i, :].rearrange("p (a c) -> p a c", a=2), ACT.Sigmoid), h, prev)
                    bank_free[i] = [h]
                    hr.append(h)
                for t in range(0, TB_, 2):
                    i, fr = bank()
                    for j in range(2):
                        for k in range(2):
                            h = mm(PS[:, i, D * j:D * j + D], ka[:, k, P * (t + j):P * (t + j) + P], Wv7[:, k, :], k == 0, k == 1, [fr, hk])
                    xs = X[:, TB_ * b + t:TB_ * b + t + 2, :]
                    h = dv(lambda e, i=i, t=t: e.tensor_tensor(R[:, t:t + 2, :], R[:, t:t + 2, :], PS[:, i, :].rearrange("p (a c) -> p a c", a=2), ALU.mult), h, hr[t // 2])
                    bank_free[i] = [h]
                    h = op("pool", lambda e, t=t, xs=xs: e.tensor_tensor(xs, xs, R[:, t:t + 2, :], ALU.add), h)
                prev = [(pr.sem[e], pr.n[pr.sem[e]]) for e in ("pe", "act", "dve", "pool")]

        phase_g()
        finish()


def layouts(i):
    f = {k: np.asarray(v) for k, v in i.items()}
    a = {}
    a["x"] = f["x"].reshape(N, D)
    a["xT"] = f["x"].reshape(N, D).T
    a["ids"] = np.concatenate([f["itok_B_0_6"], f["itok_B_0_7"], f["itok_B_0_8"]]).reshape(1, 6)
    a["u"] = f["condB_uprev"].reshape(1, B)
    a["idx"] = f["itok_Sx32_0_1023"]
    a["imask"] = f["mask_Sx32_bk1"]
    a["pmask"] = f["mask_SxS_bk0"]

    def col(v):
        return v.reshape(-1, P).T

    vecs = {"maa_x": "L0_attn_time_maa_x", "maa_w": "L0_attn_time_maa_w", "maa_k": "L0_attn_time_maa_k",
            "maa_v": "L0_attn_time_maa_v", "maa_r": "L0_attn_time_maa_r", "decay": "L0_attn_time_decay",
            "faaaa": "L0_attn_time_faaaa", "ln_w": "L0_attn_ln_w", "ln_b": "L0_attn_ln_b",
            "bq": "L1_cond_bq", "bk": "L1_cond_bk", "mu_r": "L1_ffn_mu_r", "mu_k": "L1_ffn_mu_k", "bo": "L1_cond_bo"}
    a["cvec"] = np.concatenate([col(f[vecs[n]].reshape(-1)) for n in CV]
                               + [col(f["L0_cond2_b1"]), col(f["L0_ffn_b1"].reshape(-1))], axis=1)

    def gb(g, b, bd):
        e = g.shape[0]
        pad = np.zeros((e, P, 1), np.float32)
        pad[:, :bd.shape[1], 0] = bd
        return np.concatenate([g.reshape(e, 2, P).transpose(0, 2, 1), b.reshape(e, 2, P).transpose(0, 2, 1), pad], axis=2)

    a["gb0"] = gb(f["L0_cond_ln_g"], f["L0_cond_ln_b"], f["L0_cond_down_b"])
    a["gb1"] = gb(f["L1_cond2_gamma"], f["L1_cond2_beta"], f["L1_cond2_b1"])
    for n in ("L0_cond_down_w", "L0_cond_up_w", "L0_cond_up_b", "L0_attn_time_maa_w1", "L0_attn_time_decay_w1",
              "L0_attn_time_decay_w2", "L0_attn_W_r", "L0_attn_W_k", "L0_attn_W_v", "L0_attn_W_o",
              "L0_cond2_W1", "L0_cond2_W2", "L0_cond2_b2", "L0_cond2_We", "L0_cond2_be", "L0_ffn_Wg",
              "L0_ffn_W1", "L0_ffn_W2", "L0_ffn_b2", "L1_cond_bv", "L1_cond2_W1",
              "L1_cond2_W2", "L1_cond2_b2"):
        a[n] = f[n]
    a["L0_attn_time_maa_w2"] = f["L0_attn_time_maa_w2"].reshape(P, D)
    for n in ("Wq", "Wk", "Wv", "Wo"):
        a["L1_cond_" + n] = f["L1_cond_" + n].T
        w = f["L1_attn_" + n]
        a["L1_attn_" + n] = w.reshape(1024, 256) if n == "Wo" else w.reshape(256, 1024)
    for n in ("W_r", "W_k", "W_v"):
        a["L1_ffn_" + n] = f["L1_ffn_" + n].T
    i = np.arange(P)
    a["k_ident"] = np.eye(P, dtype=np.float32)
    a["k_headb"] = (i[:, None] // 64 == i[None, :] // 64).astype(np.float32)
    a["k_triu"] = (i[:, None] <= i[None, :]).astype(np.float32)
    NEG = np.float32(-1e9)
    z = np.zeros((P, P), np.float32)
    prev = np.where(i[None, :] > i[:, None], np.float32(0), -NEG)
    nxt = np.where(i[None, :] < i[:, None], np.float32(0), -NEG)
    a["k_band"] = np.concatenate([prev, z, nxt, z[:, :64], prev, z, z[:, :64]], axis=1).astype(np.float32)
    a["k_iota"] = np.broadcast_to(np.arange(S, dtype=np.float32), (P, S))
    a["k_slot"] = np.concatenate([np.broadcast_to(np.arange(8, dtype=np.float32), (P, 8)),
                                  np.arange(N, dtype=np.float32).reshape(NT, P).T + E * CAP], axis=1)
    return {k: np.ascontiguousarray(v) for k, v in a.items()}


def kernel(**inputs):
    import concourse.bacc as _bacc
    from concourse.bass_utils import run_bass_kernel_spmd as _run

    nc = _bacc.Bacc("TRN2", target_bir_lowering=False, num_devices=1)
    arrays, aps = {}, {}
    for name, v in layouts(inputs).items():
        arrays[f"in_{name}"] = v
        aps[name] = nc.dram_tensor(f"in_{name}", v.shape, mybir.dt.from_np(v.dtype), kind="ExternalInput").ap()
    out = nc.dram_tensor("out_0", (N, D), F32, kind="ExternalOutput").ap()
    build(nc, aps, out)
    r = _run(nc, [arrays], core_ids=[0])
    return r.results[0]["out_0"].reshape(B, S, D)
```

```python
from contextlib import ExitStack

import numpy as np

import concourse.bass as bass
from concourse import mybir

F32 = mybir.dt.float32
BF16 = mybir.dt.bfloat16
I32 = mybir.dt.int32
U32 = mybir.dt.uint32
U8 = mybir.dt.uint8
ALU = mybir.AluOpType
ACT = mybir.ActivationFunctionType
AX = mybir.AxisListType

P = 128
B = 2
S = 1024
D = 256
N = B * S
NT = N // P
TB_ = S // P
E = 8
FH = 1024
CAP = 512
ENG = ("pe", "act", "dve", "pool", "sp")


class Prog:

    def __init__(self, nc, ctx):
        self.nc, self.ctx = nc, ctx
        self.q = {e: [] for e in ENG}
        self.n = {}
        self.seen = {e: {} for e in ENG}
        self.sem = {}
        self.k = 0
        self.bar = []
        self.phase("p0")

    def new_sem(self, name):
        self.k += 1
        s = self.ctx.enter_context(self.nc.semaphore(f"{name}_{self.k}"))
        self.n[s] = 0
        return s

    def phase(self, name):
        for e in ("pe", "act", "dve", "pool"):
            self.sem[e] = self.new_sem(f"{name}_{e}")

    def wait(self, e, *hs):
        for h in hs:
            if h is None:
                continue
            if isinstance(h, list):
                self.wait(e, *h)
                continue
            s, v = h
            if self.seen[e].get(s, 0) < v:
                self.seen[e][s] = v
                self.q[e].append(lambda eng, s=s, v=v: eng.wait_ge(s, v))

    def op(self, e, fn, *waits, inc=True):
        self.wait(e, *waits)
        if not inc:
            self.q[e].append(lambda eng: fn(eng))
            return None
        s = self.sem[e]
        self.n[s] += 1
        self.q[e].append(lambda eng, s=s: fn(eng).then_inc(s, 1))
        return (s, self.n[s])

    def dma(self, e, sem, fn, *waits):
        self.wait(e, *waits)
        self.n[sem] += 16
        self.q[e].append(lambda eng, s=sem: fn(eng).then_inc(s, 16))
        return (sem, self.n[sem])

    def barrier(self, name):
        last = [(self.sem[e], self.n[self.sem[e]]) for e in ("pe", "act", "dve", "pool")]
        last = [h for h in last if h[1]]
        self.bar = last
        for e in ("pe", "act", "dve", "pool"):
            self.wait(e, *last)
        self.phase(name)
        return last


class Arena:

    def __init__(self, t, size):
        self.t, self.size, self.lo, self.hi = t, size, 0, size

    def up(self, n, dt=F32):
        a, self.lo = self.lo, self.lo + n
        assert self.lo <= self.hi, (self.lo, self.hi)
        v = self.t[:, a:a + n]
        return v if dt == F32 else v.bitcast(dt)

    def down(self, n):
        self.hi -= n
        assert self.lo <= self.hi, (self.lo, self.hi)
        return self.t[:, self.hi:self.hi + n]


CV = ["maa_x", "maa_w", "maa_k", "maa_v", "maa_r", "decay", "faaaa", "ln_w", "ln_b", "bq", "bk", "mu_r", "mu_k", "bo"]
CIDX = {n: 2 * i for i, n in enumerate(CV)}
CB1 = 2 * len(CV)
NCV = CB1 + 8 + 64


def build(nc, a, out, dbg=None):
    with ExitStack() as ctx:
        pr = Prog(nc, ctx)
        op, dma = pr.op, pr.dma
        WORDS = 52600
        arena = Arena(ctx.enter_context(nc.sbuf_tensor("arena", [P, WORDS], F32)), WORDS)
        PS = ctx.enter_context(nc.psum_tensor("PS", [P, 8, 512], F32))
        bank_free = [[] for _ in range(8)]
        bank_at = [0]

        def bank():
            i = bank_at[0]
            bank_at[0] = (i + 1) % 8
            return i, bank_free[i]

        def mm(out_, lhsT, rhs, start, stop, waits=(), inc=None):
            return op("pe", lambda e: e.matmul(out_, lhsT, rhs, start=start, stop=stop), *waits,
                      inc=stop if inc is None else inc)

        ident = arena.up(P)
        headb = arena.up(P)
        triu = arena.up(P)
        onesm = arena.up(P)
        cvec = arena.up(NCV)
        X = arena.up(NT * D).rearrange("p (t c) -> p t c", t=NT)
        s_c = pr.new_sem("s_c")
        h_cst = [dma("sp", s_c, lambda e: e.dma_start(ident, a["k_ident"])),
                 dma("sp", s_c, lambda e: e.dma_start(cvec, a["cvec"])),
                 dma("sp", s_c, lambda e: e.dma_start(headb, a["k_headb"])),
                 dma("sp", s_c, lambda e: e.dma_start(triu, a["k_triu"]))][-1]

        def cv(name, c):
            i = CIDX[name] + c
            return cvec[:, i:i + 1]

        kslot = arena.up(24)
        dma("sp", s_c, lambda e: e.dma_start(kslot, a["k_slot"]))
        ids = arena.up(8).bitcast(I32)
        h_ids = dma("sp", s_c, lambda e: e.dma_start(ids[0:1, 0:6], a["ids"]))
        h_cst = h_ids
        h_ones = op("pool", lambda e: e.memset(onesm, 1.0))
        regs = {}

        def load_id(i, n):
            def f(e):
                regs[i] = e.value_load(ids[0:1, i:i + 1], min_val=0, max_val=n - 1)
            pr.wait("sp", h_ids)
            pr.q["sp"].append(f)

        def load(sem, dst, src, *waits):
            return dma("sp", sem, lambda e: e.dma_start(dst, src), *waits)

        def load_by(sem, dst, src_of, i, *waits):
            return dma("sp", sem, lambda e: e.dma_start(dst, src_of(regs[i])), *waits)

        def kmaj(name, c=2):
            return a[name].rearrange("(c p) n -> p c n", c=c)

        base0 = arena.lo
        Xg = nc.dram_tensor("xg", (2 * E * CAP, D), F32, kind="Internal").ap()
        Ye = nc.dram_tensor("ye", (E * CAP, D), F32, kind="Internal").ap()
        s_x = pr.new_sem("s_x")

        def adapter(tag, bi, K, n_ids, idx0, down, down_b, up, up_b, gb, srcT, dstT, waits, wb):
            sem = pr.new_sem("s_ad")
            wd, wu, small, bub, zT, xb, y, st = wb
            load_id(idx0 + bi, n_ids)
            load_by(sem, wd, lambda r: a[down].rearrange("e (c p) k -> e p c k", c=2)[bass.ds(r, 1)].rearrange("e p c k -> (e p) c k"), idx0 + bi, *waits)
            load_by(sem, wu[0:K], lambda r: a[up][bass.ds(r, 1)].rearrange("e k h -> (e k) h"), idx0 + bi)
            load_by(sem, small, lambda r: a[gb][bass.ds(r, 1)].rearrange("e p c -> (e p) c"), idx0 + bi)
            h_w = load_by(sem, bub, lambda r: a[up_b][bass.ds(r, 1)].rearrange("e h -> (e h)").partition_broadcast(P), idx0 + bi)
            xs = X[:, TB_ * bi:TB_ * bi + TB_, :]
            h_xb = op("pool", lambda e: e.tensor_tensor(xb, xs, bub.unsqueeze(1).broadcast_to([P, TB_, D]), ALU.add), h_w, *waits)
            hz = []
            yield
            for n in range(2):
                i, fr = bank()
                for c in range(2):
                    h = mm(PS[0:K, i, :], wd[:, c, :], srcT[:, c, 512 * n:512 * n + 512], c == 0, c == 1, [h_w, fr, waits])
                h = op("act", lambda e, i=i, n=n: e.activation(zT[0:K, 512 * n:512 * n + 512], PS[0:K, i, :], ACT.Relu, bias=small[0:K, 4:5]), h)
                bank_free[i] = [h]
                hz.append(h)
                yield
            hy = []
            for t in range(TB_):
                i, fr = bank()
                h = mm(PS[:, i, 0:D], zT[0:K, P * t:P * t + P], wu[0:K, :], True, True, [hz[t // 4], fr])
                h = op("dve", lambda e, i=i, t=t: e.tensor_tensor(y[:, t, :], PS[:, i, 0:D], xb[:, t, :], ALU.add), h, h_xb)
                bank_free[i] = [h]
                h = op("dve", lambda e, t=t: e.bn_stats(st[:, 6 * t:6 * t + 6], y[:, t, :]), h)
                hy.append(h)
                yield
            mv = st[:, 48:64].rearrange("p (t k) -> p t k", k=2)
            for t in range(TB_):
                h = op("dve", lambda e, t=t: e.bn_aggr(mv[:, t, :], st[:, 6 * t:6 * t + 6]), hy[t])
            h = op("dve", lambda e: e.tensor_scalar(st[:, 64:72], mv[:, :, 1], 1e-5, None, ALU.add), h)
            yield
            h = op("act", lambda e: e.activation(st[:, 72:80], st[:, 64:72], ACT.Sqrt), h)
            h = op("dve", lambda e: e.reciprocal(st[:, 80:88], st[:, 72:80]), h)
            hn = []
            for t in range(TB_):
                h2 = op("dve", lambda e, t=t: e.tensor_scalar(y[:, t, :], y[:, t, :], mv[:, t, 0:1], st[:, 80 + t:81 + t], ALU.subtract, ALU.mult), h)
                hn.append(h2)
            yield
            last = []
            for c in range(2):
                for g in range(2):
                    i, fr = bank()
                    for j in range(4):
                        t = 4 * g + j
                        h = op("pe", lambda e, i=i, j=j, t=t, c=c: e.transpose(PS[:, i, P * j:P * j + P], y[:, t, P * c:P * c + P], ident), hn[t], fr, h_cst, inc=(j == 3))
                    h = op("act", lambda e, i=i, c=c, g=g: e.activation(dstT[:, c, 512 * g:512 * g + 512], PS[:, i, :], ACT.Identity, bias=small[:, 2 + c:3 + c], scale=small[:, c:c + 1]), h)
                    bank_free[i] = [h]
                    last.append(h)
                    yield
            yield last

        def in_turns(gens):
            out_ = [None] * len(gens)
            live = list(range(len(gens)))
            while live:
                for g in list(live):
                    v = next(gens[g], "end")
                    if v == "end":
                        live.remove(g)
                    else:
                        out_[g] = v
            return out_

        def adapter_space(K):
            return (arena.up(2 * K).rearrange("p (c k) -> p c k", c=2), arena.up(D), arena.up(8)[:, 0:5], arena.up(D),
                    arena.up(S), arena.up(TB_ * D).rearrange("p (t c) -> p t c", t=TB_),
                    arena.up(TB_ * D).rearrange("p (t c) -> p t c", t=TB_), arena.up(96))

        def to_T(src, dst, waits, eng="act"):
            last = []
            for g in range(2):
                for c in range(2):
                    i, fr = bank()
                    for j in range(4):
                        t = 4 * g + j
                        h = op("pe", lambda e, i=i, j=j, t=t, c=c: e.transpose(PS[:, i, P * j:P * j + P], src[:, t, P * c:P * c + P], ident), fr, waits, inc=(j == 3))
                    if eng == "act":
                        h = op("act", lambda e, i=i, c=c, g=g: e.copy(dst[:, c, 512 * g:512 * g + 512], PS[:, i, :]), h)
                    else:
                        h = op("dve", lambda e, i=i, c=c, g=g: e.tensor_copy(dst[:, c, 512 * g:512 * g + 512], PS[:, i, :]), h)
                    bank_free[i] = [h]
                    last.append(h)
            return last

        def finish():
            last = [(pr.sem[e], pr.n[pr.sem[e]]) for e in ("pe", "act", "dve", "pool") if pr.n[pr.sem[e]]] or pr.bar
            s_o = pr.new_sem("s_o")
            for b in range(B):
                h = dma("sp", s_o, lambda e, b=b: e.dma_start(out.rearrange("(t p) c -> p t c", p=P)[:, TB_ * b:TB_ * b + TB_, :], X[:, TB_ * b:TB_ * b + TB_, :]), last)
            pr.wait("sp", h)
            with nc.Block() as block:
                for name, eng in (("sync", "sp"), ("tensor", "pe"), ("scalar", "act"), ("vector", "dve"), ("gpsimd", "pool")):
                    def run(e, items=pr.q[eng]):
                        for it in items:
                            it(e)
                    {"sync": block.sync, "tensor": block.tensor, "scalar": block.scalar, "vector": block.vector, "gpsimd": block.gpsimd}[name](run)

        hi0 = arena.hi
        W1c = arena.down(2 * FH).rearrange("p (c n) -> p c n", c=2)
        Wc = [arena.down(8 * D).rearrange("p (f n) -> p f n", f=8) for _ in range(B)]
        bc = [arena.down(D) for _ in range(B)]
        Wg = arena.down(16).rearrange("p (c n) -> p c n", c=2)
        mark = arena.lo
        w1 = arena.up(2 * P).rearrange("p (c n) -> p c n", c=2)
        w2 = arena.up(D)
        dw1 = arena.up(2 * 64).rearrange("p (c n) -> p c n", c=2)
        dw2 = arena.up(D)
        Wr, Wk, Wv, Wo = (arena.up(2 * D).rearrange("p (c n) -> p c n", c=2) for _ in range(4))
        hT2 = [arena.up(2 * S).rearrange("p (c s) -> p c s", c=2) for _ in range(B)]
        mark2 = arena.lo
        s_w = pr.new_sem("s_w")
        for b in range(B):
            h_x = load(s_x, hT2[b], a["xT"].rearrange("(c p) n -> p c n", c=2)[:, :, S * b:S * b + S])
            h_x = load(s_x, X[:, TB_ * b:TB_ * b + TB_, :], a["x"].rearrange("(t p) c -> p t c", p=P)[:, TB_ * b:TB_ * b + TB_, :])
        wA = [adapter_space(P) for _ in range(B)]
        in_turns([adapter("a", b, P, 8, 0, "L0_cond_down_w", None, "L0_cond_up_w", "L0_cond_up_b", "gb0", hT2[b], hT2[b], [h_x], wA[b]) for b in range(B)])
        load(s_w, w1, kmaj("L0_attn_time_maa_w1"))
        load(s_w, w2, a["L0_attn_time_maa_w2"])
        load(s_w, dw1, kmaj("L0_attn_time_decay_w1"))
        load(s_w, dw2[0:64], a["L0_attn_time_decay_w2"])
        for w_, n_ in ((Wr, "r"), (Wk, "k"), (Wv, "v"), (Wo, "o")):
            h_w = load(s_w, w_, kmaj("L0_attn_W_" + n_))
        s_wc = pr.new_sem("s_wc")
        load(s_wc, W1c, kmaj("L0_cond2_W1"))
        for b in range(B):
            load_id(2 + b, E)
            load(s_wc, Wc[b][:, :, 0:192], a["L0_cond2_W2"].rearrange("(f p) n -> p f n", f=8))
            load_by(s_wc, Wc[b][:, :, 192:256], lambda r: a["L0_cond2_We"].rearrange("e (f p) n -> e p f n", f=8)[bass.ds(r, 1)].rearrange("e p f n -> (e p) f n"), 2 + b)
            load(s_wc, bc[b][:, 0:192], a["L0_cond2_b2"].partition_broadcast(P))
            load_by(s_wc, bc[b][:, 192:256], lambda r: a["L0_cond2_be"][bass.ds(r, 1)].rearrange("e n -> (e n)").partition_broadcast(P), 2 + b)
        h_wc = load(s_wc, Wg, kmaj("L0_ffn_Wg"))
        pr.barrier("b")
        arena.lo = mark2

        def full():
            return arena.up(2 * S).rearrange("p (c s) -> p c s", c=2)

        xx, tmp, xf = full(), full(), full()
        rT, kT, vT, wT, yl = full(), full(), full(), full(), full()
        vtok = arena.up(TB_ * D).rearrange("p (t c) -> p t c", t=TB_)
        mT = arena.up(S)
        Gb = tmp
        rg = xx
        tpb = arena.up(2048)
        tp2 = [tpb[:, 512 * j:512 * j + 512] for j in range(4)]
        tp_free = [[] for _ in range(4)]
        KR, RR = full(), full()
        rp = full()
        Wb = arena.up(P)
        PB = arena.up(P)
        TD = arena.up(16).rearrange("p (c n) -> p c n", c=2)
        KD = [arena.up(S) for _ in range(2)]
        ATb = arena.up(14 * P)

        def flat(z):
            return z.rearrange("p c s -> p (c s)")

        RP2 = [flat(z).rearrange("p (n a h l) -> p n a h l", n=8, a=8, h=2) for z in (kT, wT)]
        AS = flat(tmp)[:, 0:14 * P].rearrange("p (q m k) -> p q m k", q=7, m=2)
        TT = [z.rearrange("p (q m n h l) -> p q m n h l", q=7, m=2, n=4, h=2) for z in (ATb, flat(rT)[:, 0:14 * P])]
        SD = [flat(xx)[:, S * j:S * j + S].rearrange("p (n j) -> p n j", n=8) for j in range(2)]
        KEs = [mT, tpb[:, 0:S]]
        St = arena.up(2 * 9 * 64).rearrange("p (c n j) -> p c n j", c=2, n=9)
        ytok, rpp = xf.rearrange("p c s -> p (c s)").rearrange("p (t c) -> p t c", t=TB_), RR
        st = arena.up(6 * 32 + 2 * 32 + 96)
        h0b = None

        hprev = []
        for b in range(B):
            hT = hT2[b]
            h1 = op("dve", lambda e, hT=hT: e.tensor_tensor(xx[:, :, 1:S], hT[:, :, 0:S - 1], hT[:, :, 1:S], ALU.subtract), hprev)
            h2 = op("dve", lambda e, hT=hT: e.tensor_scalar(xx[:, :, 0:1], hT[:, :, 0:1], -1.0, None, ALU.mult))
            hx = []
            for c in range(2):
                hx.append(op("dve", lambda e, c=c, hT=hT: e.scalar_tensor_tensor(out=tmp[:, c], in0=xx[:, c], scalar=cv("maa_x", c), in1=hT[:, c], op0=ALU.mult, op1=ALU.add), h1, h2, h_cst))
            hm = []
            for n in range(2):
                i, fr = bank()
                for c in range(2):
                    h = mm(PS[:, i, :], w1[:, c, :], tmp[:, c, 512 * n:512 * n + 512], c == 0, c == 1, [h_w, fr, hx])
                h = op("act", lambda e, i=i, n=n: e.activation(mT[:, 512 * n:512 * n + 512], PS[:, i, :], ACT.Tanh), h)
                bank_free[i] = [h]
                hm.append(h)
            hxf_rd = [hx]
            bufs = [tmp, xf]
            rd = [[hm], [hprev]]
            ek = {}
            for q, (f, nm) in enumerate(((0, "w"), (1, "k"), (2, "v"), (3, "r"))):
                dst = bufs[q % 2]
                hf = []
                for c in range(2):
                    for n in range(2):
                        i, fr = bank()
                        sl = slice(512 * n, 512 * n + 512)
                        h = mm(PS[:, i, :], w2[32 * f:32 * f + 32, P * c:P * c + P], mT[32 * f:32 * f + 32, sl], True, True, [fr, hm])
                        h = op("dve", lambda e, i=i, c=c, sl=sl, dst=dst, nm=nm: e.scalar_tensor_tensor(out=dst[:, c, sl], in0=PS[:, i, :], scalar=cv("maa_" + nm, c), in1=xx[:, c, sl], op0=ALU.add, op1=ALU.mult), h, rd[q % 2])
                        bank_free[i] = [h]
                        h = op("pool", lambda e, c=c, sl=sl, dst=dst, hT=hT: e.tensor_tensor(dst[:, c, sl], dst[:, c, sl], hT[:, c, sl], ALU.add), h)
                        hf.append(h)
                if nm == "w":
                    hw2 = []
                    for n in range(2):
                        sl = slice(512 * n, 512 * n + 512)
                        i, fr = bank()
                        for c in range(2):
                            h = mm(PS[0:64, i, :], dw1[:, c, :], dst[:, c, sl], c == 0, c == 1, [fr, hf])
                        h = op("act", lambda e, i=i, sl=sl: e.activation(yl[0:64, 0, sl], PS[0:64, i, :], ACT.Tanh), h, hprev)
                        bank_free[i] = [h]
                        hw2.append(h)
                    rd[q % 2] = [hw2]
                    hw = []
                    for c in range(2):
                        for n in range(2):
                            sl = slice(512 * n, 512 * n + 512)
                            i, fr = bank()
                            h = mm(PS[:, i, :], dw2[0:64, P * c:P * c + P], yl[0:64, 0, sl], True, True, [fr, hw2[n]])
                            h = op("act", lambda e, i=i, c=c, sl=sl: e.activation(wT[:, c, sl], PS[:, i, :], ACT.Exp, bias=cv("decay", c)), h)
                            bank_free[i] = [h]
                            h = op("act", lambda e, c=c, sl=sl: e.activation(wT[:, c, sl], wT[:, c, sl], ACT.Exp, scale=-1.0), h)
                            hw.append(h)
                    continue
                Wm = {"k": Wk, "v": Wv, "r": Wr}[nm]
                dT = {"k": kT, "v": vT, "r": rT}[nm]
                hh = []
                for c in range(2):
                    for n in range(2):
                        sl = slice(512 * n, 512 * n + 512)
                        i, fr = bank()
                        for k in range(2):
                            h = mm(PS[:, i, :], Wm[:, k, P * c:P * c + P], dst[:, k, sl], k == 0, k == 1, [fr, hf])
                        h = op("act", lambda e, i=i, c=c, sl=sl, dT=dT: e.copy(dT[:, c, sl], PS[:, i, :]), h, hprev)
                        bank_free[i] = [h]
                        hh.append(h)
                if nm == "v":
                    for t in range(0, TB_, 2):
                        i, fr = bank()
                        for j in range(2):
                            for k in range(2):
                                h = mm(PS[:, i, D * j:D * j + D], dst[:, k, P * (t + j):P * (t + j) + P], Wm[:, k, :], k == 0, k == 1, [fr, hf])
                        h = op("act", lambda e, i=i, t=t: e.copy(vtok[:, t:t + 2, :], PS[:, i, :].rearrange("p (a c) -> p a c", a=2)), h, hprev)
                        bank_free[i] = [h]
                        hh.append(h)
                rd[q % 2] = [hh]
                ek[nm] = hh
            hk, hv, hr = ek["k"], ek["v"], ek["r"]
            w4, r4, k4, v4 = (z.rearrange("p c (m l) -> p (c m) l", l=16) for z in (wT, rT, kT, vT))
            KR4, RR4, rp4 = (z.rearrange("p c (m l) -> p (c m) l", l=16) for z in (KR, RR, rp))
            h = op("dve", lambda e: e.memset(RR4[:, :, 0:1], 1.0), hprev)
            hR = op("pool", lambda e: e.memset(KR4[:, :, 15:16], 1.0), hprev)
            for j in range(1, 16):
                h = op("dve", lambda e, j=j: e.tensor_tensor(RR4[:, :, j:j + 1], RR4[:, :, j - 1:j], w4[:, :, j - 1:j], ALU.mult), h, hw)
                hR = op("pool", lambda e, j=j: e.tensor_tensor(KR4[:, :, 15 - j:16 - j], KR4[:, :, 16 - j:17 - j], w4[:, :, 16 - j:17 - j], ALU.mult), hR, hw)
            hWb = op("dve", lambda e: e.tensor_tensor(Wb.unsqueeze(2), RR4[:, :, 15:16], w4[:, :, 15:16], ALU.mult), h)
            hKR = op("pool", lambda e: e.tensor_tensor(KR, KR, kT, ALU.mult), hR, hk)
            hrp = op("dve", lambda e: e.tensor_tensor(rp, RR, rT, ALU.mult), h, hr)
            Wb4 = Wb.rearrange("p (c n a) -> p c n a", c=2, a=8)
            PB4 = PB.rearrange("p (c n a) -> p c n a", c=2, a=8)
            h = op("dve", lambda e: e.memset(PB4[:, :, :, 0:1], 1.0), hprev)
            for j in range(1, 8):
                h = op("dve", lambda e, j=j: e.tensor_tensor(PB4[:, :, :, j:j + 1], PB4[:, :, :, j - 1:j], Wb4[:, :, :, j - 1:j], ALU.mult), h, hWb)
            hTD = op("dve", lambda e: e.tensor_tensor(TD.unsqueeze(3), PB4[:, :, :, 7:8], Wb4[:, :, :, 7:8], ALU.mult), h)
            hrpp = op("dve", lambda e: e.tensor_tensor(RR4, rp4, PB.unsqueeze(2).broadcast_to([P, P, 16]), ALU.mult), h, hrp)

            hG = op("act", lambda e: e.copy(Gb, kT), hk, rd[0], rd[1])
            for c in range(2):
                hrg = op("dve", lambda e, c=c: e.scalar_tensor_tensor(out=rg[:, c], in0=rT[:, c], scalar=cv("faaaa", c), in1=kT[:, c], op0=ALU.mult, op1=ALU.mult), hr, hk, hf)
            rp5 = rp.rearrange("p c (n a l) -> p c n a l", n=8, a=8)

            def spread(c, eng, waits):
                h = op(eng, lambda e: e.memset(RP2[c], 0.0), waits)
                hs_ = []
                for hh_ in range(2):
                    rows = slice(64 * hh_, 64 * hh_ + 64)
                    hs_.append(op("act", lambda e, rows=rows, hh_=hh_: e.copy(RP2[c][rows, :, :, hh_, :], rp5[rows, c]), h, hrp))
                return hs_

            G4, y4 = (z.rearrange("p c (m l) -> p (c m) l", l=16) for z in (Gb, yl))
            rg4 = [z.rearrange("p c (m l) -> p (c m) l", l=16) for z in (rg, kT)]
            hyl = [None] * 4
            hG = [hG, hKR]
            rg_rd = [[], hrg]
            pv_ = {}
            for dl in range(17):
                L = 16 - dl
                if dl < 16:
                    dst = rg4[dl % 2]
                    if dl:
                        hrg = [op(eng, lambda e, ms=ms, dl=dl, L=L, dst=dst: e.tensor_tensor(dst[:, ms, 0:L], r4[:, ms, dl:16], G4[:, ms, 0:L], ALU.mult), hG, rg_rd[dl % 2])
                               for eng, ms in (("pool", slice(96, 128)), ("dve", slice(0, 96)))]
                        if dl < 15:
                            hG = op("dve", lambda e, dl=dl, L=L: e.tensor_tensor(G4[:, :, 0:L - 1], G4[:, :, 0:L - 1], w4[:, :, dl:15], ALU.mult), hrg, hw)
                    for g in range(4):
                        i, fr = bank()
                        ms = slice(32 * g, 32 * g + 32)
                        h = mm(PS[:, i, 0:32 * L], headb, dst[:, ms, 0:L], True, True, [fr, hrg, h_cst])
                        pv_[dl, g] = (i, h)
                    rg_rd[dl % 2] = [h]
                if dl == 0:
                    continue
                dp, L = dl - 1, L + 1
                for g in range(4):
                    i, h = pv_.pop((dp, g))
                    ms = slice(32 * g, 32 * g + 32)
                    pv = PS[:, i, 0:32 * L].rearrange("p (m l) -> p m l", l=L)
                    if dp == 0:
                        h = op("dve", lambda e, pv=pv, ms=ms: e.tensor_tensor(y4[:, ms, :], pv, v4[:, ms, :], ALU.mult), h, hv, hw)
                        bank_free[i] = [h]
                        hyl[g] = h
                        continue
                    tb = tp2[g][:, 0:32 * L].rearrange("p (m l) -> p m l", l=L)
                    h = op("dve", lambda e, pv=pv, ms=ms, tb=tb, L=L: e.tensor_tensor(tb, pv, v4[:, ms, 0:L], ALU.mult), h, tp_free[g])
                    bank_free[i] = [h]
                    h = op("pool", lambda e, ms=ms, tb=tb, dp=dp: e.tensor_tensor(y4[:, ms, dp:16], y4[:, ms, dp:16], tb, ALU.add), h, hyl[g])
                    hyl[g] = h
                    tp_free[g] = [h]

            lagged = [(pr.sem[e], pr.n[pr.sem[e]]) for e in ("pe", "dve", "pool")]
            h_as0 = op("pool", lambda e: e.memset(AS, 0.0), lagged)
            h_rp2 = [spread(0, "dve", lagged), spread(1, "pool", lagged)]
            h_sd0 = op("pool", lambda e: e.memset(flat(xx), 0.0), lagged)
            KRn = KR.rearrange("p c (n s) -> p c n s", n=8)
            KDv = [z.rearrange("p (n s) -> p n s", n=8) for z in KD]
            kd_rd = [[], []]
            as_rd = [h_as0]
            hTT, hKE, hS_ = {}, {}, {}

            def rounds(c):
                nonlocal as_rd
                hkd = None
                ha = {}

                def turn(q0):
                    nonlocal as_rd
                    i, fr = bank()
                    nq = min(2, 8 - q0)
                    for q in range(q0, q0 + nq):
                        for m in range(2):
                            o = 256 * (q - q0) + P * m
                            h = op("pe", lambda e, q=q, m=m, o=o: e.transpose(PS[:, i, o:o + P], AS[:, q - 1, m, :], ident), fr, ha[q], inc=(q == q0 + nq - 1 and m == 1))
                    as_new.append(h)
                    o = TT[c][:, q0 - 1:q0 - 1 + nq].rearrange("p q m n h l -> p (q m n h l)")
                    h = op("act", lambda e: e.copy(o, PS[:, i, 0:256 * nq]), h, lagged)
                    bank_free[i] = [h]
                    hTT.setdefault(c, []).append(h)

                as_new = []
                for q in range(1, 9):
                    cur, old = KDv[q % 2], KDv[(q - 1) % 2]
                    h1 = op("act", lambda e, cur=cur, q=q: e.copy(cur[:, :, 16 * (q - 1):16 * q], KRn[:, c, :, 16 * (q - 1):16 * q]), hKR, kd_rd[q % 2], lagged)
                    h2 = None
                    if q > 1:
                        h2 = op("dve", lambda e, cur=cur, old=old, q=q: e.tensor_tensor(cur[:, :, 0:16 * (q - 1)], old[:, :, 0:16 * (q - 1)], Wb4[:, c, :, q - 1:q].broadcast_to([P, 8, 16 * (q - 1)]), ALU.mult), hkd, kd_rd[q % 2], hWb)
                    hkd = [h1, h2]
                    if q == 8:
                        break
                    i, fr = bank()
                    for n in range(8):
                        r_, m = 32 * (n % 4), P * (n // 4)
                        h = mm(PS[r_:r_ + 32, i, m:m + 16 * q], RP2[c][:, n, q].rearrange("p h l -> p (h l)"), cur[:, n, 0:16 * q], True, True, [fr, hkd, h_rp2[c]], inc=(n == 7))
                    ha[q] = op("act", lambda e, i=i, q=q: e.copy(AS[:, q - 1, :, 0:16 * q], PS[:, i, 0:256].rearrange("p (m k) -> p m k", m=2)[:, :, 0:16 * q]), h, as_rd)
                    bank_free[i] = [ha[q]]
                    kd_rd[q % 2] = [h, h2]
                    kd_rd[(q - 1) % 2] = kd_rd[(q - 1) % 2] + [h2]
                    if q in (3, 5, 7):
                        turn(q - 2)
                hKE[c] = []
                for g in range(2):
                    i, fr = bank()
                    for j in range(4):
                        n = 4 * g + j
                        h = op("pe", lambda e, i=i, j=j, n=n: e.transpose(PS[:, i, P * j:P * j + P], KDv[0][:, n, :], ident), fr, hkd, inc=(j == 3))
                    kd_rd[0] = [h]
                    h = op("act", lambda e, i=i, g=g: e.copy(KEs[c][:, 512 * g:512 * g + 512], PS[:, i, :]), h, lagged)
                    bank_free[i] = [h]
                    hKE[c].append(h)
                turn(7)
                as_rd = as_new

            def states(c):
                i, fr = bank()
                for n in range(8):
                    for hh_ in range(2):
                        ch = P * c + 64 * hh_
                        h = mm(PS[64 * hh_:64 * hh_ + 64, i, 64 * n:64 * n + 64], KEs[c][:, P * n + 64 * hh_:P * n + 64 * hh_ + 64], vtok[:, n, ch:ch + 64], True, True, [fr, hKE[c], hv], inc=(n == 7 and hh_ == 1))
                hs = op("dve", lambda e: e.memset(St[:, c, 0, :], 0.0), hprev)
                for n in range(7):
                    hs = op("dve", lambda e, n=n: e.scalar_tensor_tensor(out=St[:, c, n + 1, :], in0=St[:, c, n, :], scalar=TD[:, c, n:n + 1], in1=PS[:, i, 64 * n:64 * n + 64], op0=ALU.mult, op1=ALU.add), h, hs, hTD)
                bank_free[i] = [hs]
                hS_[c] = []
                for hh_ in range(2):
                    rows, co = slice(64 * hh_, 64 * hh_ + 64), slice(64 * hh_, 64 * hh_ + 64)
                    hS_[c].append(op("act", lambda e, rows=rows, co=co: e.copy(SD[c][rows, :, co], St[rows, c, 0:8, :]), hs, h_sd0))

            def outputs(c):
                for g in range(2):
                    i, fr = bank()
                    for j in range(4):
                        n = 4 * g + j
                        o = P * j
                        mm(PS[:, i, o:o + P], SD[c][:, n, :], RR[:, c, P * n:P * n + P], True, False, [fr, hS_[c], hrpp, hTT[c], hv], inc=False)
                        for hh_ in range(2):
                            r_, ch = 64 * hh_, P * c + 64 * hh_
                            h = mm(PS[r_:r_ + 64, i, o + 16:o + P].rearrange("p (q l) -> p q l", l=16), vtok[:, n, ch:ch + 64], TT[c][:, :, n // 4, n % 4, hh_, :], False, True, inc=(j == 3 and hh_ == 1))
                    ys = yl[:, c, 512 * g:512 * g + 512]
                    h = op("dve", lambda e, i=i, ys=ys: e.tensor_tensor(ys, ys, PS[:, i, :], ALU.add), h, hyl)
                    bank_free[i] = [h]
                    i, fr = bank()
                    for j in range(4):
                        h2 = op("pe", lambda e, i=i, j=j, ys=ys: e.transpose(PS[:, i, P * j:P * j + P], ys[:, P * j:P * j + P], ident), fr, h, inc=(j == 3))
                    h2 = op("act", lambda e, i=i, g=g: e.copy(ytok[:, 4 * g:4 * g + 4, P * c:P * c + P], PS[:, i, :].rearrange("p (t x) -> p t x", t=4)), h2, rd[1], lagged)
                    bank_free[i] = [h2]
                    hy_all.append(h2)

            hy_all = []
            rounds(0)
            states(0)
            rounds(1)
            outputs(0)
            states(1)
            outputs(1)
            yg = ytok.rearrange("p t (h j) -> p (t h) j", j=64)
            mv = st[:, 192:256].rearrange("p (g k) -> p g k", k=2)
            for g in range(32):
                h = op("dve", lambda e, g=g: e.bn_stats(st[:, 6 * g:6 * g + 6], yg[:, g, :]), hy_all)
            for g in range(32):
                h = op("dve", lambda e, g=g: e.bn_aggr(mv[:, g, :], st[:, 6 * g:6 * g + 6]), h if g == 0 else None)
            h = op("dve", lambda e: e.tensor_scalar(st[:, 256:288], mv[:, :, 1], 0.00064, None, ALU.add), h)
            h = op("act", lambda e: e.activation(st[:, 288:320], st[:, 256:288], ACT.Sqrt), h)
            h = op("dve", lambda e: e.reciprocal(st[:, 320:352], st[:, 288:320]), h)
            h = op("dve", lambda e: e.tensor_tensor(yg, yg, mv[:, :, 0:1].broadcast_to([P, 32, 64]), ALU.subtract), h)
            h = op("dve", lambda e: e.tensor_tensor(yg, yg, st[:, 320:352].unsqueeze(2).broadcast_to([P, 32, 64]), ALU.mult), h)
            hyn = h
            hT_n = []
            for c in range(2):
                for g in range(2):
                    i, fr = bank()
                    for j in range(4):
                        t = 4 * g + j
                        h = op("pe", lambda e, i=i, j=j, t=t, c=c: e.transpose(PS[:, i, P * j:P * j + P], ytok[:, t, P * c:P * c + P], ident), fr, hyn, inc=(j == 3))
                    h = op("act", lambda e, i=i, c=c, g=g: e.activation(tmp[:, c, 512 * g:512 * g + 512], PS[:, i, :], ACT.Identity, bias=cv("ln_b", c), scale=cv("ln_w", c)), h, as_rd)
                    bank_free[i] = [h]
                    hT_n.append(h)
            for t in range(0, TB_, 2):
                i, fr = bank()
                for j in range(2):
                    for k in range(2):
                        h = mm(PS[:, i, D * j:D * j + D], tmp[:, k, P * (t + j):P * (t + j) + P], Wo[:, k, :], k == 0, k == 1, [fr, hT_n])
                xs = X[:, TB_ * b + t:TB_ * b + t + 2, :]
                h = op("dve", lambda e, i=i, xs=xs: e.tensor_tensor(xs, xs, PS[:, i, :].rearrange("p (a c) -> p a c", a=2), ALU.add), h)
                bank_free[i] = [h]
            hprev = [(pr.sem[e], pr.n[pr.sem[e]]) for e in ("pe", "act", "dve", "pool")]
        bar = pr.barrier("c")
        if dbg == "x0":
            return finish()

        arena.lo = base0
        CN = arena.up(4 * S).bitcast(BF16).rearrange("p (t k) -> p t k", t=TB_)
        PM = arena.up(2 * S).bitcast(U8).rearrange("p (t k) -> p t k", t=TB_)
        e_mark = arena.lo
        C1 = arena.up(NT * D).rearrange("p (t c) -> p t c", t=NT)
        c_mark = arena.lo
        b2e = arena.up(E * D)
        s_b2 = pr.new_sem("s_b2")
        h_wc = [h_wc, load(s_b2, b2e, a["L0_ffn_b2"].rearrange("e c -> (e c)").partition_broadcast(P), bar)]
        NEX = 2
        exw = [(arena.up(2 * FH).rearrange("p (c n) -> p c n", c=2), arena.up(8 * D).rearrange("p (f n) -> p f n", f=8)) for _ in range(NEX)]
        h_ex = {}
        s_ex = [[pr.new_sem("s_ex") for _ in range(NEX)] for _ in range(2)]

        def get_w(e_, layer, waits=()):
            src = (a["L0_ffn_W1"][e_].rearrange("(c p) n -> p c n", c=2), a["L0_ffn_W2"][e_].rearrange("(f p) n -> p f n", f=8))[layer]
            h_ex[e_, layer] = load(s_ex[layer][e_ % NEX], exw[e_ % NEX][layer], src, *waits)

        for e_ in range(NEX):
            get_w(e_, 0, [bar])
            get_w(e_, 1)
        zt = arena.up(2048)
        iota = arena.up(S)
        pki = arena.up(TB_ * 32).bitcast(I32).rearrange("p (t j) -> p t j", t=TB_)
        pkf = arena.up(TB_ * 32).rearrange("p (t j) -> p t j", t=TB_)
        pkm = arena.up(TB_ * 8).bitcast(U8).rearrange("p (t j) -> p t j", t=TB_)
        hit = arena.up(S // 2).bitcast(BF16)
        pkmf = arena.up(TB_ * 32).rearrange("p (t j) -> p t j", t=TB_)
        s_pk = pr.new_sem("s_pk")
        load(s_pk, iota, a["k_iota"])
        load(s_pk, pki, a["idx"].rearrange("(t p) j -> p t j", p=P))
        load(s_pk, pkm, a["imask"].rearrange("(t p) j -> p t j", p=P))
        h_pk = load(s_pk, PM, a["pmask"].rearrange("(t p) k -> p t k", p=P))
        h = op("pool", lambda e: e.tensor_copy(pkf, pki), h_pk)
        h = op("pool", lambda e: e.tensor_scalar(pkf, pkf, 1.0, None, ALU.add), h)
        h2 = op("pool", lambda e: e.tensor_copy(pkmf, pkm), h_pk)
        h = op("pool", lambda e: e.tensor_tensor(pkf, pkf, pkmf, ALU.mult), h, h2)
        h = op("pool", lambda e: e.tensor_scalar(pkf, pkf, 1.0, None, ALU.subtract), h)
        h_pkf = h

        def count(eng, t, j, h):
            col = pkf[:, t, j:j + 1]
            if j == 0:
                return op(eng, lambda e: e.tensor_scalar(CN[:, t, :], iota, col, None, ALU.is_equal), h_pkf)
            if eng == "dve":
                return op(eng, lambda e: e.scalar_tensor_tensor(out=CN[:, t, :], in0=iota, scalar=col, in1=CN[:, t, :], op0=ALU.is_equal, op1=ALU.add), h)
            h = op(eng, lambda e: e.tensor_scalar(hit, iota, col, None, ALU.is_equal), h)
            return op(eng, lambda e: e.tensor_tensor(CN[:, t, :], CN[:, t, :], hit, ALU.add), h)

        cn_h = [None] * TB_
        cn_work = {"pool": [(t, j) for t in range(2) for j in range(32)],
                   "dve": [(t, j) for t in range(2, 8) for j in range(32)]}

        LB = nc.dram_tensor("prior", (S, S), F32, kind="Internal").ap()
        lbw, lbt = zt[:, 0:S], zt[:, S:2 * S]
        s_lb = pr.new_sem("s_lb")
        h_lb = [None] * TB_
        lb_at = []

        logs, diffs = [], []

        def take_logs():
            while logs:
                logs.pop(0)()

        def store_diffs():
            take_logs()
            while diffs:
                diffs.pop(0)()

        def prior(t):
            store_diffs()
            busy = h_lb[lb_at[-1]] if lb_at else h_zero
            lb_at.append(t)
            h1 = op("dve", lambda e: e.tensor_scalar(lbw, CN[:, t, :], 1.0, None, ALU.max), cn_h[t], busy)
            h2 = op("dve", lambda e: e.tensor_scalar(lbt, CN[:, t, :], 0.0, 1e30, ALU.is_equal, ALU.mult), busy)

            def log():
                h = op("act", lambda e: e.activation(lbw, lbw, ACT.Ln), h1)

                def diff():
                    h3 = op("dve", lambda e: e.tensor_tensor(lbt, lbt, lbw, ALU.subtract), h, h2)
                    h_lb[t] = load(s_lb, LB[P * t:P * t + P, :], lbt, h3)

                diffs.append(diff)

            logs.append(log)

        def pump(eng, n):
            for _ in range(min(n, len(cn_work[eng]))):
                t, j = cn_work[eng].pop(0)
                cn_h[t] = count(eng, t, j, cn_h[t])
                if eng == "dve" and j == 31:
                    prior(t)

        pump("pool", 18)
        h = op("dve", lambda e: e.memset(zt, 0.0))
        s_z = pr.new_sem("s_z")
        for j in range(4):
            h_zero = dma("act", s_z, lambda e, j=j: e.dma_start(Xg[1024 * j:1024 * j + 1024, :].rearrange("(p r) c -> p (r c)", p=P), zt), h)
        xT1 = [arena.up(2 * S).rearrange("p (c s) -> p c s", c=2) for _ in range(B)]
        hb = [arena.up(8 * 512).rearrange("p (f s) -> p f s", f=8) for _ in range(2)]
        hb_rd = [[], []]
        xT_h = [to_T(X[:, TB_ * b:TB_ * b + TB_, :], xT1[b], [], "dve") for b in range(B)]

        def mlp_hidden(src, s0, w, bias, func, dst, waits):
            last = None
            for f in range(8):
                i, fr = bank()
                for k in range(2):
                    h = mm(PS[:, i, :], w[:, k, P * f:P * f + P], src[:, k, s0:s0 + 512], k == 0, k == 1, [fr, waits])
                last = op("act", lambda e, i=i, f=f: e.activation(dst[:, f, :], PS[:, i, :], func, bias=cvec[:, bias + f:bias + f + 1]), h)
                bank_free[i] = [last]
            return last

        def mlp_out(src, w, bias, dst, waits, dwaits):
            hs_ = []
            for t in range(0, 4, 2):
                i, fr = bank()
                for j in range(2):
                    for f in range(8):
                        h = mm(PS[:, i, D * j:D * j + D], src[:, f, P * (t + j):P * (t + j) + P], w[:, f, :], f == 0, f == 7, [fr, waits])
                h2 = op("dve", lambda e, i=i, t=t: e.tensor_tensor(dst[:, t:t + 2, :], PS[:, i, :].rearrange("p (a c) -> p a c", a=2), bias.unsqueeze(1).broadcast_to([P, 2, D]), ALU.add), h, dwaits)
                bank_free[i] = [h2]
                hs_.append(h2)
            return h, hs_

        pend = None
        hC = []
        for q in range(5):
            pump("dve", 10 if q < 4 else 0)
            if q < 4:
                b, n = q // 2, q % 2
                hh = mlp_hidden(xT1[b], 512 * n, W1c, CB1, ACT.Gelu, hb[q % 2], [h_wc, xT_h[b], hb_rd[q % 2]])
            if pend is not None:
                pq, ph = pend
                hp, hs_ = mlp_out(hb[pq % 2], Wc[pq // 2], bc[pq // 2], C1[:, 4 * pq:4 * pq + 4, :], [ph], [h_wc])
                hb_rd[pq % 2] = [hp]
                hC += hs_
            pend = (q, hh) if q < 4 else None

        xr0, xr1 = (z.rearrange("p c s -> p (c s)") for z in xT1)
        hT_ = [to_T(C1[:, TB_ * b:TB_ * b + TB_, :], xT1[b], [hC], "dve") for b in range(B)]
        rt = arena.up(1600)
        at = [0]

        def ra(n):
            at[0] += n
            return rt[:, at[0] - n:at[0]]

        def v8(z):
            return z.rearrange("p (t e) -> p t e", e=8)

        PR, M8, OH, PQ = ra(128), ra(128), ra(256), ra(256)
        IX = ra(128).bitcast(U32)
        IXF = ra(32).rearrange("p (k t) -> p k t", k=2)
        BS = ra(256)
        s1, s2, wk, posk, keep, sl, tk = (ra(32).rearrange("p (k t) -> p k t", k=2) for _ in range(7))
        cnt = ra(8)
        WK = ra(32).rearrange("p (k t) -> p k t", k=2)
        SI = ra(32).bitcast(I32).rearrange("p (k t) -> p k t", k=2)
        GI = ra(32).bitcast(I32).rearrange("p (k t) -> p k t", k=2)
        i, fr = bank()
        for t in range(NT):
            for k in range(2):
                h = mm(PS[:, i, 8 * t:8 * t + 8], xT1[t // 8][:, k, P * (t % 8):P * (t % 8) + P], Wg[:, k, :], k == 0, k == 1, [fr, hT_, h_wc], inc=(t == NT - 1 and k == 1))
        LG = v8(PS[:, i, 0:128])

        def dv(fn, *w):
            return op("dve", fn, *w)

        mx = s1.rearrange("p k t -> p (k t)")[:, 0:16]
        sm = s2.rearrange("p k t -> p (k t)")[:, 0:16]
        h = dv(lambda e: e.tensor_reduce(mx, LG, AX.X, ALU.max), h)
        h = dv(lambda e: e.tensor_tensor(v8(PR), LG, mx.unsqueeze(2).broadcast_to([P, 16, 8]), ALU.subtract), h)
        bank_free[i] = [h]
        h = op("act", lambda e: e.activation(PR, PR, ACT.Exp), h)
        h = dv(lambda e: e.tensor_reduce(sm, v8(PR), AX.X, ALU.add), h)
        h = dv(lambda e: e.reciprocal(mx, sm), h)
        h = dv(lambda e: e.tensor_tensor(v8(PR), v8(PR), mx.unsqueeze(2).broadcast_to([P, 16, 8]), ALU.mult), h)
        for t in range(NT):
            h2 = dv(lambda e, t=t: e.max(v8(M8)[:, t, :], v8(PR)[:, t, :]), h)
        for t in range(NT):
            h3 = dv(lambda e, t=t: e.max_index(IX[:, 8 * t:8 * t + 8], v8(M8)[:, t, :], v8(PR)[:, t, :]), h2)
        M8k = v8(M8)[:, :, 0:2].rearrange("p t k -> p k t")
        h = dv(lambda e: e.tensor_copy(IXF, v8(IX)[:, :, 0:2].rearrange("p t k -> p k t")), h3)
        iota8 = kslot[:, 0:8]
        OHv = OH.rearrange("p (k t e) -> p k t e", k=2, t=16)
        for k in range(2):
            hoh = dv(lambda e, k=k: e.tensor_tensor(OHv[:, k], iota8.unsqueeze(1).broadcast_to([P, 16, 8]), IXF[:, k, :].unsqueeze(2).broadcast_to([P, 16, 8]), ALU.is_equal), h, h_wc)
        h = dv(lambda e: e.tensor_tensor(s1[:, 0, :], M8k[:, 0, :], M8k[:, 1, :], ALU.add), h2)
        h = dv(lambda e: e.tensor_scalar(s1[:, 0, :], s1[:, 0, :], 1e-9, None, ALU.add), h)
        h = dv(lambda e: e.reciprocal(s2[:, 0, :], s1[:, 0, :]), h)
        hwk = dv(lambda e: e.tensor_tensor(wk, M8k, s2[:, 0:1, :].broadcast_to([P, 2, 16]), ALU.mult), h)
        i, fr = bank()
        h = mm(PS[:, i, 0:256], triu, OH, True, True, [fr, hoh])
        h = mm(PS[:, i, 256:512], onesm, OH, True, True)
        BSv = BS.rearrange("p (k t e) -> p k t e", k=2, t=16)
        TOT = PS[:, i, 256:512].rearrange("p (k t e) -> p k t e", k=2, t=16)
        PQv = PQ.rearrange("p (k t e) -> p k t e", k=2, t=16)
        h0_ = dv(lambda e: e.memset(BSv[:, :, 0, :], -1.0), h)
        for t in range(1, NT):
            h0_ = dv(lambda e, t=t: e.tensor_tensor(BSv[:, :, t, :], BSv[:, :, t - 1, :], TOT[:, :, t - 1, :], ALU.add), h0_)
        h1 = dv(lambda e: e.tensor_tensor(cnt, BSv[:, 0, 15, :], TOT[:, 0, 15, :], ALU.add), h0_)
        h1 = dv(lambda e: e.tensor_scalar(cnt, cnt, 1.0, float(CAP), ALU.add, ALU.min), h1)
        h2 = dv(lambda e, i=i: e.tensor_tensor(PQ, PS[:, i, 0:256], BS, ALU.add), h0_)
        bank_free[i] = [h2]
        h2 = dv(lambda e: e.tensor_tensor(PQv[:, 1], PQv[:, 1], cnt.unsqueeze(1).broadcast_to([P, 16, 8]), ALU.add), h2, h1)
        h2 = dv(lambda e: e.tensor_tensor(PQ, PQ, OH, ALU.mult), h2)
        h2 = dv(lambda e: e.tensor_reduce(posk, PQv, AX.X, ALU.add), h2)
        h3 = dv(lambda e: e.tensor_scalar(keep, posk, float(CAP), None, ALU.is_lt), h2)
        h4 = dv(lambda e: e.scalar_tensor_tensor(out=sl, in0=IXF, scalar=float(CAP), in1=posk, op0=ALU.mult, op1=ALU.add), h2)
        hWK = dv(lambda e: e.tensor_tensor(WK, wk, keep, ALU.mult), hwk, h3)
        h5 = dv(lambda e: e.tensor_tensor(sl, sl, keep, ALU.mult), h3, h4)
        hGI = dv(lambda e: e.tensor_copy(GI, sl), h5)
        trash = kslot[:, 8:24]
        h6 = dv(lambda e: e.tensor_scalar(tk, keep, -1.0, 1.0, ALU.mult, ALU.add), h3)
        for k in range(2):
            h7 = dv(lambda e, k=k: e.tensor_scalar(s1[:, k, :], trash, float(N * k), None, ALU.add), h)
        h7 = dv(lambda e: e.tensor_tensor(tk, tk, s1, ALU.mult), h6, h7)
        h7 = dv(lambda e: e.tensor_tensor(sl, sl, tk, ALU.add), h7, hGI)
        hSI = dv(lambda e: e.tensor_copy(SI, sl), h7)
        s_sc = pr.new_sem("s_sc")
        for k in range(2):
            for t in range(NT):
                h_sc = dma("pool", s_sc, lambda e, k=k, t=t: e.indirect_dma_start(
                    Xg[:, :], bass.IndirectOffsetOnAxis(ap=SI[:, k, t:t + 1].bitcast(U32), axis=0), C1[:, t, :], None), hSI, hC, h_zero)

        pump("pool", 46)

        xg = [arena.up(4 * D).rearrange("p (t c) -> p t c", t=4) for _ in range(2)]
        xgT = [xr0[:, 1024 * j:1024 * j + 1024].rearrange("p (c s) -> p c s", c=2) for j in range(2)]
        ye = [xr1[:, 1024 * j:1024 * j + 1024].rearrange("p (t c) -> p t c", t=4) for j in range(2)]
        xg_rd, xgT_rd, ye_rd = [[]] * 3, [[]] * 2, [[]] * 2
        s_xg = [pr.new_sem("s_xg") for _ in range(2)]
        s_ye = [pr.new_sem("s_ye") for _ in range(2)]
        hb_rd = [[(pr.sem["pe"], pr.n[pr.sem["pe"]])]] * 2
        h_yst = []
        h_xg = {}

        def get_x(e_):
            h_xg[e_] = load(s_xg[e_ % 2], xg[e_ % 2], Xg[CAP * e_:CAP * e_ + CAP, :].rearrange("(t p) c -> p t c", p=P), h_sc, xg_rd[e_ % 2])

        for e_ in range(2):
            get_x(e_)
        pend = None
        for e_ in range(E + 1):
            if diffs:
                store_diffs()
            pump("dve", 200 if e_ == E else 9 if e_ else 32)
            if e_ in (E - 2, E):
                prior(e_ // E)
            if e_ == E:
                store_diffs()
            if e_ < E:
                u = e_ % 2
                T_ = []
                for c in range(2):
                    i, fr = bank()
                    for j in range(4):
                        h = op("pe", lambda e, i=i, j=j, c=c, u=u: e.transpose(PS[:, i, P * j:P * j + P], xg[u][:, j, P * c:P * c + P], ident), fr, h_xg[e_], inc=(j == 3))
                    h2 = op("act", lambda e, i=i, c=c, e_=e_: e.copy(xgT[e_ % 2][:, c, :], PS[:, i, :]), h, xgT_rd[e_ % 2])
                    bank_free[i] = [h2]
                    T_.append(h2)
                xg_rd[u] = [h]
                if e_ + 2 < E:
                    get_x(e_ + 2)
                w1e, w2e = exw[e_ % NEX]
                hh = mlp_hidden(xgT[e_ % 2], 0, w1e, CB1 + 8 + 8 * e_, ACT.Gelu_apprx_tanh, hb[e_ % 2], [h_ex[e_, 0], T_, hb_rd[e_ % 2]])
                xgT_rd[e_ % 2] = [(pr.sem["pe"], pr.n[pr.sem["pe"]])]
                if e_ + NEX < E:
                    get_w(e_ + NEX, 0, xgT_rd[e_ % 2])
                take_logs()
                pump("dve", 8 if e_ else 5)
            if pend is not None:
                pe_, ph = pend
                hp, hs_ = mlp_out(hb[pe_ % 2], exw[pe_ % NEX][1], b2e[:, D * pe_:D * pe_ + D], ye[pe_ % 2], [ph, h_ex[pe_, 1]], [h_wc, ye_rd[pe_ % 2]])
                hb_rd[pe_ % 2] = [hp]
                h = load(s_ye[pe_ % 2], Ye[CAP * pe_:CAP * pe_ + CAP, :].rearrange("(t p) c -> p t c", p=P), ye[pe_ % 2], hs_)
                ye_rd[pe_ % 2] = [h]
                h_yst.append(h)
                if pe_ + NEX < E:
                    get_w(pe_ + NEX, 1, [hp])
            pend = (e_, hh) if e_ < E else None
        done_x = [(pr.sem[e], pr.n[pr.sem[e]]) for e in ("pe", "act", "dve", "pool")] + [h_sc, h_yst]
        gt = [zt[:, D * j:D * j + D] for j in range(8)]
        s_g = [pr.new_sem("s_g") for _ in range(8)]
        gt_rd = [[] for _ in range(8)]
        hx_ = [None] * NT

        def combine(t):
            for k in range(2):
                u = (2 * t + k) % 8
                h = dma("pool", s_g[u], lambda e, k=k, t=t, u=u: e.indirect_dma_start(
                    gt[u], None, Ye[:, :], bass.IndirectOffsetOnAxis(ap=GI[:, k, t:t + 1].bitcast(U32), axis=0)), h_yst, gt_rd[u], hGI, h_lb)
                h = dv(lambda e, k=k, t=t, u=u: e.scalar_tensor_tensor(out=X[:, t, :], in0=gt[u], scalar=WK[:, k, t:t + 1], in1=X[:, t, :], op0=ALU.mult, op1=ALU.add), h, hx_[t], hWK)
                hx_[t] = h
                gt_rd[u] = [h]

        for t in range(TB_):
            combine(t)
        x_rdy = [[hx_[TB_ - 1]], None]

        def phase_e(ebar, x_rdy):
            arena.lo = e_mark
            arena.hi = hi0
            FP = [nc.dram_tensor(f"parts{k}", (3, D, S), BF16, kind="Internal").ap() for k in range(4)]
            Wall = arena.up(8 * D)
            Wq4, Wk4, Wv4, Wo4 = (Wall[:, 2 * D * j:2 * D * j + 2 * D].rearrange("p (c n) -> p c n", c=2) for j in range(4))
            bvb = arena.up(D)
            xT4 = arena.up(2 * S).rearrange("p (c s) -> p c s", c=2)
            LOb = arena.up(S)
            K6 = arena.up(8 * S).bitcast(BF16).rearrange("p (h s) -> p h s", h=16)
            Q6 = [arena.up(8 * P).bitcast(BF16).rearrange("p (h s) -> p h s", h=16) for _ in range(2)]
            V4 = [arena.up(TB_ * 272).rearrange("p (t h j) -> p t h j", t=TB_, h=16) for _ in range(2)]
            X4T = [arena.down(2 * S).rearrange("p (c s) -> p c s", c=2) for _ in range(2)]
            Oc = arena.up(2 * S).rearrange("p (t c) -> p t c", t=TB_)
            Ab = [arena.up(S) for _ in range(2)]
            Sb = [arena.up(S) for _ in range(3)]
            Pt = [arena.up(S) for _ in range(8)]
            Tb = arena.up(S)
            OT = arena.up(512)
            mr = arena.up(8)
            rc = arena.up(16)
            ub = arena.up(8)
            s_e = pr.new_sem("s_e")
            for w_, n_ in ((Wq4, "Wq"), (Wk4, "Wk"), (Wv4, "Wv"), (Wo4, "Wo")):
                load(s_e, w_, kmaj("L1_cond_" + n_), ebar)
            h_we = load(s_e, bvb, a["L1_cond_bv"].partition_broadcast(P))
            QF = X4T[0]
            HM = X4T[1].rearrange("p c s -> p (c s)").bitcast(BF16).rearrange("p (k c s) -> p k c s", k=2, c=2)
            LO = LOb.bitcast(BF16).rearrange("p (c s) -> p c s", c=2)
            s_fp = [pr.new_sem("s_fp") for _ in range(4)]
            s_k6 = [pr.new_sem("s_k6") for _ in range(4)]
            s_q6 = [pr.new_sem("s_q6") for _ in range(2)]
            h_fp, h_k6, h_v4 = {}, {}, {}
            stg = []
            xt_rd = []
            SBK, PBK, OBK = [(0, 1), (2, 3)], [4, 5, 6], 7
            p_at = [0]
            p_fr = [list(bank_free[i]) for i in PBK]

            def pbank():
                u = p_at[0] % 3
                p_at[0] += 1
                return PBK[u], u

            def get_k(b, g4):
                for g, part in enumerate((0, 1, 0, 2, 0, 1)):
                    h_k6[b, g4] = dma("sp", s_k6[g4], lambda e, g=g, part=part: e.dma_start(
                        K6[16 * g:16 * g + 16, 4 * g4:4 * g4 + 4, :], FP[2 * b + 1][part].rearrange("(h r) s -> r h s", r=16)[:, 4 * g4:4 * g4 + 4, :]), h_fp[2 * b + 1], k_fr[g4])

            def prep(b):
                nonlocal stg, xt_rd
                hx4 = []
                for g in range(2):
                    for c in range(2):
                        i, u = pbank()
                        for j in range(4):
                            t = 4 * g + j
                            h = op("pe", lambda e, i=i, j=j, t=t, c=c: e.transpose(PS[:, i, P * j:P * j + P], X[:, TB_ * b + t, P * c:P * c + P], ident), p_fr[u], x_rdy[b], inc=(j == 3))
                        h = op("act", lambda e, i=i, c=c, g=g: e.copy(xT4[:, c, 512 * g:512 * g + 512], PS[:, i, :]), h, xt_rd)
                        p_fr[u] = [h]
                        hx4.append(h)
                        yield
                for kq in (1, 0):
                    w_, bias_, sc = ((Wq4, "bq", -0.25), (Wk4, "bk", 1.0))[kq]
                    hq = []
                    for c in range(2):
                        for n in range(2):
                            sl = slice(512 * n, 512 * n + 512)
                            i, u = pbank()
                            for k in range(2):
                                h = mm(PS[:, i, :], w_[:, k, P * c:P * c + P], xT4[:, k, sl], k == 0, k == 1, [p_fr[u], hx4, h_we])
                            h = dv(lambda e, i=i, c=c, sl=sl, bias_=bias_, sc=sc: e.tensor_scalar(QF[:, c, sl], PS[:, i, :], cv(bias_, c), sc, ALU.add, ALU.mult), h, stg)
                            p_fr[u] = [h]
                            hq.append(h)
                            yield
                    hh = []
                    for c in range(2):
                        h = op("act", lambda e, c=c: e.copy(HM[:, 0, c], QF[:, c]), hq, stg)
                        h = dv(lambda e, c=c: e.tensor_tensor(QF[:, c], QF[:, c], HM[:, 0, c], ALU.subtract), h)
                        yield
                        h = op("act", lambda e, c=c: e.copy(HM[:, 1, c], QF[:, c]), h)
                        hh.append(dv(lambda e, c=c: e.tensor_tensor(LO[:, c], QF[:, c], HM[:, 1, c], ALU.subtract), h, stg))
                        yield
                    j = 2 * b + kq
                    for part, src in ((0, HM[:, 0]), (1, HM[:, 1]), (2, LO)):
                        hd = dma("sp", s_fp[j], lambda e, j=j, part=part, src=src: e.dma_start(FP[j][part].rearrange("(c p) s -> p c s", p=P), src), hh)
                    h_fp[j] = hd
                    stg = [hd]
                    if kq and b == 0:
                        for g4 in range(4):
                            get_k(0, g4)
                for t in range(0, TB_, 2):
                    i, u = pbank()
                    for j in range(2):
                        for k in range(2):
                            h = mm(PS[:, i, D * j:D * j + D], xT4[:, k, P * (t + j):P * (t + j) + P], Wv4[:, k, :], k == 0, k == 1, [p_fr[u], hx4, h_we])
                    xt_rd = [h]
                    h_v4[b] = dv(lambda e, i=i, t=t: e.tensor_tensor(V4[b][:, t:t + 2, :, 0:16], PS[:, i, :].rearrange("p (a h j) -> p a h j", a=2, h=16), bvb.rearrange("p (h j) -> p h j", h=16).unsqueeze(1).broadcast_to([P, 2, 16, 16]), ALU.add), h)
                    p_fr[u] = [h_v4[b]]
                    yield

            k_fr = [[] for _ in range(4)]
            first = prep(0)
            for _ in range(20):
                next(first)
                yield
            pr.barrier("e")
            if dbg == "x1":
                return
            s_u = pr.new_sem("s_u")
            h_u = load(s_u, ub[:, 0:B], a["u"].rearrange("o b -> (o b)").partition_broadcast(P), pr.bar)
            h = op("act", lambda e: e.activation(ub[:, 2:4], ub[:, 0:2], ACT.Exp, scale=-5.0), h_u)
            h = op("pool", lambda e: e.tensor_scalar(ub[:, 2:4], ub[:, 2:4], 10.0, None, ALU.mult), h)
            h1 = op("pool", lambda e: e.tensor_scalar(ub[:, 4:6], ub[:, 2:4], 1.0, None, ALU.is_ge), h)
            h = op("pool", lambda e: e.tensor_scalar(ub[:, 2:4], ub[:, 2:4], 1.0, None, ALU.min), h1)
            h = op("pool", lambda e: e.tensor_scalar(ub[:, 6:8], ub[:, 4:6], -1.0, 1.0, ALU.mult, ALU.add), h)
            h_u = op("pool", lambda e: e.tensor_tensor(ub[:, 6:8], ub[:, 6:8], ub[:, 2:4], ALU.mult), h)
            SP_, LD_ = ub[:, 4:6], ub[:, 6:8]
            h_one = [op("pool", lambda e, v=v: e.memset(v[:, :, :, 16:17], 1.0)) for v in V4]
            s_fr = [[], []]
            h_oz = dv(lambda e: e.memset(PS[:, OBK, :], 0.0), pr.bar)
            sb_fr, pt_fr, ab_fr = [[], [], []], [[] for _ in range(8)], [[], []]
            q_fr = [[], []]
            h_q6, h_ab = {}, {}
            s_ab = [pr.new_sem("s_ab") for _ in range(2)]

            def get_q(m):
                b, t = m // TB_, m % TB_
                for g, part in enumerate((0, 0, 1, 0, 2, 1)):
                    h_q6[m] = dma("sp", s_q6[m % 2], lambda e, g=g, part=part, b=b, t=t, m=m: e.dma_start(
                        Q6[m % 2][16 * g:16 * g + 16], FP[2 * b][part].rearrange("(h r) s -> r h s", r=16)[:, :, P * t:P * t + P]), q_fr[m % 2], h_fp[2 * b])

            def bias(m, part):
                b, t = m // TB_, m % TB_
                A, T = Ab[m % 2], Tb
                if part == 0:
                    h_ab[m] = load(s_ab[m % 2], A, LB[P * t:P * t + P, :], ab_fr[m % 2], h_lb, pr.bar)
                    return
                hh, h2 = h_ab[m], h_ab.get(m - 1)
                hh = op("pool", lambda e: e.tensor_scalar(A, A, SP_[:, b:b + 1], 1.0, ALU.mult, ALU.mult), hh, h_u)
                h2 = op("pool", lambda e: e.tensor_scalar(T, PM[:, t, :], -1.0, 1.0, ALU.mult, ALU.add), h2, h_u)
                h2 = op("pool", lambda e: e.tensor_scalar(T, T, LD_[:, b:b + 1], 1.0, ALU.mult, ALU.mult), h2)
                h_ab[m] = op("pool", lambda e: e.tensor_tensor(A, A, T, ALU.add), hh, h2)

            Tb1 = X4T[1]
            Tb2 = K6.rearrange("p h s -> p (h s)").bitcast(F32)[:, 0:2 * S].rearrange("p (c s) -> p c s", c=2)
            items = [(m, h_) for m in range(B * TB_) for h_ in range(16)]
            st_ = {}
            bias(0, 0)
            for _ in first:
                pass
            bias(0, 1)
            get_q(0)
            get_q(1)
            hx_prev = None

            def scores(z):
                m, h_ = items[z]
                b = m // TB_
                bk = SBK[z % 2]
                for n in range(2):
                    h = mm(PS[:, bk[n], :], Q6[m % 2][0:96, h_, :], K6[0:96, h_, 512 * n:512 * n + 512], True, True, [s_fr[z % 2], h_q6[m], h_k6[b, h_ // 4]], inc=(n == 1))
                if h_ % 4 == 3 and m == TB_ - 1:
                    k_fr[h_ // 4] = [h]
                    get_k(1, h_ // 4)
                if h_ == 15:
                    q_fr[m % 2] = [h]
                    if m + 2 < B * TB_:
                        get_q(m + 2)
                ps = PS[:, bk[0]:bk[0] + 2, :].rearrange("p a s -> p (a s)")
                sbt, acc = Sb[z % 3], mr[:, z % 4:z % 4 + 1]
                h = dv(lambda e: e.tensor_tensor_reduce(sbt, ps, Ab[m % 2], 1.0, 3e38, ALU.add, ALU.min, acc), h, sb_fr[z % 3], h_ab[m], mr_rd.get(z - 4))
                s_fr[z % 2] = [h]
                if h_ == 15:
                    ab_fr[m % 2] = [h]
                st_[z] = h

            def expo(z):
                sbt, acc = Sb[z % 3], mr[:, z % 4:z % 4 + 1]
                h = op("act", lambda e: e.activation(sbt, sbt, ACT.Exp, bias=acc, scale=-1.0), st_[z])
                mr_rd[z] = h
                st_[z] = h

            def turn(z):
                sbt, ptt = Sb[z % 3], Pt[z % 8]
                hs_ = []
                for g in range(2):
                    i, u = pbank()
                    for j in range(4):
                        k = 4 * g + j
                        h = op("pe", lambda e, i=i, j=j, k=k: e.transpose(PS[:, i, P * j:P * j + P], sbt[:, P * k:P * k + P], ident), p_fr[u], st_[z], inc=(j == 3))
                    eng = "dve" if g == 0 else "act"
                    if eng == "dve":
                        h2 = dv(lambda e, i=i: e.tensor_copy(ptt[:, 0:512], PS[:, i, :]), h, pt_fr[z % 8])
                    else:
                        h2 = op("act", lambda e, i=i, g=g: e.copy(ptt[:, 512 * g:512 * g + 512], PS[:, i, :]), h, pt_fr[z % 8])
                    p_fr[u] = [h2]
                    hs_.append(h2)
                sb_fr[z % 3] = [h]
                st_[z] = hs_

            def values(z, ks):
                nonlocal o_fr, ot_rd
                m, h_ = items[z]
                b, t = m // TB_, m % TB_
                g = h_ // 4
                for k in ks:
                    for d in range(4):
                        r = 32 * d
                        h = mm(PS[r:r + 17, OBK, P * g:P * g + P], V4[b][:, k, h_ + d, :], Pt[(z + d) % 8][:, P * k:P * k + P], k == 0, k == 7, [[st_[z + x] for x in range(4)], o_fr, h_v4[b], h_one], inc=(k == 7 and d == 3))
                if ks[-1] < 7:
                    return
                for d in range(4):
                    pt_fr[(z + d) % 8] = [h]
                h = op("act", lambda e: e.copy(OT[:, P * g:P * g + P], PS[:, OBK, P * g:P * g + P]), h, ot_rd)
                o_fr = [h]
                ot_h.append(h)

            def gather(m):
                nonlocal ot_rd
                i, u = pbank()
                for j in range(4):
                    h = op("pe", lambda e, j=j: e.transpose(PS[:, i, P * j:P * j + P], OT[:, P * j:P * j + P], ident), p_fr[u], ot_h[-4:], inc=(j == 3))
                ot_rd = [h]
                p_fr[u] = None
                return i, u, h

            def normal(m, i, u, h):
                ov = PS[:, i, :].rearrange("p (h j) -> p h j", h=16)
                h = dv(lambda e: e.reciprocal(rc, ov[:, :, 16]), h)
                h = dv(lambda e: e.tensor_tensor(Oc[:, m % TB_, :].rearrange("p (h j) -> p h j", h=16), ov[:, :, 0:16], rc.unsqueeze(2).broadcast_to([P, 16, 16]), ALU.mult), h, oc_fr)
                p_fr[u] = [h]
                return h

            def closing(b, h):
                nonlocal oc_fr
                Ot = (Tb2 if b else Tb1)
                hs_ = []
                for g in range(2):
                    for c in range(2):
                        i, u = pbank()
                        for j in range(4):
                            t = 4 * g + j
                            h2 = op("pe", lambda e, i=i, j=j, t=t, c=c: e.transpose(PS[:, i, P * j:P * j + P], Oc[:, t, P * c:P * c + P], ident), p_fr[u], h, inc=(j == 3))
                        oc_fr = [h2]
                        h3 = op("act", lambda e, i=i, c=c, g=g: e.copy(Ot[:, c, 512 * g:512 * g + 512], PS[:, i, :]), h2)
                        p_fr[u] = [h3]
                        hs_.append(h3)
                        yield
                for c in range(2):
                    for n in range(2):
                        i, u = pbank()
                        for k in range(2):
                            h2 = mm(PS[:, i, :], Wo4[:, k, P * c:P * c + P], Ot[:, k, 512 * n:512 * n + 512], k == 0, k == 1, [p_fr[u], hs_])
                        h3 = op("act", lambda e, i=i, c=c, n=n: e.activation(X4T[b][:, c, 512 * n:512 * n + 512], PS[:, i, :], ACT.Identity, bias=cv("bo", c)), h2)
                        p_fr[u] = [h3]
                        yield

            last = None
            ot_rd, ot_h = [], []
            o_fr = [h_oz]
            extra = prep(1)
            mr_rd = {}
            oc_fr = []
            hx4T = []
            NZ = len(items)
            for z in range(NZ + 12):
                if z >= 20 and z % 2:
                    next(extra, None)
                if z < NZ:
                    if items[z][1] in (3, 7) and items[z][0] + 1 < B * TB_:
                        bias(items[z][0] + 1, items[z][1] // 4)
                    scores(z)
                if 2 <= z < NZ + 2:
                    turn(z - 2)
                if z < NZ:
                    expo(z)
                if z >= 5 and (z - 5) // 4 < NZ // 4 and (z - 5) % 4:
                    values((z - 5) // 4 * 4, ((0, 1, 2), (3, 4, 5), (6, 7))[(z - 5) % 4 - 1])
                if z >= 23 and (z - 23) % 16 == 0:
                    m = (z - 23) // 16
                    h = normal(m, *gather(m))
                    if m % TB_ == TB_ - 1:
                        last = closing(m // TB_, h)
                        next(last)
                elif last is not None:
                    next(last, None)
            for _ in last:
                pass
            X4T_.extend(X4T)

        X4T_ = []
        attend = phase_e(done_x, x_rdy)
        for t in range(TB_, NT):
            combine(t)
            x_rdy[1] = [hx_[NT - 1]]
            next(attend)
        for _ in attend:
            pass
        if dbg == "x1":
            return finish()
        X4T = X4T_
        pr.barrier("f")
        if dbg == "c2":
            hh = []
            for b in range(B):
                for t in range(TB_):
                    for c in range(2):
                        i, fr = bank()
                        h = op("pe", lambda e, i=i, t=t, c=c, b=b: e.transpose(PS[:, i, 0:P], X4T[b][:, c, P * t:P * t + P], ident), fr)
                        h = dv(lambda e, i=i, t=t, c=c, b=b: e.tensor_copy(X[:, TB_ * b + t, P * c:P * c + P], PS[:, i, 0:P]), h)
                        bank_free[i] = [h]
            return finish()

        def phase_f():
            arena.lo = base0
            fbar = pr.bar
            Wq5, Wk5, Wv5 = (arena.up(2 * FH).rearrange("p (c n) -> p c n", c=2) for _ in range(3))
            Wo5 = arena.up(8 * D).rearrange("p (f n) -> p f n", f=8)
            band = arena.up(768)
            gT = arena.up(B * 2 * 64).rearrange("p (b c g) -> p b c g", b=B, c=2)
            yT = [arena.up(8 * S).rearrange("p (f s) -> p f s", f=8) for _ in range(B)]
            q5, k5, v5 = ([arena.up(S) for _ in range(2)] for _ in range(3))
            sk = [arena.up(64) for _ in range(2)]
            sv = [arena.up(P) for _ in range(2)]
            Sb = [arena.up(449) for _ in range(3)]
            Se = [arena.up(321) for _ in range(2)]
            Pb = [arena.up(512) for _ in range(6)]
            Pt = [arena.up(512) for _ in range(4)]
            sm = arena.up(8)
            mr = arena.up(8)
            s_f = pr.new_sem("s_f")
            for w_, n_ in ((Wk5, "Wk"), (Wq5, "Wq"), (Wv5, "Wv")):
                load(s_f, w_, kmaj("L1_attn_" + n_), fbar)
            load(s_f, band, a["k_band"])
            h_w5 = load(s_f, Wo5, a["L1_attn_Wo"].rearrange("(f p) n -> p f n", f=8))
            hz = [op("pool", lambda e, z=z: e.memset(z, 0.0)) for z in Sb + Se + Pb + sv][-1]
            h_g = [dv(lambda e, b=b: e.tensor_reduce(gT[:, b], X4T[b].rearrange("p c (g l) -> p c g l", l=16), AX.X, ALU.add)) for b in range(B)]
            bfree = {i: [] for i in range(8)}
            units = [(b, f) for b in range(B) for f in range(8)]
            steps = [(u, t) for u in range(len(units)) for t in range(8)]
            u_rdy = [[] for _ in units]
            k_rd, v_rd, y_at = [[], []], [[], []], [[] for _ in range(B)]
            s_fr, se_fr = [[], [], []], [[], []]
            p_fr, pt_fr = [[] for _ in range(6)], [[] for _ in range(4)]
            state = {}

            def chunk(u, c, i=7):
                b, f = units[u]
                r, x_ = u % 2, X4T[b]
                fs = slice(P * f, P * f + P)
                if c < 4:
                    w_, dst, n = (Wk5, k5, c) if c < 2 else (Wq5, q5, c - 2)
                    for k in range(2):
                        h = mm(PS[:, i, :], w_[:, k, fs], x_[:, k, 512 * n:512 * n + 512], k == 0, k == 1, [bfree[i], h_w5])
                    o = dst[r][:, 512 * n:512 * n + 512]
                    if c < 2:
                        h = op("act", lambda e: e.copy(o, PS[:, i, :]), h, k_rd[r])
                    else:
                        h = dv(lambda e: e.tensor_scalar(o, PS[:, i, :], -0.125, None, ALU.mult), h, k_rd[r])
                elif c < 6:
                    for j in range(4):
                        t = 4 * (c - 4) + j
                        for k in range(2):
                            h = mm(PS[:, i, P * j:P * j + P], x_[:, k, P * t:P * t + P], Wv5[:, k, fs], k == 0, k == 1, [bfree[i]], inc=(j == 3 and k == 1))
                    o = v5[r][:, 512 * (c - 4):512 * (c - 4) + 512]
                    h = op("act", lambda e: e.copy(o, PS[:, i, :]), h, v_rd[r])
                elif c == 6:
                    for k in range(2):
                        h = mm(PS[:, i, 0:64], Wk5[:, k, fs], gT[:, b, k, :], k == 0, k == 1, [bfree[i], h_g])
                    h = dv(lambda e: e.tensor_copy(sk[r], PS[:, i, 0:64]), h, k_rd[r])
                else:
                    for k in range(2):
                        h = mm(PS[0:64, i, 0:P], gT[:, b, k, :], Wv5[:, k, fs], k == 0, k == 1, [bfree[i]])
                    h = dv(lambda e: e.tensor_copy(sv[r][0:64, :], PS[0:64, i, 0:P]), h, v_rd[r], hz)
                bfree[i] = [h]
                u_rdy[u].append(h)

            def geom(t):
                k0 = max(t - 1, 0)
                k1 = min(t + 2, 8)
                return k0, k1, P * (k1 - k0)

            def scores(z):
                u, t = steps[z]
                k0, k1, nk = geom(t)
                r = u % 2
                hs = []
                for d in range(2):
                    i = (2 * z + d) % 3
                    rows = slice(64 * d, 64 * d + 64)
                    q_ = q5[r][rows, P * t:P * t + P]
                    mm(PS[:, i, 0:nk], q_, k5[r][rows, P * k0:P * k1], True, True, [bfree[i], u_rdy[u]], inc=False)
                    hs.append(mm(PS[:, i, nk:nk + 64], q_, sk[r][rows, :], True, True))
                if t == 7:
                    k_rd[r] = [hs[-1]]
                w = nk + 64
                hx = []
                for d in range(2):
                    i, x, g = (2 * z + d) % 3, 2 * z + d, 2 * (z % 4) + d
                    if nk == 384:
                        sbt, frs, o, bnd = Sb[x % 3], s_fr, x % 3, band[:, 0:448]
                    else:
                        sbt, frs, o = Se[x % 2], se_fr, x % 2
                        bnd = band[:, 128:448] if t == 0 else band[:, 448:768]
                    pbt, acc, smc = Pb[x % 6], mr[:, g:g + 1], sm[:, g:g + 1]
                    h = dv(lambda e, i=i, sbt=sbt, bnd=bnd, acc=acc: e.tensor_tensor_reduce(sbt[:, 0:w], PS[:, i, 0:w], bnd, 1.0, 0.0, ALU.add, ALU.min, acc), hs[d], frs[o], hz, h_w5, state.get(("e", z - 4)))
                    bfree[i] = [h]
                    h = op("act", lambda e, sbt=sbt, pbt=pbt, acc=acc, smc=smc: e.activation(pbt[:, 0:w + 1], sbt[:, 0:w + 1], ACT.Exp, bias=acc, scale=-1.0, accum_out=smc), h, p_fr[x % 6], state.get(("d", z - 4)))
                    frs[o] = [h]
                    hx.append(h)
                state["e", z] = hx

            def scale(z):
                u, t = steps[z]
                w = geom(t)[2] + 64
                g = 2 * (z % 4)
                h = dv(lambda e: e.reciprocal(sm[:, g:g + 2], sm[:, g:g + 2]), state["e", z])
                hd = []
                for d in range(2):
                    pbt = Pb[(2 * z + d) % 6]
                    hd.append(op("pool", lambda e, pbt=pbt, d=d: e.tensor_scalar(pbt[:, 0:w], pbt[:, 0:w], sm[:, g + d:g + d + 1], 1.0, ALU.mult, ALU.mult), h))
                state["d", z] = hd

            def turn(z):
                u, t = steps[z]
                nj = geom(t)[2] // P + 1
                hs = []
                for d in range(2):
                    i, o = 3 + d, (2 * z + d) % 4
                    pbt, ptt = Pb[(2 * z + d) % 6], Pt[o]
                    for j in range(nj):
                        h = op("pe", lambda e, i=i, j=j, pbt=pbt: e.transpose(PS[:, i, P * j:P * j + P], pbt[:, P * j:P * j + P], ident), bfree[i], state["d", z][d], inc=(j == nj - 1))
                    p_fr[(2 * z + d) % 6] = [h]
                    if d:
                        h = dv(lambda e, i=i, ptt=ptt: e.tensor_copy(ptt[:, 0:P * nj], PS[:, i, 0:P * nj]), h, pt_fr[o])
                    else:
                        h = op("act", lambda e, i=i, ptt=ptt: e.copy(ptt[:, 0:P * nj], PS[:, i, 0:P * nj]), h, pt_fr[o])
                    bfree[i] = [h]
                    hs.append(h)
                state["t", z] = hs

            def values(z):
                u, t = steps[z]
                b, f = units[u]
                r = u % 2
                k0, k1, nk = geom(t)
                nj = k1 - k0 + 1
                n = z // 4
                i = 5 + n % 2
                for j in range(nj):
                    for d in range(2):
                        c = slice(64 * d, 64 * d + 64)
                        w_ = v5[r][:, P * (k0 + j):P * (k0 + j) + P][:, c] if j < nj - 1 else sv[r][:, c]
                        h = mm(PS[c, i, P * (t % 4):P * (t % 4) + P], w_, Pt[(2 * z + d) % 4][:, P * j:P * j + P], j == 0, j == nj - 1, [state["t", z], bfree[i] if t % 4 == 0 else None], inc=(j == nj - 1 and d == 1))
                pt_fr[(2 * z) % 4] = [h]
                pt_fr[(2 * z + 1) % 4] = [h]
                if t == 7:
                    v_rd[r] = [h]
                if t % 4 < 3:
                    return
                o = yT[b][:, f, 512 * (t // 4):512 * (t // 4) + 512]
                h = dv(lambda e: e.tensor_copy(o, PS[:, i, :]), h)
                bfree[i] = [h]
                y_at[b] = [h]

            def project(b, t, i=7):
                for k in range(8):
                    h = mm(PS[:, i, 0:D], yT[b][:, k, P * t:P * t + P], Wo5[:, k, :], k == 0, k == 7, [bfree[i], y_at[b]])
                xs = X[:, TB_ * b + t, :]
                h = dv(lambda e: e.tensor_tensor(xs, xs, PS[:, i, 0:D], ALU.add), h)
                bfree[i] = [h]

            for c in range(8):
                chunk(0, c, c)
            NZ = len(steps)
            for z in range(NZ + 2):
                if 1 <= z <= NZ:
                    scale(z - 1)
                if z < NZ:
                    scores(z)
                if z > 65 and z % 2 == 0 and z < 82:
                    project(0, (z - 66) // 2)
                if 2 <= z:
                    values(z - 2)
                if 1 <= z <= NZ:
                    turn(z - 1)
                if z < NZ and steps[z][0] + 1 < len(units):
                    chunk(steps[z][0] + 1, z % 8)
            for t in range(8):
                project(1, t, t)

        phase_f()
        pr.barrier("g")
        if dbg == "x2":
            return finish()

        def phase_g():
            arena.lo, arena.hi = base0, hi0
            gbar = pr.bar
            Wr7, Wk7, Wv7 = (arena.up(2 * D).rearrange("p (c n) -> p c n", c=2) for _ in range(3))
            s_h = pr.new_sem("s_h")
            for w_, n_ in ((Wr7, "r"), (Wk7, "k"), (Wv7, "v")):
                h_w7 = load(s_h, w_, kmaj("L1_ffn_W_" + n_), gbar)
            om = arena.up(4)
            for q, nm in enumerate(("mu_r", "mu_k")):
                i0 = CIDX[nm]
                h_om = dv(lambda e, q=q, i0=i0: e.tensor_scalar(om[:, 2 * q:2 * q + 2], cvec[:, i0:i0 + 2], -1.0, 1.0, ALU.mult, ALU.add))
            hT = [arena.up(2 * S).rearrange("p (c s) -> p c s", c=2) for _ in range(B)]
            xr, xk, ka = ([arena.up(2 * S).rearrange("p (c s) -> p c s", c=2) for _ in range(1)][0] for _ in range(3))
            R = arena.up(TB_ * D).rearrange("p (t c) -> p t c", t=TB_)
            wB = [adapter_space(64) for _ in range(B)]
            hx = [to_T(X[:, TB_ * b:TB_ * b + TB_, :], hT[b], [], ("act", "dve")[b]) for b in range(B)]
            hc = in_turns([adapter("g", b, 64, 10, 4, "L1_cond2_W1", None, "L1_cond2_W2", "L1_cond2_b2", "gb1", hT[b], hT[b], [hx[b], gbar], wB[b]) for b in range(B)])
            prev = []
            for b in range(B):
                hh = []
                for q, (dst, nm) in enumerate(((xr, "mu_r"), (xk, "mu_k"))):
                    for c in range(2):
                        h = dv(lambda e, dst=dst, c=c, nm=nm, b=b: e.tensor_scalar(dst[:, c], hT[b][:, c], cv(nm, c), None, ALU.mult), hc[b], prev)
                        h = dv(lambda e, dst=dst, c=c, q=q, b=b: e.scalar_tensor_tensor(out=dst[:, c, 1:S], in0=hT[b][:, c, 0:S - 1], scalar=om[:, 2 * q + c:2 * q + c + 1], in1=dst[:, c, 1:S], op0=ALU.mult, op1=ALU.add), h, h_om)
                        hh.append(h)
                hk = []
                for c in range(2):
                    for n in range(2):
                        i, fr = bank()
                        for k in range(2):
                            h = mm(PS[:, i, :], Wk7[:, k, P * c:P * c + P], xk[:, k, 512 * n:512 * n + 512], k == 0, k == 1, [fr, hh, h_w7])
                        o = ka[:, c, 512 * n:512 * n + 512]
                        h = op("act", lambda e, i=i, o=o: e.activation(o, PS[:, i, :], ACT.Relu), h, prev)
                        bank_free[i] = [h]
                        hk.append(op("pool", lambda e, o=o: e.tensor_tensor(o, o, o, ALU.mult), h))
                hr = []
                for t in range(0, TB_, 2):
                    i, fr = bank()
                    for j in range(2):
                        for k in range(2):
                            h = mm(PS[:, i, D * j:D * j + D], xr[:, k, P * (t + j):P * (t + j) + P], Wr7[:, k, :], k == 0, k == 1, [fr, hh, h_w7])
                    h = op("act", lambda e, i=i, t=t: e.activation(R[:, t:t + 2, :], PS[:, i, :].rearrange("p (a c) -> p a c", a=2), ACT.Sigmoid), h, prev)
                    bank_free[i] = [h]
                    hr.append(h)
                for t in range(0, TB_, 2):
                    i, fr = bank()
                    for j in range(2):
                        for k in range(2):
                            h = mm(PS[:, i, D * j:D * j + D], ka[:, k, P * (t + j):P * (t + j) + P], Wv7[:, k, :], k == 0, k == 1, [fr, hk])
                    xs = X[:, TB_ * b + t:TB_ * b + t + 2, :]
                    h = dv(lambda e, i=i, t=t: e.tensor_tensor(R[:, t:t + 2, :], R[:, t:t + 2, :], PS[:, i, :].rearrange("p (a c) -> p a c", a=2), ALU.mult), h, hr[t // 2])
                    bank_free[i] = [h]
                    h = op("pool", lambda e, t=t, xs=xs: e.tensor_tensor(xs, xs, R[:, t:t + 2, :], ALU.add), h)
                prev = [(pr.sem[e], pr.n[pr.sem[e]]) for e in ("pe", "act", "dve", "pool")]

        phase_g()
        finish()


def layouts(i):
    f = {k: np.asarray(v) for k, v in i.items()}
    a = {}
    a["x"] = f["x"].reshape(N, D)
    a["xT"] = f["x"].reshape(N, D).T
    a["ids"] = np.concatenate([f["itok_B_0_6"], f["itok_B_0_7"], f["itok_B_0_8"]]).reshape(1, 6)
    a["u"] = f["condB_uprev"].reshape(1, B)
    a["idx"] = f["itok_Sx32_0_1023"]
    a["imask"] = f["mask_Sx32_bk1"]
    a["pmask"] = f["mask_SxS_bk0"]

    def col(v):
        return v.reshape(-1, P).T

    vecs = {"maa_x": "L0_attn_time_maa_x", "maa_w": "L0_attn_time_maa_w", "maa_k": "L0_attn_time_maa_k",
            "maa_v": "L0_attn_time_maa_v", "maa_r": "L0_attn_time_maa_r", "decay": "L0_attn_time_decay",
            "faaaa": "L0_attn_time_faaaa", "ln_w": "L0_attn_ln_w", "ln_b": "L0_attn_ln_b",
            "bq": "L1_cond_bq", "bk": "L1_cond_bk", "mu_r": "L1_ffn_mu_r", "mu_k": "L1_ffn_mu_k", "bo": "L1_cond_bo"}
    a["cvec"] = np.concatenate([col(f[vecs[n]].reshape(-1)) for n in CV]
                               + [col(f["L0_cond2_b1"]), col(f["L0_ffn_b1"].reshape(-1))], axis=1)

    def gb(g, b, bd):
        e = g.shape[0]
        pad = np.zeros((e, P, 1), np.float32)
        pad[:, :bd.shape[1], 0] = bd
        return np.concatenate([g.reshape(e, 2, P).transpose(0, 2, 1), b.reshape(e, 2, P).transpose(0, 2, 1), pad], axis=2)

    a["gb0"] = gb(f["L0_cond_ln_g"], f["L0_cond_ln_b"], f["L0_cond_down_b"])
    a["gb1"] = gb(f["L1_cond2_gamma"], f["L1_cond2_beta"], f["L1_cond2_b1"])
    for n in ("L0_cond_down_w", "L0_cond_up_w", "L0_cond_up_b", "L0_attn_time_maa_w1", "L0_attn_time_decay_w1",
              "L0_attn_time_decay_w2", "L0_attn_W_r", "L0_attn_W_k", "L0_attn_W_v", "L0_attn_W_o",
              "L0_cond2_W1", "L0_cond2_W2", "L0_cond2_b2", "L0_cond2_We", "L0_cond2_be", "L0_ffn_Wg",
              "L0_ffn_W1", "L0_ffn_W2", "L0_ffn_b2", "L1_cond_bv", "L1_cond2_W1",
              "L1_cond2_W2", "L1_cond2_b2"):
        a[n] = f[n]
    a["L0_attn_time_maa_w2"] = f["L0_attn_time_maa_w2"].reshape(P, D)
    for n in ("Wq", "Wk", "Wv", "Wo"):
        a["L1_cond_" + n] = f["L1_cond_" + n].T
        w = f["L1_attn_" + n]
        a["L1_attn_" + n] = w.reshape(1024, 256) if n == "Wo" else w.reshape(256, 1024)
    for n in ("W_r", "W_k", "W_v"):
        a["L1_ffn_" + n] = f["L1_ffn_" + n].T
    i = np.arange(P)
    a["k_ident"] = np.eye(P, dtype=np.float32)
    a["k_headb"] = (i[:, None] // 64 == i[None, :] // 64).astype(np.float32)
    a["k_triu"] = (i[:, None] <= i[None, :]).astype(np.float32)
    NEG = np.float32(-1e9)
    z = np.zeros((P, P), np.float32)
    prev = np.where(i[None, :] > i[:, None], np.float32(0), -NEG)
    nxt = np.where(i[None, :] < i[:, None], np.float32(0), -NEG)
    a["k_band"] = np.concatenate([prev, z, nxt, z[:, :64], prev, z, z[:, :64]], axis=1).astype(np.float32)
    a["k_iota"] = np.broadcast_to(np.arange(S, dtype=np.float32), (P, S))
    a["k_slot"] = np.concatenate([np.broadcast_to(np.arange(8, dtype=np.float32), (P, 8)),
                                  np.arange(N, dtype=np.float32).reshape(NT, P).T + E * CAP], axis=1)
    return {k: np.ascontiguousarray(v) for k, v in a.items()}


def kernel(**inputs):
    import concourse.bacc as _bacc
    from concourse.bass_utils import run_bass_kernel_spmd as _run

    nc = _bacc.Bacc("TRN2", target_bir_lowering=False, num_devices=1)
    arrays, aps = {}, {}
    for name, v in layouts(inputs).items():
        arrays[f"in_{name}"] = v
        aps[name] = nc.dram_tensor(f"in_{name}", v.shape, mybir.dt.from_np(v.dtype), kind="ExternalInput").ap()
    out = nc.dram_tensor("out_0", (N, D), F32, kind="ExternalOutput").ap()
    build(nc, aps, out)
    r = _run(nc, [arrays], core_ids=[0])
    return r.results[0]["out_0"].reshape(B, S, D)
```
